# Optimizing a Trainium2 kernel written in Bass

```python
import numpy as np
import jax
import jax.numpy as jnp

def _softmax(x, axis=-1):
    return jax.nn.softmax(x, axis=axis)

def _gelu(x):
    return jax.nn.gelu(x, approximate=True)

def _silu(x):
    return jax.nn.silu(x)

def _sigmoid(x):
    return jax.nn.sigmoid(x)

def _layernorm(x, axis=-1, eps=1e-05):
    m = jnp.mean(x, axis=axis, keepdims=True)
    v = jnp.var(x, axis=axis, keepdims=True)
    return (x - m) / jnp.sqrt(v + eps)

def _scatter_add(tgt, idx, src, axis=0):
    return tgt.at[idx].add(src)

def _segment_sum(src, seg, n):
    return jax.ops.segment_sum(src, seg, n)
kernel_name = 'mk_xattn_ffn_d4_seqx_r8_047983'

def setup_inputs(seed: int=0):
    np.random.seed(seed)
    _w = jnp.asarray

    def _rec_inputs():
        import jax
        import jax.numpy as jnp
        _rk = jax.random.key(seed)
        x = -0.0002928 + 1 * jax.random.normal(jax.random.fold_in(_rk, 1), (8, 256, 128), jnp.float32)
        _lenS = 256 - jax.random.randint(jax.random.fold_in(_rk, 7), (8,), 0, max(1, 256 // 4) + 1, jnp.int32)
        _lenS2 = 1601 - jax.random.randint(jax.random.fold_in(_rk, 8), (8,), 0, max(1, 1601 // 4) + 1, jnp.int32)
        _ctx_1024P = jax.random.normal(jax.random.fold_in(_rk, 11), (8, 16, 128), jnp.float32)
        _ctx_1024c = jax.random.dirichlet(jax.random.fold_in(_rk, 511), 0.3 * jnp.ones((16,), jnp.float32), (8, 1601))
        _ctx_1024t = jnp.einsum('bsk,bkd->bsd', _ctx_1024c, _ctx_1024P)
        _ctx_1024t = _ctx_1024t * jax.lax.rsqrt(jnp.mean(jnp.square(_ctx_1024t)) + 1e-12) * 0.953939
        ctx_1024 = -1.39393e-06 + 0.999914 * (_ctx_1024t + 0.3 * jax.random.normal(jax.random.fold_in(_rk, 611), (8, 1601, 128), jnp.float32))
        _validS = jnp.arange(256)[None, :] < _lenS[:, None]
        _validS2 = jnp.arange(1601)[None, :] < _lenS2[:, None]
        _causal = jnp.tril(jnp.ones((256, 256), dtype=bool))
        mask_Bx1xSxS2_ik1 = jnp.where(jnp.broadcast_to(_validS2[:, None, None, :], (8, 1, 256, 1601)), 1, 0).astype(jnp.int32)
        mask_1x1xSxS2_ik1 = jnp.where(jnp.broadcast_to(_validS2[0:1, None, None, :], (1, 1, 256, 1601)), 1, 0).astype(jnp.int32)
        return (x, ctx_1024, mask_Bx1xSxS2_ik1, mask_1x1xSxS2_ik1)
    x, ctx_1024, mask_Bx1xSxS2_ik1, mask_1x1xSxS2_ik1 = _rec_inputs()

    def _L0_xattn_setup():
        import jax, jax.numpy as jnp
        import numpy as np
        DIM = 128
        HEADS = 16
        HEAD_DIM = DIM // HEADS
        key = jax.random.key(seed)
        ks = jax.random.split(key, 12)
        B, Tq, Tk = (2, 256, 256)
        inp = {'query': jax.random.normal(ks[0], (B, Tq, DIM), jnp.float32), 'key': jax.random.normal(ks[1], (B, Tk, DIM), jnp.float32), 'value': jax.random.normal(ks[2], (B, Tk, DIM), jnp.float32), 'mask': jax.random.randint(ks[3], (B, 1, Tq, Tk), 0, 2, jnp.int32), 'wq': jax.random.uniform(ks[4], (DIM, DIM), jnp.float32, -1.0, 1.0) * np.sqrt(6.0 / (2 * DIM)), 'wk': jax.random.uniform(ks[5], (DIM, DIM), jnp.float32, -1.0, 1.0) * np.sqrt(6.0 / (2 * DIM)), 'wv': jax.random.uniform(ks[6], (DIM, DIM), jnp.float32, -1.0, 1.0) * np.sqrt(6.0 / (2 * DIM)), 'wo': jax.random.uniform(ks[7], (DIM, DIM), jnp.float32, -1.0, 1.0) * np.sqrt(6.0 / (2 * DIM)), 'bq': jnp.zeros((DIM,), jnp.float32), 'bk': jnp.zeros((DIM,), jnp.float32), 'bv': jnp.zeros((DIM,), jnp.float32), 'bo': jnp.zeros((DIM,), jnp.float32)}
        return inp
    _L0_xattn_all = _L0_xattn_setup()
    _L0_xattn_in = {k: v for k, v in _L0_xattn_all.items() if k in ('wq', 'wk', 'wv', 'wo', 'bq', 'bk', 'bv', 'bo')}
    del _L0_xattn_all

    def _L0_ffn_setup():
        import jax, jax.numpy as jnp
        import numpy as np
        D = 128
        H = 16
        DK = D // H
        E = 8
        DFF = 4 * D
        TOPK = 2
        EPS = 1e-05

        def _layernorm(x, g, b):
            m = jnp.mean(x, axis=-1, keepdims=True)
            v = jnp.mean(jnp.square(x - m), axis=-1, keepdims=True)
            return (x - m) * jax.lax.rsqrt(v + EPS) * g + b
        key = jax.random.key(seed)
        ks = jax.random.split(key, 16)
        s_in = 1.0 / np.sqrt(D)
        s_ff = 1.0 / np.sqrt(DFF)
        return {'x': jax.random.normal(ks[0], (2, 256, D), dtype=jnp.float32), 'ln1_g': jnp.ones((D,), jnp.float32), 'ln1_b': jnp.zeros((D,), jnp.float32), 'w_qkv': jax.random.normal(ks[1], (D, 3 * D), jnp.float32) * s_in, 'b_qkv': jnp.zeros((3 * D,), jnp.float32), 'w_o': jax.random.normal(ks[2], (D, D), jnp.float32) * s_in, 'b_o': jnp.zeros((D,), jnp.float32), 'ln2_g': jnp.ones((D,), jnp.float32), 'ln2_b': jnp.zeros((D,), jnp.float32), 'gate_w': jax.random.normal(ks[3], (D, E), jnp.float32) * s_in, 'gate_b': jnp.zeros((E,), jnp.float32), 'W1': jax.random.normal(ks[4], (E, D, DFF), jnp.float32) * s_in, 'b1': jnp.zeros((E, DFF), jnp.float32), 'W2': jax.random.normal(ks[5], (E, DFF, D), jnp.float32) * s_ff, 'b2': jnp.zeros((E, D), jnp.float32)}
    _L0_ffn_all = _L0_ffn_setup()
    _L0_ffn_in = {k: v for k, v in _L0_ffn_all.items() if k in ('ln1_g', 'ln1_b', 'w_qkv', 'b_qkv', 'w_o', 'b_o', 'ln2_g', 'ln2_b', 'gate_w', 'gate_b', 'W1', 'b1', 'W2', 'b2')}
    del _L0_ffn_all

    def _L1_xattn_setup():
        import jax, jax.numpy as jnp
        import numpy as np
        EMBED = 128
        HEADS = 16
        HEAD_DIM = EMBED // HEADS
        B, S = (4, 256)
        key = jax.random.key(seed)
        ks = jax.random.split(key, 9)
        q = jax.random.normal(ks[0], (B, S, EMBED), dtype=jnp.float32)
        k = jax.random.normal(ks[1], (B, S, EMBED), dtype=jnp.float32)
        v = jax.random.normal(ks[2], (B, S, EMBED), dtype=jnp.float32)
        mask = jax.random.randint(ks[3], (1, 1, S, S), 0, 2, dtype=jnp.int32)
        sc = 1.0 / np.sqrt(HEAD_DIM)
        Wq = jax.random.normal(ks[4], (HEAD_DIM, HEAD_DIM), dtype=jnp.float32) * sc
        Wk = jax.random.normal(ks[5], (HEAD_DIM, HEAD_DIM), dtype=jnp.float32) * sc
        Wv = jax.random.normal(ks[6], (HEAD_DIM, HEAD_DIM), dtype=jnp.float32) * sc
        Wo = jax.random.normal(ks[7], (EMBED, EMBED), dtype=jnp.float32) * (1.0 / np.sqrt(EMBED))
        bo = jax.random.normal(ks[8], (EMBED,), dtype=jnp.float32) * 0.01
        return {'q': q, 'k': k, 'v': v, 'mask': mask, 'Wq': Wq, 'Wk': Wk, 'Wv': Wv, 'Wo': Wo, 'bo': bo}
    _L1_xattn_all = _L1_xattn_setup()
    _L1_xattn_in = {k: v for k, v in _L1_xattn_all.items() if k in ('Wq', 'Wk', 'Wv', 'Wo', 'bo')}
    del _L1_xattn_all

    def _L1_ffn_setup():
        import jax, jax.numpy as jnp
        import numpy as np
        E = 8
        K = 2
        D = 128
        H = 342
        B, S = (2, 256)

        def _moe_forward(x, centroid, Wg, bg, W1, b1, W2, b2):
            T = x.shape[0] * x.shape[1]
            xs = x.reshape(T, D)
            d2 = jnp.sum(xs * xs, axis=-1, keepdims=True) + jnp.sum(centroid * centroid, axis=-1)[None, :] - 2.0 * (xs @ centroid.T)
            dist = jnp.sqrt(jnp.maximum(d2, 1e-12))
            w, sel = jax.lax.top_k(dist, K)
            w = jax.nn.softmax(w.astype(jnp.float32), axis=1).astype(x.dtype)
            we = jnp.zeros((T, E), dtype=x.dtype).at[jnp.arange(T)[:, None], sel].add(w)
            out = jnp.zeros_like(xs)
            for e in range(E):
                h = jax.nn.silu(xs @ Wg[e] + bg[e]) * (xs @ W1[e] + b1[e])
                out = out + we[:, e:e + 1] * (h @ W2[e] + b2[e])
            return out.reshape(x.shape)
        key = jax.random.key(seed)
        ks = jax.random.split(key, 9)
        scale = 0.02
        return {'x': jax.random.normal(ks[0], (B, S, D), dtype=jnp.float32), 'centroid': jax.random.normal(ks[1], (E, D), dtype=jnp.float32), 'Wg': jax.random.normal(ks[2], (E, D, H), dtype=jnp.float32) * scale, 'bg': jnp.zeros((E, H), dtype=jnp.float32), 'W1': jax.random.normal(ks[3], (E, D, H), dtype=jnp.float32) * scale, 'b1': jnp.zeros((E, H), dtype=jnp.float32), 'W2': jax.random.normal(ks[4], (E, H, D), dtype=jnp.float32) * scale, 'b2': jnp.zeros((E, D), dtype=jnp.float32)}
    _L1_ffn_all = _L1_ffn_setup()
    _L1_ffn_in = {k: v for k, v in _L1_ffn_all.items() if k in ('centroid', 'Wg', 'bg', 'W1', 'b1', 'W2', 'b2')}
    del _L1_ffn_all

    def _L2_xattn_setup():
        import jax, jax.numpy as jnp
        import numpy as np
        N_HEAD = 16
        key = jax.random.key(seed)
        ks = jax.random.split(key, 5)
        b, l, d = (4, 256, 128)
        dh = d // N_HEAD
        return {'q': jax.random.normal(ks[0], (b, l, d), dtype=jnp.float32), 'kv': jax.random.normal(ks[1], (b, l, d), dtype=jnp.float32), 'Wq': jax.random.normal(ks[2], (d, d), dtype=jnp.float32) * 0.02, 'Wkv': jax.random.normal(ks[3], (2 * dh, d), dtype=jnp.float32) * 0.02, 'Wc': jax.random.normal(ks[4], (d, d), dtype=jnp.float32) * 0.02}
    _L2_xattn_all = _L2_xattn_setup()
    _L2_xattn_in = {k: v for k, v in _L2_xattn_all.items() if k in ('Wq', 'Wkv', 'Wc')}
    del _L2_xattn_all

    def _L2_ffn_setup():
        import jax, jax.numpy as jnp
        import numpy as np
        D, H, E, K = (128, 512, 8, 2)
        B, T = (2, 256)

        def _layernorm(x, g, b, eps=1e-05):
            mu = jnp.mean(x, axis=-1, keepdims=True)
            var = jnp.mean(jnp.square(x - mu), axis=-1, keepdims=True)
            return (x - mu) * jax.lax.rsqrt(var + eps) * g + b

        def _expert(x, g, b, W1, b1, W2, b2, Wo, bo):
            x = _layernorm(x, g, b)
            x1 = x @ W1 + b1
            x2 = jnp.clip(x @ W2 + b2, -20.0, 20.0)
            hidden = jnp.clip(x1 * (x2 * jax.nn.sigmoid(x2)), -10000.0, 10000.0)
            return jnp.clip(hidden @ Wo + bo, -10000.0, 10000.0)
        key = jax.random.key(seed)
        ks = jax.random.split(key, 6)
        s = 0.02
        return {'x': jax.random.normal(ks[0], (B, T, D), jnp.float32), 'ln_g': jnp.ones((D,), jnp.float32), 'ln_b': jnp.zeros((D,), jnp.float32), 'router_w': jax.random.normal(ks[1], (D, E), jnp.float32) * s, 'eg': jnp.ones((E, D), jnp.float32), 'eb': jnp.zeros((E, D), jnp.float32), 'W1': jax.random.normal(ks[2], (E, D, H), jnp.float32) * s, 'b1': jnp.zeros((E, H), jnp.float32), 'W2': jax.random.normal(ks[3], (E, D, H), jnp.float32) * s, 'b2': jnp.zeros((E, H), jnp.float32), 'Wo': jax.random.normal(ks[4], (E, H, D), jnp.float32) * s, 'bo': jnp.zeros((E, D), jnp.float32)}
    _L2_ffn_all = _L2_ffn_setup()
    _L2_ffn_in = {k: v for k, v in _L2_ffn_all.items() if k in ('ln_g', 'ln_b', 'router_w', 'eg', 'eb', 'W1', 'b1', 'W2', 'b2', 'Wo', 'bo')}
    del _L2_ffn_all

    def _L3_xattn_setup():
        import jax, jax.numpy as jnp
        import numpy as np
        NDIM = 128
        NHEAD = 16
        HEAD_DIM = NDIM // NHEAD
        key = jax.random.key(seed)
        ks = jax.random.split(key, 12)
        B, L, C = (2, 256, NDIM)
        s = 0.02
        return {'q': jax.random.normal(ks[0], (B, L, C), jnp.float32), 'k': jax.random.normal(ks[1], (B, L, C), jnp.float32), 'v': jax.random.normal(ks[2], (B, L, C), jnp.float32), 'Wq': jax.random.normal(ks[3], (C, C), jnp.float32) * s, 'bq': jax.random.normal(ks[4], (C,), jnp.float32) * s, 'Wk': jax.random.normal(ks[5], (C, C), jnp.float32) * s, 'bk': jax.random.normal(ks[6], (C,), jnp.float32) * s, 'Wv': jax.random.normal(ks[7], (C, C), jnp.float32) * s, 'bv': jax.random.normal(ks[8], (C,), jnp.float32) * s, 'Wo': jax.random.normal(ks[9], (C, C), jnp.float32) * s, 'bo': jax.random.normal(ks[10], (C,), jnp.float32) * s}
    _L3_xattn_all = _L3_xattn_setup()
    _L3_xattn_in = {k: v for k, v in _L3_xattn_all.items() if k in ('Wq', 'bq', 'Wk', 'bk', 'Wv', 'bv', 'Wo', 'bo')}
    del _L3_xattn_all

    def _L3_ffn_setup():
        import jax, jax.numpy as jnp
        import numpy as np
        B, T, DIM = (4, 128, 128)
        H, E, DH, K = (8, 5, 64, 3)

        def _topk_mask(s, k):
            idx = jax.lax.top_k(s, k)[1]
            return jnp.sum(jax.nn.one_hot(idx, s.shape[-1], dtype=s.dtype), axis=-2)
        key = jax.random.key(seed)
        ks = jax.random.split(key, 6)
        w = lambda k, shape: jax.random.normal(k, shape, jnp.float32) * 0.02
        return {'x': jax.random.normal(ks[0], (B, T, DIM), jnp.float32), 'Wq': w(ks[1], (DIM, H * E * DH)), 'Wkv': w(ks[2], (DIM, 2 * H * E * DH)), 'Ws': w(ks[3], (DIM, H * E)), 'Wd': w(ks[4], (DIM, H * E)), 'Wo': w(ks[5], (DH, E * DIM))}
    _L3_ffn_all = _L3_ffn_setup()
    _L3_ffn_in = {k: v for k, v in _L3_ffn_all.items() if k in ('Wq', 'Wkv', 'Ws', 'Wd', 'Wo')}
    del _L3_ffn_all
    return {'x': x, 'ctx_1024': ctx_1024, 'mask_Bx1xSxS2_ik1': mask_Bx1xSxS2_ik1, 'mask_1x1xSxS2_ik1': mask_1x1xSxS2_ik1, 'L0_xattn_wq': _L0_xattn_in['wq'], 'L0_xattn_wk': _L0_xattn_in['wk'], 'L0_xattn_wv': _L0_xattn_in['wv'], 'L0_xattn_wo': _L0_xattn_in['wo'], 'L0_xattn_bq': _L0_xattn_in['bq'], 'L0_xattn_bk': _L0_xattn_in['bk'], 'L0_xattn_bv': _L0_xattn_in['bv'], 'L0_xattn_bo': _L0_xattn_in['bo'], 'L0_ffn_ln1_g': _L0_ffn_in['ln1_g'], 'L0_ffn_ln1_b': _L0_ffn_in['ln1_b'], 'L0_ffn_w_qkv': _L0_ffn_in['w_qkv'], 'L0_ffn_b_qkv': _L0_ffn_in['b_qkv'], 'L0_ffn_w_o': _L0_ffn_in['w_o'], 'L0_ffn_b_o': _L0_ffn_in['b_o'], 'L0_ffn_ln2_g': _L0_ffn_in['ln2_g'], 'L0_ffn_ln2_b': _L0_ffn_in['ln2_b'], 'L0_ffn_gate_w': _L0_ffn_in['gate_w'], 'L0_ffn_gate_b': _L0_ffn_in['gate_b'], 'L0_ffn_W1': _L0_ffn_in['W1'], 'L0_ffn_b1': _L0_ffn_in['b1'], 'L0_ffn_W2': _L0_ffn_in['W2'], 'L0_ffn_b2': _L0_ffn_in['b2'], 'L1_xattn_Wq': _L1_xattn_in['Wq'], 'L1_xattn_Wk': _L1_xattn_in['Wk'], 'L1_xattn_Wv': _L1_xattn_in['Wv'], 'L1_xattn_Wo': _L1_xattn_in['Wo'], 'L1_xattn_bo': _L1_xattn_in['bo'], 'L1_ffn_centroid': _L1_ffn_in['centroid'], 'L1_ffn_Wg': _L1_ffn_in['Wg'], 'L1_ffn_bg': _L1_ffn_in['bg'], 'L1_ffn_W1': _L1_ffn_in['W1'], 'L1_ffn_b1': _L1_ffn_in['b1'], 'L1_ffn_W2': _L1_ffn_in['W2'], 'L1_ffn_b2': _L1_ffn_in['b2'], 'L2_xattn_Wq': _L2_xattn_in['Wq'], 'L2_xattn_Wkv': _L2_xattn_in['Wkv'], 'L2_xattn_Wc': _L2_xattn_in['Wc'], 'L2_ffn_ln_g': _L2_ffn_in['ln_g'], 'L2_ffn_ln_b': _L2_ffn_in['ln_b'], 'L2_ffn_router_w': _L2_ffn_in['router_w'], 'L2_ffn_eg': _L2_ffn_in['eg'], 'L2_ffn_eb': _L2_ffn_in['eb'], 'L2_ffn_W1': _L2_ffn_in['W1'], 'L2_ffn_b1': _L2_ffn_in['b1'], 'L2_ffn_W2': _L2_ffn_in['W2'], 'L2_ffn_b2': _L2_ffn_in['b2'], 'L2_ffn_Wo': _L2_ffn_in['Wo'], 'L2_ffn_bo': _L2_ffn_in['bo'], 'L3_xattn_Wq': _L3_xattn_in['Wq'], 'L3_xattn_bq': _L3_xattn_in['bq'], 'L3_xattn_Wk': _L3_xattn_in['Wk'], 'L3_xattn_bk': _L3_xattn_in['bk'], 'L3_xattn_Wv': _L3_xattn_in['Wv'], 'L3_xattn_bv': _L3_xattn_in['bv'], 'L3_xattn_Wo': _L3_xattn_in['Wo'], 'L3_xattn_bo': _L3_xattn_in['bo'], 'L3_ffn_Wq': _L3_ffn_in['Wq'], 'L3_ffn_Wkv': _L3_ffn_in['Wkv'], 'L3_ffn_Ws': _L3_ffn_in['Ws'], 'L3_ffn_Wd': _L3_ffn_in['Wd'], 'L3_ffn_Wo': _L3_ffn_in['Wo']}

def reference(x, ctx_1024, mask_Bx1xSxS2_ik1, mask_1x1xSxS2_ik1, L0_xattn_wq, L0_xattn_wk, L0_xattn_wv, L0_xattn_wo, L0_xattn_bq, L0_xattn_bk, L0_xattn_bv, L0_xattn_bo, L0_ffn_ln1_g, L0_ffn_ln1_b, L0_ffn_w_qkv, L0_ffn_b_qkv, L0_ffn_w_o, L0_ffn_b_o, L0_ffn_ln2_g, L0_ffn_ln2_b, L0_ffn_gate_w, L0_ffn_gate_b, L0_ffn_W1, L0_ffn_b1, L0_ffn_W2, L0_ffn_b2, L1_xattn_Wq, L1_xattn_Wk, L1_xattn_Wv, L1_xattn_Wo, L1_xattn_bo, L1_ffn_centroid, L1_ffn_Wg, L1_ffn_bg, L1_ffn_W1, L1_ffn_b1, L1_ffn_W2, L1_ffn_b2, L2_xattn_Wq, L2_xattn_Wkv, L2_xattn_Wc, L2_ffn_ln_g, L2_ffn_ln_b, L2_ffn_router_w, L2_ffn_eg, L2_ffn_eb, L2_ffn_W1, L2_ffn_b1, L2_ffn_W2, L2_ffn_b2, L2_ffn_Wo, L2_ffn_bo, L3_xattn_Wq, L3_xattn_bq, L3_xattn_Wk, L3_xattn_bk, L3_xattn_Wv, L3_xattn_bv, L3_xattn_Wo, L3_xattn_bo, L3_ffn_Wq, L3_ffn_Wkv, L3_ffn_Ws, L3_ffn_Wd, L3_ffn_Wo):
    import jax
    import jax.numpy as jnp

    def _L0_xattn_ref(query, key, value, mask, wq, wk, wv, wo, bq, bk, bv, bo):
        import jax, jax.numpy as jnp
        import numpy as np
        DIM = 128
        HEADS = 16
        HEAD_DIM = DIM // HEADS
        B, Tq, C = query.shape
        Tk = key.shape[1]
        scale = 1.0 / np.sqrt(HEAD_DIM)
        q = (query @ wq.T + bq).reshape(B, Tq, HEADS, HEAD_DIM).transpose(0, 2, 1, 3)
        k = (key @ wk.T + bk).reshape(B, Tk, HEADS, HEAD_DIM).transpose(0, 2, 1, 3)
        v = (value @ wv.T + bv).reshape(B, Tk, HEADS, HEAD_DIM).transpose(0, 2, 1, 3)
        scores = jnp.einsum('bhqd,bhkd->bhqk', q, k) * scale
        scores = jnp.clip(scores, -100.0, 100.0)
        scores = jnp.where(mask == 0, -jnp.inf, scores)
        attn = jax.nn.softmax(scores, axis=-1)
        out = jnp.einsum('bhqk,bhkd->bhqd', attn, v)
        out = out.transpose(0, 2, 1, 3).reshape(B, Tq, HEADS * HEAD_DIM)
        return out @ wo.T + bo

    def _L0_ffn_ref(x, ln1_g, ln1_b, w_qkv, b_qkv, w_o, b_o, ln2_g, ln2_b, gate_w, gate_b, W1, b1, W2, b2):
        import jax, jax.numpy as jnp
        import numpy as np
        D = 128
        H = 16
        DK = D // H
        E = 8
        DFF = 4 * D
        TOPK = 2
        EPS = 1e-05

        def _layernorm(x, g, b):
            m = jnp.mean(x, axis=-1, keepdims=True)
            v = jnp.mean(jnp.square(x - m), axis=-1, keepdims=True)
            return (x - m) * jax.lax.rsqrt(v + EPS) * g + b
        B, S, _ = x.shape
        h = _layernorm(x, ln1_g, ln1_b)
        qkv = h @ w_qkv + b_qkv
        q, k, v = jnp.split(qkv, 3, axis=-1)
        q = q.reshape(B, S, H, DK)
        k = k.reshape(B, S, H, DK)
        v = v.reshape(B, S, H, DK)
        scores = jnp.einsum('bqhd,bkhd->bhqk', q, k) / np.sqrt(DK)
        attn = jax.nn.softmax(scores, axis=-1)
        o = jnp.einsum('bhqk,bkhd->bqhd', attn, v).reshape(B, S, D)
        x = x + o @ w_o + b_o
        h = _layernorm(x, ln2_g, ln2_b).reshape(B * S, D)
        logits = h @ gate_w + gate_b
        topv, topi = jax.lax.top_k(logits, TOPK)
        gw = jax.nn.softmax(topv, axis=-1)
        ew = jnp.sum(jax.nn.one_hot(topi, E, dtype=h.dtype) * gw[..., None], axis=1)
        hid = jax.nn.relu(jnp.einsum('td,edf->etf', h, W1) + b1[:, None, :])
        out_e = jnp.einsum('etf,efd->etd', hid, W2) + b2[:, None, :]
        moe = jnp.einsum('etd,te->td', out_e, ew)
        return x + moe.reshape(B, S, D)

    def _L1_xattn_ref(q, k, v, mask, Wq, Wk, Wv, Wo, bo):
        import jax, jax.numpy as jnp
        import numpy as np
        EMBED = 128
        HEADS = 16
        HEAD_DIM = EMBED // HEADS
        B, S = (4, 256)
        N, qlen = (q.shape[0], q.shape[1])
        klen, vlen = (k.shape[1], v.shape[1])
        qh = q.reshape(N, qlen, HEADS, HEAD_DIM)
        kh = k.reshape(N, klen, HEADS, HEAD_DIM)
        vh = v.reshape(N, vlen, HEADS, HEAD_DIM)
        qh = jnp.einsum('nqhd,ed->nqhe', qh, Wq)
        kh = jnp.einsum('nkhd,ed->nkhe', kh, Wk)
        vh = jnp.einsum('nkhd,ed->nkhe', vh, Wv)
        energy = jnp.einsum('nqhd,nkhd->nhqk', qh, kh)
        energy = jnp.where(mask == 0, jnp.float32(-1e+20), energy)
        attention = jax.nn.softmax(energy / jnp.float32(EMBED ** 0.5), axis=3)
        out = jnp.einsum('nhqk,nkhd->nqhd', attention, vh)
        out = out.reshape(N, qlen, EMBED)
        return out @ Wo.T + bo

    def _L1_ffn_ref(x, centroid, Wg, bg, W1, b1, W2, b2):
        import jax, jax.numpy as jnp
        import numpy as np
        E = 8
        K = 2
        D = 128
        H = 342
        B, S = (2, 256)

        def _moe_forward(x, centroid, Wg, bg, W1, b1, W2, b2):
            T = x.shape[0] * x.shape[1]
            xs = x.reshape(T, D)
            d2 = jnp.sum(xs * xs, axis=-1, keepdims=True) + jnp.sum(centroid * centroid, axis=-1)[None, :] - 2.0 * (xs @ centroid.T)
            dist = jnp.sqrt(jnp.maximum(d2, 1e-12))
            w, sel = jax.lax.top_k(dist, K)
            w = jax.nn.softmax(w.astype(jnp.float32), axis=1).astype(x.dtype)
            we = jnp.zeros((T, E), dtype=x.dtype).at[jnp.arange(T)[:, None], sel].add(w)
            out = jnp.zeros_like(xs)
            for e in range(E):
                h = jax.nn.silu(xs @ Wg[e] + bg[e]) * (xs @ W1[e] + b1[e])
                out = out + we[:, e:e + 1] * (h @ W2[e] + b2[e])
            return out.reshape(x.shape)
        return _moe_forward(x, centroid, Wg, bg, W1, b1, W2, b2)

    def _L2_xattn_ref(q, kv, Wq, Wkv, Wc):
        import jax, jax.numpy as jnp
        import numpy as np
        N_HEAD = 16
        b, l, d = q.shape
        h = N_HEAD
        dh = d // h
        qp = jnp.einsum('bld,ed->ble', q, Wq)
        scores = jnp.einsum('bld,bmd->blm', qp, kv)
        idx = jnp.argmax(scores, axis=-1)
        mem = jnp.take_along_axis(kv, idx[..., None], axis=1)
        mkv = jnp.einsum('bld,ed->ble', mem, Wkv)
        mk, mv = jnp.split(mkv, 2, axis=-1)
        qh = qp.reshape(b, l, h, dh).transpose(0, 2, 1, 3)
        scale = 1.0 / np.sqrt(dh).astype(np.float32)
        logits = jnp.einsum('bhld,bmd->bhlm', qh, mk) * scale
        attn = jax.nn.softmax(logits, axis=-1)
        out = jnp.einsum('bhlm,bmd->bhld', attn, mv)
        out = out.transpose(0, 2, 1, 3).reshape(b, l, d)
        return jnp.einsum('bld,ed->ble', out, Wc)

    def _L2_ffn_ref(x, ln_g, ln_b, router_w, eg, eb, W1, b1, W2, b2, Wo, bo):
        import jax, jax.numpy as jnp
        import numpy as np
        D, H, E, K = (128, 512, 8, 2)
        B, T = (2, 256)

        def _layernorm(x, g, b, eps=1e-05):
            mu = jnp.mean(x, axis=-1, keepdims=True)
            var = jnp.mean(jnp.square(x - mu), axis=-1, keepdims=True)
            return (x - mu) * jax.lax.rsqrt(var + eps) * g + b

        def _expert(x, g, b, W1, b1, W2, b2, Wo, bo):
            x = _layernorm(x, g, b)
            x1 = x @ W1 + b1
            x2 = jnp.clip(x @ W2 + b2, -20.0, 20.0)
            hidden = jnp.clip(x1 * (x2 * jax.nn.sigmoid(x2)), -10000.0, 10000.0)
            return jnp.clip(hidden @ Wo + bo, -10000.0, 10000.0)
        Bb, Tt, Dd = x.shape
        xf = _layernorm(x.reshape(-1, Dd), ln_g, ln_b)
        N = xf.shape[0]
        logits = xf @ router_w
        scores, idx = jax.lax.top_k(logits, K)
        gate = jax.nn.softmax(scores, axis=-1)
        gates_e = jnp.zeros((N, E), xf.dtype).at[jnp.arange(N)[:, None], idx].add(gate)

        def body(acc, p):
            gcol, g, b, w1, bb1, w2, bb2, wo, bbo = p
            return (acc + gcol[:, None] * _expert(xf, g, b, w1, bb1, w2, bb2, wo, bbo), None)
        out, _ = jax.lax.scan(body, jnp.zeros_like(xf), (gates_e.T, eg, eb, W1, b1, W2, b2, Wo, bo))
        return out.reshape(Bb, Tt, Dd)

    def _L3_xattn_ref(q, k, v, Wq, bq, Wk, bk, Wv, bv, Wo, bo):
        import jax, jax.numpy as jnp
        import numpy as np
        NDIM = 128
        NHEAD = 16
        HEAD_DIM = NDIM // NHEAD
        B, Lq, C = q.shape
        H, D = (NHEAD, HEAD_DIM)
        qh = (q @ Wq + bq).reshape(B, Lq, H, D).transpose(0, 2, 1, 3)
        kh = (k @ Wk + bk).reshape(B, k.shape[1], H, D).transpose(0, 2, 1, 3)
        vh = (v @ Wv + bv).reshape(B, v.shape[1], H, D).transpose(0, 2, 1, 3)
        scale = 1.0 / jnp.sqrt(jnp.asarray(D, qh.dtype))
        att = jnp.einsum('bhqd,bhkd->bhqk', qh, kh) * scale
        att = jax.nn.softmax(att, axis=-1)
        y = jnp.einsum('bhqk,bhkd->bhqd', att, vh)
        y = y.transpose(0, 2, 1, 3).reshape(B, Lq, C)
        return y @ Wo + bo

    def _L3_ffn_ref(x, Wq, Wkv, Ws, Wd, Wo):
        import jax, jax.numpy as jnp
        import numpy as np
        B, T, DIM = (4, 128, 128)
        H, E, DH, K = (8, 5, 64, 3)

        def _topk_mask(s, k):
            idx = jax.lax.top_k(s, k)[1]
            return jnp.sum(jax.nn.one_hot(idx, s.shape[-1], dtype=s.dtype), axis=-2)
        b, t, _ = x.shape
        scale = DH ** (-0.5)
        ss = jax.nn.sigmoid(x @ Ws).reshape(b, t, H, E)
        sd = jax.nn.sigmoid(x @ Wd).reshape(b, t, H, E)
        ms = _topk_mask(ss, K)
        md = _topk_mask(sd, K)
        ss_g = ss * ms
        sd_g = sd * md
        q5 = (x @ Wq).reshape(b, t, H, E, DH)
        kv = (x @ Wkv).reshape(b, t, 2, H, E, DH)
        k5, v5 = (kv[:, :, 0], kv[:, :, 1])
        q = jnp.einsum('bthed,bthe->bhtd', q5, sd_g)
        k = jnp.einsum('bthed,bthe->bhtd', k5, ss_g)
        v = jnp.einsum('bthed,bthe->bhtd', v5, ss_g)
        attn = jax.nn.softmax(jnp.einsum('bhid,bhjd->bhij', q * scale, k), axis=-1)
        out = jnp.einsum('bhij,bhjd->bihd', attn, v)
        o5 = jnp.einsum('bthd,dm->bthm', out, Wo).reshape(b, t, H, E, DIM)
        return jnp.einsum('bthem,bthe->btm', o5, md)
    x = x + _L0_xattn_ref(_layernorm(x, axis=-1), ctx_1024, ctx_1024, mask_Bx1xSxS2_ik1, L0_xattn_wq, L0_xattn_wk, L0_xattn_wv, L0_xattn_wo, L0_xattn_bq, L0_xattn_bk, L0_xattn_bv, L0_xattn_bo)
    x = x + _L0_ffn_ref(_layernorm(x, axis=-1), L0_ffn_ln1_g, L0_ffn_ln1_b, L0_ffn_w_qkv, L0_ffn_b_qkv, L0_ffn_w_o, L0_ffn_b_o, L0_ffn_ln2_g, L0_ffn_ln2_b, L0_ffn_gate_w, L0_ffn_gate_b, L0_ffn_W1, L0_ffn_b1, L0_ffn_W2, L0_ffn_b2)
    x = x + _L1_xattn_ref(_layernorm(x, axis=-1), ctx_1024, ctx_1024, mask_1x1xSxS2_ik1, L1_xattn_Wq, L1_xattn_Wk, L1_xattn_Wv, L1_xattn_Wo, L1_xattn_bo)
    x = x + _L1_ffn_ref(_layernorm(x, axis=-1), L1_ffn_centroid, L1_ffn_Wg, L1_ffn_bg, L1_ffn_W1, L1_ffn_b1, L1_ffn_W2, L1_ffn_b2)
    x = x + _L2_xattn_ref(_layernorm(x, axis=-1), ctx_1024, L2_xattn_Wq, L2_xattn_Wkv, L2_xattn_Wc)
    x = x + _L2_ffn_ref(_layernorm(x, axis=-1), L2_ffn_ln_g, L2_ffn_ln_b, L2_ffn_router_w, L2_ffn_eg, L2_ffn_eb, L2_ffn_W1, L2_ffn_b1, L2_ffn_W2, L2_ffn_b2, L2_ffn_Wo, L2_ffn_bo)
    x = x + _L3_xattn_ref(_layernorm(x, axis=-1), ctx_1024, ctx_1024, L3_xattn_Wq, L3_xattn_bq, L3_xattn_Wk, L3_xattn_bk, L3_xattn_Wv, L3_xattn_bv, L3_xattn_Wo, L3_xattn_bo)
    x = x + _L3_ffn_ref(_layernorm(x, axis=-1), L3_ffn_Wq, L3_ffn_Wkv, L3_ffn_Ws, L3_ffn_Wd, L3_ffn_Wo)
    return x

_drawn_inputs = setup_inputs


def setup_inputs(seed=0):
    import zlib

    import numpy as np

    out = dict(_drawn_inputs(seed))
    spreads = {'L0_xattn_bq': (0.0, 0.1),
     'L0_xattn_bk': (0.0, 2.0),
     'L0_xattn_bv': (0.0, 0.1),
     'L0_xattn_bo': (0.0, 0.1),
     'L0_ffn_ln1_g': (1.0, 0.2),
     'L0_ffn_ln1_b': (0.0, 0.1),
     'L0_ffn_b_qkv': (0.0, 0.1),
     'L0_ffn_b_o': (0.0, 0.1),
     'L0_ffn_ln2_g': (1.0, 0.2),
     'L0_ffn_ln2_b': (0.0, 0.1),
     'L0_ffn_gate_b': (0.0, 0.1),
     'L0_ffn_b1': (0.0, 0.343),
     'L0_ffn_b2': (0.0, 0.1),
     'L1_ffn_bg': (0.0, 0.8),
     'L1_ffn_b1': (0.0, 0.8),
     'L1_ffn_b2': (0.0, 0.1),
     'L2_ffn_ln_g': (1.0, 0.6),
     'L2_ffn_ln_b': (0.0, 0.8),
     'L2_ffn_eg': (1.0, 0.6),
     'L2_ffn_eb': (0.0, 0.8),
     'L2_ffn_b1': (0.0, 0.8),
     'L2_ffn_b2': (0.0, 0.8),
     'L2_ffn_bo': (0.0, 0.8)}
    factors = {'L1_xattn_bo': 8.0,
     'L1_ffn_Wg': 8.0,
     'L1_ffn_W1': 8.0,
     'L1_ffn_W2': 8.0,
     'L2_xattn_Wq': 5.317,
     'L2_xattn_Wkv': 3.669,
     'L2_xattn_Wc': 3.337,
     'L2_ffn_W1': 8.0,
     'L2_ffn_W2': 8.0,
     'L2_ffn_Wo': 8.0,
     'L3_xattn_Wq': 8.0,
     'L3_xattn_bq': 54.996,
     'L3_xattn_Wk': 8.0,
     'L3_xattn_bk': 64.0,
     'L3_xattn_Wv': 5.359,
     'L3_xattn_bv': 35.447,
     'L3_xattn_Wo': 5.251,
     'L3_xattn_bo': 41.844,
     'L3_ffn_Wq': 64.0,
     'L3_ffn_Ws': 41.168,
     'L3_ffn_Wd': 22.856,
     'L3_ffn_Wkv': 8.0,
     'L3_ffn_Wo': 8.0}
    for name, (base, spread) in spreads.items():
        noise = np.random.default_rng([zlib.crc32(name.encode()), seed]).standard_normal(out[name].shape)
        drawn = base * np.exp(spread * noise) if base else spread * noise
        out[name] = jnp.asarray(drawn.astype(out[name].dtype))
    for name, factor in factors.items():
        out[name] = (out[name] * factor).astype(out[name].dtype)
    return out
```

```python
from contextlib import ExitStack

import concourse.bass as bass
from concourse import mybir

P = 128
F32 = mybir.dt.float32
BF16 = mybir.dt.bfloat16
I32 = mybir.dt.int32
U32 = mybir.dt.uint32
ALU = mybir.AluOpType
ACT = mybir.ActivationFunctionType
AX = mybir.AxisListType

BATCH, SEQ, DIM = 8, 256, 128
LOOPS = BATCH
FIRST_SEMAPHORE = 120
CTX = 1601
HEADS, HD = 16, 8
PAIRS = HEADS // 2
QT = SEQ // P
EPS = 1e-5
MASKED = -1e30
HALF = 64
PARTS = 6 * HD
SHIFT = PARTS


class Phase:

    def __init__(self, nc, ctx, tag):
        self.nc, self.ctx, self.tag, self.sems = nc, ctx, tag, []

    def sb(self, name, shape, dt=F32):
        return self.ctx.enter_context(self.nc.sbuf_tensor(f"{self.tag}_{name}", shape, dt))

    def ps(self, name, shape, dt=F32):
        return self.ctx.enter_context(self.nc.psum_tensor(f"{self.tag}_{name}", shape, dt))

    def sem(self, name):
        num = self.sems[-1].num + 1 if self.sems else FIRST_SEMAPHORE
        s = self.ctx.enter_context(self.nc.semaphore(f"{self.tag}_{name}", num=num))
        self.sems.append(s)
        return s

    def barrier(self):
        self.nc.all_engine_barrier(sems_to_clear=range(self.sems[0].num, self.sems[-1].num + 1))


class Chain:

    def __init__(self, eng, sem):
        self.eng, self.sem, self.n = eng, sem, 0

    def __call__(self, ins):
        self.n += 1
        ins.then_inc(self.sem, 1)
        self.eng.wait_ge(self.sem, self.n)


def ceil(a, b):
    return -(-a // b)


def inverse_root(dve, chain, out, variance, var, tmp, eps=EPS):
    chain(dve.tensor_scalar(var[:], variance, eps, None, ALU.add))
    chain(dve.tensor_scalar(tmp[:].bitcast(I32), var[:].bitcast(I32), 1, None, ALU.arith_shift_right))
    chain(dve.tensor_scalar(out.bitcast(I32), tmp[:].bitcast(I32), -1.0, 1597463007.0, ALU.mult, ALU.add))
    for _ in range(4):
        chain(dve.tensor_tensor(tmp[:], out, out, ALU.mult))
        chain(dve.scalar_tensor_tensor(tmp[:], tmp[:], -0.5, var[:], ALU.mult, ALU.mult))
        chain(dve.scalar_tensor_tensor(out, tmp[:], 1.5, out, ALU.add, ALU.mult))


def attention_phase(nc, tag, x_in, x_out, w, consts, ctxT=None, ctx_rows=None, mask=None, maskT=None,
                    scale=1.0, clip=None, self_ln=None):
    hard = ctx_rows is not None
    NK = CTX if (ctxT is not None and not hard) else SEQ
    KT = ceil(NK, P)
    KP = ceil(KT, 2)
    NC = ceil(NK, 512)
    AHEAD = 2 if KP > 1 else 3
    N = PAIRS * KP
    ITEMS = 2 * QT * NC
    MASK_ONCE = mask is not None and mask.shape[0] == 1

    def keys(kt):
        return min(P, NK - kt * P)

    def chunk(c):
        return min(512, NK - c * 512)

    with ExitStack() as ctx:
        ph = Phase(nc, ctx, tag)
        sb, ps, sem = ph.sb, ph.ps, ph.sem
        ident = sb("ident", [P, P])
        identb = sb("identb", [P, P], BF16)
        pick = sb("pick", [P, 2 * (HD + 1)])
        shiftsel_f = sb("shiftsel_f", [P, P])
        shiftsel = sb("shiftsel", [P, P], BF16)
        wsb = {k: sb("w_" + k, list(w[k].shape)) for k in ("wq", "wk", "wv", "wo", "wqn") if k in w}
        cols = {k: sb("c_" + k, [P, 1]) for k in ("bq", "bk", "lng", "lnb") if k in w}
        rows = {k: sb("r_" + k, [P, P]) for k in ("bv", "bo") if k in w}
        x_sb = sb("x_sb", [P, QT, DIM])
        stats = sb("stats", [P, QT, 6])
        mv = sb("mv", [P, QT, 2])
        rstd = sb("rstd", [P, QT, 1])
        var = sb("var", [P, QT, 1])
        root = sb("root", [P, QT, 1])
        xn = sb("xn", [P, QT, DIM])
        xn2 = sb("xn2", [P, QT, DIM])
        xT = sb("xT", [P, SEQ])
        srcT = sb("srcT", [P, CTX]) if ctxT is not None else None
        memT = sb("memT", [P, SEQ]) if hard else None
        kf = sb("kf", [P, NK])
        kr = sb("kr", [P, NK])
        kparts = sb("kparts", [P, 3, NK], BF16)
        qf = sb("qf", [P, SEQ])
        qr = sb("qr", [P, SEQ])
        qparts = sb("qparts", [P, 3, SEQ], BF16)
        KS = sb("KS", [P, PAIRS, NK], BF16)
        QS = sb("QS", [P, PAIRS, SEQ], BF16)
        V = sb("V", [P, KT, HEADS, HD + 1])
        PT = [sb(f"PT{i}", [P, 2, 512]) for i in range(3)]
        mx = sb("mx", [P, PAIRS, QT * 2, NC])
        mm = sb("mm", [P, PAIRS, QT * 2])
        MB = sb("MB", [P, PAIRS, QT * 2, 2], BF16)
        MT = [sb(f"MT{i}", [4, SEQ], BF16) for i in range(2)]
        junk = [sb(f"junk{i}", [P, 512], BF16) for i in range(2)] if mask is not None else None
        osb = [sb(f"osb{i}", [P, SEQ]) for i in range(2)]
        oc = sb("oc", [P, QT, HEADS, HD + 1])
        rec = sb("rec", [P, QT, HEADS, 1])
        attn = sb("attn", [P, QT, DIM])
        attnT = sb("attnT", [P, SEQ])
        y = sb("y", [P, QT, DIM])
        if mask is not None:
            mask_i = sb("mask_i", [P, QT, CTX], I32)
            maskq = sb("maskq", [P, QT, CTX], BF16)
            maskT_i = sb("maskT_i", [P, KT, SEQ], I32)
            maskk = sb("maskk", [P, KT, SEQ], BF16)
        if hard:
            hs = sb("hs", [P, QT, CTX])
            rowbase = sb("rowbase", [P, 1])
            hmax = sb("hmax", [P, QT, 8])
            hidx = sb("hidx", [P, QT, 8], U32)
            mem = sb("mem", [P, QT, DIM])
            qpT = sb("qpT", [P, SEQ])
        ST = [ps(f"ST{i}", [P, 2, 512]) for i in range(2)]
        SQ = [ps(f"SQ{i}", [P, 512]) for i in range(2)]
        O = ps("O", [P, 512])
        misc = ps("misc", [P, 512])
        miscb = misc[:, :].bitcast(BF16)

        names = ("consts_in x_in ctx_in mask_in setup chain_v xn_ready xT_done xT_ready proj_q proj_k "
                 "proj_v kf_ready q_split k_split k_hi qs_in ks_in v_ready mask_ready sq_done max_done mb_ready "
                 "mt_done mtc_done pair_done st_raw clipped st_done exp_done pv_done o_copied fin_done "
                 "attn_ready at_done at_ready out_done y_ready y_out hs_done hs_copied idx_ready base_in mem_ready memT_done "
                 "memT_ready").split()
        S = {n: sem(n) for n in names}
        mem_in = ctx.enter_context(nc.semaphore(f"{tag}_mem_in")) if hard else None
        m_in = [sem(f"m_in{p}") for p in range(PAIRS)]

        def convert_masks(pool):
            k = keys(KT - 1)
            pool.tensor_scalar(maskq[:, :, :], mask_i[:, :, :], 0, MASKED, ALU.is_equal, ALU.mult).then_inc(S["mask_ready"], 1)
            pool.wait_ge(S["mask_ready"], 1)
            pool.tensor_scalar(maskk[:, 0:KT - 1, :], maskT_i[:, 0:KT - 1, :], 0, MASKED, ALU.is_equal, ALU.mult).then_inc(S["mask_ready"], 1)
            pool.wait_ge(S["mask_ready"], 2)
            pool.tensor_scalar(maskk[0:k, KT - 1, :], maskT_i[0:k, KT - 1, :], 0, MASKED, ALU.is_equal, ALU.mult).then_inc(S["mask_ready"], 1)

        with nc.Block() as block:
            @block.sync
            def _(sp):
                for dst, src in ((ident, consts["ident"]), (pick, consts["pick"]), (shiftsel_f, consts["shiftsel"])):
                    sp.dma_start(dst[:, :], src).then_inc(S["consts_in"], 16)
                for k in wsb:
                    sp.dma_start(wsb[k][:, :], w[k]).then_inc(S["setup"], 16)
                for k in cols:
                    sp.dma_start(cols[k][:, :], w[k].rearrange("(p o) -> p o", o=1)).then_inc(S["setup"], 16)
                for k in rows:
                    sp.dma_start(rows[k][:, :], w[k].rearrange("(o n) -> o n", o=1).broadcast_to([P, P])).then_inc(S["setup"], 16)
                sp.wait_ge(S["setup"], 16 * (len(wsb) + len(cols) + len(rows)))
                if MASK_ONCE:
                    sp.dma_start(mask_i[:, :, :], mask[0, 0].rearrange("(t p) k -> p t k", p=P)).then_inc(S["mask_in"], 16)
                    sp.dma_start(maskT_i[:, 0:KT - 1, :], maskT[0, 0:(KT - 1) * P].rearrange("(t p) q -> p t q", p=P)).then_inc(S["mask_in"], 16)
                    sp.dma_start(maskT_i[0:keys(KT - 1), KT - 1, :], maskT[0, (KT - 1) * P:NK]).then_inc(S["mask_in"], 16)

            @block.gpsimd
            def _(pool):
                if MASK_ONCE:
                    pool.wait_ge(S["mask_in"], 48)
                    convert_masks(pool)

            @block.vector
            def _(dve):
                dve.memset(V[:, :, :, :], 1.0)
                for half in (32, 96):
                    dve.memset(KS[half:half + 32, :, :], 1.0)
                    dve.memset(QS[half:half + 32, :, :], 0.0)
                dve.wait_ge(S["consts_in"], 48)
                dve.tensor_copy(identb[:, :], ident[:, :])
                dve.tensor_copy(shiftsel[:, :], shiftsel_f[:, :])

        ph.barrier()

        def item(i):
            p, r = divmod(i, ITEMS)
            col, c = divmod(r, NC)
            return p, col, col // 2, col % 2, c

        def items_of_slot(p, kp):
            if p + AHEAD >= PAIRS:
                return range(0)
            a, b = ITEMS * kp // KP, ITEMS * (kp + 1) // KP
            return range((p + AHEAD) * ITEMS + a, (p + AHEAD) * ITEMS + b)

        QPROD = (0, 1, 0, 1, 2, 0)
        KPROD = (0, 0, 1, 1, 0, 2)

        with nc.Fori(0, LOOPS) as b:
            with nc.Block() as block:
                @block.sync
                def _(sp):
                    sp.dma_start(x_sb[:, :, :], x_in[b].rearrange("(t p) c -> p t c", p=P)).then_inc(S["x_in"], 16)
                    if ctxT is not None:
                        sp.dma_start(srcT[:, :], ctxT[b]).then_inc(S["ctx_in"], 16)
                    if hard:
                        sp.dma_start(rowbase[:, :], consts["rowbase"][b].rearrange("(p o) -> p o", o=1)).then_inc(S["base_in"], 16)
                    if mask is not None and not MASK_ONCE:
                        sp.dma_start(mask_i[:, :, :], mask[b, 0].rearrange("(t p) k -> p t k", p=P)).then_inc(S["mask_in"], 16)
                        sp.dma_start(maskT_i[:, 0:KT - 1, :], maskT[b, 0:(KT - 1) * P].rearrange("(t p) q -> p t q", p=P)).then_inc(S["mask_in"], 16)
                        sp.dma_start(maskT_i[0:keys(KT - 1), KT - 1, :], maskT[b, (KT - 1) * P:NK]).then_inc(S["mask_in"], 16)
                    sp.wait_ge(S["q_split"], 3)
                    for par in range(2):
                        for r, part in enumerate(QPROD):
                            at = HALF * par + HD * r
                            sp.dma_start(QS[at:at + HD, :, :], qparts[HALF * par:HALF * par + HALF, part, :]).then_inc(S["qs_in"], 16)
                    sp.wait_ge(S["k_hi"], 1)
                    sp.wait_ge(S["k_split"], 3)
                    for par in range(2):
                        for r, part in enumerate(KPROD):
                            at = HALF * par + HD * r
                            sp.dma_start(KS[at:at + HD, :, :], kparts[HALF * par:HALF * par + HALF, part, :]).then_inc(S["ks_in"], 16)
                    for p in range(PAIRS):
                        sp.wait_ge(S["mtc_done"], p + 1)
                        for par in range(2):
                            at = HALF * par + SHIFT
                            sp.dma_start(QS[at:at + 2, p, :], MT[p % 2][2 * par:2 * par + 2, :]).then_inc(m_in[p], 16)
                    sp.wait_ge(S["y_ready"], 1)
                    sp.dma_start(x_out[b].rearrange("(t p) c -> p t c", p=P), y[:, :, :]).then_inc(S["y_out"], 16)
                    sp.wait_ge(S["y_out"], 16)

                @block.gpsimd
                def _(pool):
                    if mask is not None and not MASK_ONCE:
                        pool.wait_ge(S["mask_in"], 48)
                        convert_masks(pool)
                    if hard:
                        pool.wait_ge(S["idx_ready"], 1)
                        for t in range(QT):
                            pool.indirect_dma_start(mem[:, t, :], None, ctx_rows,
                                                    bass.IndirectOffsetOnAxis(ap=hidx[:, t, 0:1], axis=0)).then_inc(mem_in, 16)
                        pool.wait_ge(mem_in, (b + 1) * (16 * QT))
                        pool.sem_inc(S["mem_ready"], 1)

                @block.scalar
                def _(act):
                    act.wait_ge(S["proj_k"], 1)
                    for c in range(NC):
                        bank = ST[c // 2][:, c % 2, 0:chunk(c)]
                        if "bk" in w:
                            ins = act.activation(kf[:, c * 512:c * 512 + chunk(c)], bank, ACT.Identity, bias=cols["bk"][:, :])
                        else:
                            ins = act.copy(kf[:, c * 512:c * 512 + chunk(c)], bank)
                        ins.then_inc(S["kf_ready"], 1)
                    act.wait_ge(S["kf_ready"], NC)
                    act.copy(kparts[:, 0, :], kf[:, :]).then_inc(S["k_hi"], 1)
                    act.wait_ge(S["proj_v"], 1)
                    for g in range(ceil(KT, 4)):
                        bank = (SQ[0], SQ[1], O, misc)[g]
                        full = [kt for kt in range(4 * g, min(4 * g + 4, KT)) if keys(kt) == P]
                        if full:
                            act.copy(V[:, full[0]:full[-1] + 1, :, 0:HD],
                                     bank[:, 0:P * len(full)].rearrange("p (t h d) -> p t h d", t=len(full), d=HD)).then_inc(S["v_ready"], 1)
                        for kt in range(4 * g, min(4 * g + 4, KT)):
                            if keys(kt) < P:
                                k = kt - 4 * g
                                act.copy(V[0:keys(kt), kt, :, 0:HD],
                                         bank[0:keys(kt), k * P:(k + 1) * P].rearrange("p (h d) -> p h d", d=HD)).then_inc(S["v_ready"], 1)
                    for n in range(N):
                        p, kp = divmod(n, KP)
                        act.wait_ge(S["st_done"], n + 1)
                        if n >= 3:
                            act.wait_ge(S["pv_done"], n - 2)
                        tiles = min(2, KT - 2 * kp)
                        k = keys(2 * kp)
                        act.activation(PT[n % 3][0:k, :, 0:SEQ * tiles], ST[n % 2][0:k, :, 0:SEQ * tiles], ACT.Exp,
                                       ).then_inc(S["exp_done"], 1)

                @block.tensor
                def _(pe):
                    last_reader = []

                    def take_misc(name, count):
                        if last_reader:
                            pe.wait_ge(S[last_reader[-1][0]], last_reader[-1][1])
                        last_reader.append((name, count))

                    pe.wait_ge(S["xn_ready"], 1)
                    for t in range(QT):
                        mt = pe.transpose(misc[:, t * P:(t + 1) * P], (xn2 if self_ln else xn)[:, t, :], ident[:, :])
                    mt.then_inc(S["xT_done"], 1)
                    pe.wait_ge(S["xT_ready"], 1)
                    pe.matmul(O[:, 0:SEQ], wsb["wq"][:, :], xT[:, :], start=True, stop=True).then_inc(S["proj_q"], 1)
                    if hard:
                        pe.matmul(O[:, SEQ:2 * SEQ], wsb["wqn"][:, :], xT[:, :], start=True, stop=True).then_inc(S["proj_q"], 1)
                    if ctxT is not None:
                        pe.wait_ge(S["ctx_in"], 16)
                    if hard:
                        pe.wait_ge(S["q_split"], 4)
                        for t in range(QT):
                            if t:
                                pe.wait_ge(S["hs_copied"], 4 * t)
                            for c in range(4):
                                n = min(512, CTX - 512 * c)
                                pe.matmul(ST[c // 2][:, c % 2, 0:n], qpT[:, t * P:(t + 1) * P], srcT[:, c * 512:c * 512 + n],
                                          start=True, stop=True).then_inc(S["hs_done"], 1)
                        pe.wait_ge(S["hs_copied"], 4 * QT)
                        pe.wait_ge(S["mem_ready"], 1)
                        for t in range(QT):
                            mt = pe.transpose(misc[:, t * P:(t + 1) * P], mem[:, t, :], ident[:, :])
                        mt.then_inc(S["memT_done"], 1)
                        pe.wait_ge(S["memT_ready"], 1)
                    kv = memT if hard else (srcT if ctxT is not None else xT)
                    for c in range(NC):
                        mt = pe.matmul(ST[c // 2][:, c % 2, 0:chunk(c)], wsb["wk"][:, :], kv[:, c * 512:c * 512 + chunk(c)],
                                       start=True, stop=True)
                    mt.then_inc(S["proj_k"], 1)
                    pe.wait_ge(S["q_split"], 1)
                    for kt in range(KT):
                        bank = (SQ[0], SQ[1], O, misc)[kt // 4]
                        mt = pe.matmul(bank[0:keys(kt), kt % 4 * P:(kt % 4 + 1) * P], kv[:, kt * P:kt * P + keys(kt)], wsb["wv"][:, :],
                                       start=True, stop=True)
                    mt.then_inc(S["proj_v"], 1)
                    pe.wait_ge(S["v_ready"], ceil(KT, 4))

                    def sq(i):
                        p, col, qt, par, c = item(i)
                        if i >= 2:
                            pe.wait_ge(S["max_done"], i - 1)
                        at = HALF * par
                        pe.matmul(SQ[i % 2][:, 0:chunk(c)], QS[at:at + PARTS, p, qt * P:(qt + 1) * P],
                                  KS[at:at + PARTS, p, c * 512:c * 512 + chunk(c)], start=True, stop=True).then_inc(S["sq_done"], 1)

                    def turn_maxima(p):
                        pe.wait_ge(S["mb_ready"], p + 1)
                        take_misc("mtc_done", p + 1)
                        for qt in range(QT):
                            ins = pe.transpose(miscb[0:4, qt * P:(qt + 1) * P], MB[:, p, 2 * qt:2 * qt + 2, :].rearrange("p a b -> p (a b)"),
                                               identb[:, :])
                        ins.then_inc(S["mt_done"], 1)

                    def add_mask(n, start):
                        p, kp = divmod(n, KP)
                        tiles = min(2, KT - 2 * kp)
                        k = keys(2 * kp)
                        for par in range(2):
                            pe.matmul(ST[n % 2][0:k, par, 0:SEQ * tiles], identb[0:k, 0:k],
                                      maskk[0:k, 2 * kp:2 * kp + tiles, :].rearrange("p t q -> p (t q)"),
                                      start=start, stop=False, skip_group_check=True)

                    def scores(n):
                        p, kp = divmod(n, KP)
                        if n >= 2:
                            pe.wait_ge(S["exp_done"], n - 1)
                        if kp == 0 and not clip:
                            pe.wait_ge(m_in[p], 32)
                        if mask is not None and not clip:
                            add_mask(n, True)
                        rows_k = PARTS if clip else HALF
                        for kt in range(2 * kp, min(2 * kp + 2, KT)):
                            for par in range(2):
                                at = HALF * par
                                ins = pe.matmul(ST[n % 2][0:keys(kt), par, kt % 2 * SEQ:(kt % 2 + 1) * SEQ],
                                                KS[at:at + rows_k, p, kt * P:kt * P + keys(kt)], QS[at:at + rows_k, p, :],
                                                start=(kt % 2 == 0 and not (mask is not None and not clip)), stop=True, skip_group_check=True)
                        ins.then_inc(S["st_raw" if clip else "st_done"], 1)

                    def shift(n):
                        p, kp = divmod(n, KP)
                        if kp == 0:
                            pe.wait_ge(m_in[p], 32)
                        pe.wait_ge(S["clipped"], n + 1)
                        add_mask(n, False)
                        for kt in range(2 * kp, min(2 * kp + 2, KT)):
                            for par in range(2):
                                at = HALF * par
                                ins = pe.matmul(ST[n % 2][0:keys(kt), par, kt % 2 * SEQ:(kt % 2 + 1) * SEQ],
                                                shiftsel[at:at + HALF, 0:keys(kt)], QS[at:at + HALF, p, :],
                                                start=False, stop=True, skip_group_check=True)
                        ins.then_inc(S["st_done"], 1)

                    def weigh(n):
                        p, kp = divmod(n, KP)
                        pe.wait_ge(S["exp_done"], n + 1)
                        if kp == 0 and p:
                            pe.wait_ge(S["o_copied"], p)
                        for kt in range(2 * kp, min(2 * kp + 2, KT)):
                            for par in range(2):
                                at = 32 * (2 * (kt % 2) + par)
                                ins = pe.matmul(O[at:at + HD + 1, 0:SEQ], V[0:keys(kt), kt, 2 * p + par, :],
                                                PT[n % 3][0:keys(kt), par, kt % 2 * SEQ:(kt % 2 + 1) * SEQ],
                                                start=(kt < 2), stop=(kt + 2 >= KT), skip_group_check=True)
                        ins.then_inc(S["pv_done"], 1)

                    def gather_pair(p):
                        pe.wait_ge(S["o_copied"], p + 1)
                        take_misc("pair_done", p + 1)
                        for qt in range(QT):
                            ins = pe.matmul(misc[:, qt * 18:(qt + 1) * 18], osb[p % 2][:, qt * P:(qt + 1) * P], pick[:, :],
                                            start=(qt == 0), stop=True, skip_group_check=True)
                        ins.then_inc(S["fin_done"], 1)

                    pe.wait_ge(S["qs_in"], 16 * 12)
                    pe.wait_ge(S["ks_in"], 16 * 12)
                    if mask is not None and not MASK_ONCE:
                        pe.wait_ge(S["mask_ready"], 3)
                    for i in range(AHEAD * ITEMS):
                        sq(i)
                    for p in range(AHEAD - 1):
                        turn_maxima(p)
                    scores(0)
                    for n in range(N):
                        p, kp = divmod(n, KP)
                        if clip:
                            shift(n)
                        if n:
                            weigh(n - 1)
                        if n + 1 < N:
                            scores(n + 1)
                        for i in items_of_slot(p, kp):
                            sq(i)
                        if kp == 0 and p + AHEAD - 1 < PAIRS:
                            turn_maxima(p + AHEAD - 1)
                        if kp == min(1, KP - 1) and p:
                            gather_pair(p - 1)
                    weigh(N - 1)
                    gather_pair(PAIRS - 1)

                    pe.wait_ge(S["attn_ready"], 1)
                    for t in range(QT):
                        ins = pe.transpose(ST[0][:, 0, t * P:(t + 1) * P], attn[:, t, :], ident[:, :])
                    ins.then_inc(S["at_done"], 1)
                    pe.wait_ge(S["at_ready"], 1)
                    for t in range(QT):
                        ins = pe.matmul(ST[1][:, 0, t * P:(t + 1) * P], attnT[:, t * P:(t + 1) * P], wsb["wo"][:, :],
                                        start=(t == 0), stop=True, skip_group_check=True)
                    ins.then_inc(S["out_done"], 1)

                @block.vector
                def _(dve):
                    chain = Chain(dve, S["chain_v"])

                    def normalise(src, dst):
                        for t in range(QT):
                            ins = dve.bn_stats(stats[:, t, :], src[:, t, :])
                        chain(ins)
                        for t in range(QT):
                            ins = dve.bn_aggr(mv[:, t, :], stats[:, t, :])
                        chain(ins)
                        inverse_root(dve, chain, rstd[:, :, :], mv[:, :, 1:2], var, root)
                        for t in range(QT):
                            ins = dve.tensor_scalar(dst[:, t, :], src[:, t, :], mv[:, t, 0:1], rstd[:, t, :], ALU.subtract, ALU.mult)
                        return ins

                    dve.wait_ge(S["x_in"], 16)
                    ins = normalise(x_sb, xn)
                    if self_ln:
                        chain(ins)
                        ins = normalise(xn, xn2)
                    ins.then_inc(S["xn_ready"], 1)
                    dve.wait_ge(S["xT_done"], 1)
                    if self_ln:
                        ins = dve.tensor_scalar(xT[:, :], misc[:, 0:SEQ], cols["lng"][:, :], cols["lnb"][:, :], ALU.mult, ALU.add)
                    else:
                        ins = dve.tensor_copy(xT[:, :], misc[:, 0:SEQ])
                    ins.then_inc(S["xT_ready"], 1)

                    dve.wait_ge(S["proj_q"], 2 if hard else 1)
                    if "bq" in w:
                        chain(dve.tensor_scalar(qf[:, :], O[:, 0:SEQ], cols["bq"][:, :], scale, ALU.add, ALU.mult))
                    else:
                        chain(dve.tensor_scalar(qf[:, :], O[:, 0:SEQ], scale, None, ALU.mult))
                    dve.tensor_copy(qparts[:, 0, :], qf[:, :]).then_inc(S["q_split"], 1)
                    dve.wait_ge(S["q_split"], 1)
                    chain(dve.tensor_tensor(qr[:, :], qf[:, :], qparts[:, 0, :], ALU.subtract))
                    dve.tensor_copy(qparts[:, 1, :], qr[:, :]).then_inc(S["q_split"], 1)
                    dve.wait_ge(S["q_split"], 2)
                    dve.tensor_tensor(qparts[:, 2, :], qr[:, :], qparts[:, 1, :], ALU.subtract).then_inc(S["q_split"], 1)

                    if hard:
                        dve.tensor_copy(qpT[:, :], O[:, SEQ:2 * SEQ]).then_inc(S["q_split"], 1)
                        for t in range(QT):
                            for c in range(4):
                                n = min(512, CTX - 512 * c)
                                dve.wait_ge(S["hs_done"], 4 * t + c + 1)
                                dve.tensor_copy(hs[:, t, c * 512:c * 512 + n], ST[c // 2][:, c % 2, 0:n]).then_inc(S["hs_copied"], 1)
                            dve.wait_ge(S["hs_copied"], 4 * t + 4)
                            chain(dve.max(hmax[:, t, :], hs[:, t, :]))
                            ins = dve.max_index(hidx[:, t, :], hmax[:, t, :], hs[:, t, :])
                            if t < QT - 1:
                                chain(ins)
                        chain(ins)
                        dve.wait_ge(S["base_in"], 16)
                        dve.tensor_scalar(hidx[:, :, 0:1], hidx[:, :, 0:1], rowbase[:, :], None, ALU.add).then_inc(S["idx_ready"], 1)
                        dve.wait_ge(S["memT_done"], 1)
                        dve.tensor_copy(memT[:, :], misc[:, 0:SEQ]).then_inc(S["memT_ready"], 1)

                    dve.wait_ge(S["k_hi"], 1)
                    dve.tensor_tensor(kr[:, :], kf[:, :], kparts[:, 0, :], ALU.subtract).then_inc(S["k_split"], 1)
                    dve.wait_ge(S["k_split"], 1)
                    dve.tensor_copy(kparts[:, 1, :], kr[:, :]).then_inc(S["k_split"], 1)
                    dve.wait_ge(S["k_split"], 2)
                    dve.tensor_tensor(kparts[:, 2, :], kr[:, :], kparts[:, 1, :], ALU.subtract).then_inc(S["k_split"], 1)

                    def maximum(i):
                        p, col, qt, par, c = item(i)
                        dve.wait_ge(S["sq_done"], i + 1)
                        n = chunk(c)
                        if mask is not None:
                            if i >= 2:
                                dve.wait_ge(S["max_done"], i - 1)
                            dve.tensor_tensor_reduce(out=junk[i % 2][:, 0:n], in0=SQ[i % 2][:, 0:n], in1=maskq[:, qt, c * 512:c * 512 + n],
                                                     scale=1.0, scalar=-3e38, op0=ALU.add, op1=ALU.max,
                                                     accum_out=mx[:, p, col, c:c + 1]).then_inc(S["max_done"], 1)
                        else:
                            dve.tensor_reduce(mx[:, p, col, c:c + 1], SQ[i % 2][:, 0:n], AX.X, ALU.max).then_inc(S["max_done"], 1)

                    def split_maxima(p):
                        dve.wait_ge(S["max_done"], (p + 1) * ITEMS)
                        if NC > 1:
                            chain(dve.tensor_reduce(mm[:, p, :], mx[:, p, :, :], AX.X, ALU.max))
                            m = mm
                        else:
                            m = mx[:, :, :, 0]
                        if clip:
                            chain(dve.tensor_scalar(mm[:, p, :], m[:, p, :], clip, -clip, ALU.min, ALU.max))
                            m = mm
                        chain(dve.tensor_scalar(MB[:, p, :, 0], m[:, p, :], -1.0, None, ALU.mult))
                        dve.scalar_tensor_tensor(MB[:, p, :, 1], m[:, p, :], -1.0, MB[:, p, :, 0], ALU.mult, ALU.subtract).then_inc(S["mb_ready"], 1)

                    def copy_maxima(p):
                        dve.wait_ge(S["mt_done"], p + 1)
                        if p >= 2:
                            dve.wait_ge(m_in[p - 2], 32)
                        dve.tensor_copy(MT[p % 2][:, :], miscb[0:4, 0:SEQ]).then_inc(S["mtc_done"], 1)

                    def copy_pair(p):
                        dve.wait_ge(S["pv_done"], (p + 1) * KP)
                        if p >= 2:
                            dve.wait_ge(S["fin_done"], p - 1)
                        dve.tensor_copy(osb[p % 2][:, :], O[:, 0:SEQ]).then_inc(S["o_copied"], 1)

                    def collect_pair(p):
                        dve.wait_ge(S["fin_done"], p + 1)
                        dve.tensor_copy(oc[:, :, 2 * p:2 * p + 2, :], misc[:, 0:36].rearrange("p (t h d) -> p t h d", t=QT, d=HD + 1)).then_inc(S["pair_done"], 1)

                    def clip_scores(n):
                        p, kp = divmod(n, KP)
                        tiles = min(2, KT - 2 * kp)
                        k = keys(2 * kp)
                        dve.wait_ge(S["st_raw"], n + 1)
                        v = ST[n % 2][0:k, :, 0:SEQ * tiles]
                        dve.tensor_scalar(v, v, clip, -clip, ALU.min, ALU.max).then_inc(S["clipped"], 1)

                    if mask is not None and not MASK_ONCE:
                        dve.wait_ge(S["mask_ready"], 3)
                    for p in range(AHEAD):
                        for i in range(p * ITEMS, (p + 1) * ITEMS):
                            maximum(i)
                        split_maxima(p)
                    for p in range(AHEAD - 1):
                        copy_maxima(p)
                    for n in range(N):
                        p, kp = divmod(n, KP)
                        if clip:
                            clip_scores(n)
                        for i in items_of_slot(p, kp):
                            maximum(i)
                        if kp == KP - 1 and p + AHEAD < PAIRS:
                            split_maxima(p + AHEAD)
                        if kp == 0 and p:
                            copy_pair(p - 1)
                        if kp == 0 and p + AHEAD - 1 < PAIRS:
                            copy_maxima(p + AHEAD - 1)
                        if kp == min(1, KP - 1) and p:
                            collect_pair(p - 1)
                    copy_pair(PAIRS - 1)
                    collect_pair(PAIRS - 1)

                    dve.wait_ge(S["pair_done"], PAIRS)
                    chain(dve.reciprocal(rec[:, :, :, :], oc[:, :, :, HD:HD + 1]))
                    av = attn[:, :, :].rearrange("p t (h d) -> p t h d", d=HD)
                    for t in range(QT):
                        ins = dve.tensor_tensor(av[:, t], oc[:, t, :, 0:HD], rec[:, t, :, :].broadcast_to([P, HEADS, HD]), ALU.mult)
                        if "bv" in w:
                            chain(ins)
                            ins = dve.tensor_tensor(attn[:, t, :], attn[:, t, :], rows["bv"][:, :], ALU.add)
                    ins.then_inc(S["attn_ready"], 1)
                    dve.wait_ge(S["at_done"], 1)
                    dve.tensor_copy(attnT[:, :], ST[0][:, 0, 0:SEQ]).then_inc(S["at_ready"], 1)
                    dve.wait_ge(S["out_done"], 1)
                    base = xn if self_ln else x_sb
                    ins = dve.tensor_tensor(y[:, :, :], ST[1][:, 0, 0:SEQ].rearrange("p (t c) -> p t c", t=QT), base[:, :, :], ALU.add)
                    if "bo" in w:
                        chain(ins)
                        for t in range(QT):
                            ins = dve.tensor_tensor(y[:, t, :], y[:, t, :], rows["bo"][:, :], ALU.add)
                    ins.then_inc(S["y_ready"], 1)
            ph.barrier()


def top_k(dve, chain, values, k, tri, greater, equal, rank, chosen):
    _, T, E = values.shape
    a = values.unsqueeze(3).broadcast_to([P, T, E, E])
    b = values.unsqueeze(2).broadcast_to([P, T, E, E])
    dve.tensor_tensor(greater, a, b, ALU.is_gt)
    chain(dve.tensor_tensor(equal, a, b, ALU.is_equal))
    chain(dve.tensor_tensor(equal, equal, tri.unsqueeze(1).broadcast_to([P, T, E, E]), ALU.mult))
    chain(dve.tensor_tensor(greater, greater, equal, ALU.add))
    chain(dve.tensor_reduce(rank, greater.rearrange("p t a b -> p t b a"), AX.X, ALU.add))
    chain(dve.tensor_scalar(chosen, rank, float(k), None, ALU.is_lt))


def experts_phase(nc, tag, kind, x_in, x_out, w, consts, extra=None):
    E, TT, D = 8, 4, DIM
    TOK = TT * P
    FT = 3 if kind == "silu" else 4
    FP = 114 if kind == "silu" else P
    STEPS = E * FT
    CHUNKS = LOOPS * SEQ // TOK
    two = kind != "relu"

    with ExitStack() as ctx:
        ph = Phase(nc, ctx, tag)
        sb, ps, sem = ph.sb, ph.ps, ph.sem
        ident = sb("ident", [P, P])
        tri = sb("tri", [P, E, E])
        onehot = sb("onehot", [E, E, P])
        W1 = sb("W1", [P, E, FT * FP])
        Wg = sb("Wg", [P, E, FT * FP]) if two else None
        W2 = sb("W2", [FP, E, FT, D])
        b1 = sb("b1", [FP, STEPS])
        bg = sb("bg", [FP, STEPS]) if two else None
        b2 = sb("b2", [E, D]) if kind != "clip" else None
        bo = sb("bo", [P, E]) if kind == "clip" else None
        eg = sb("eg", [P, E]) if kind == "clip" else None
        eb = sb("eb", [P, E]) if kind == "clip" else None
        gw = sb("gw", [P, E])
        gb = sb("gb", [P, E]) if kind == "relu" else None
        lng = sb("lng", [P, D]) if kind == "clip" else (sb("lng", [P, 1]) if kind == "relu" else None)
        lnb = sb("lnb", [P, D]) if kind == "clip" else (sb("lnb", [P, 1]) if kind == "relu" else None)
        ones = sb("ones", [P, P]) if kind == "silu" else None
        csq = sb("csq", [P, E]) if kind == "silu" else None
        x_sb = sb("x_sb", [P, TT, D])
        r_sb = sb("r_sb", [P, TT, D]) if kind == "relu" else None
        stats = sb("stats", [P, TT, 6])
        mv = sb("mv", [P, TT, 2])
        rstd = sb("rstd", [P, TT, 1])
        var = sb("var", [P, TT, 1])
        root = sb("root", [P, TT, 1])
        xn = sb("xn", [P, TT, D])
        xm = sb("xm", [P, TT, D]) if kind == "clip" else None
        xT = sb("xT", [P, TOK])
        cT = sb("cT", [P, TOK]) if kind == "clip" else None
        eT = [sb(f"eT{i}", [P, TOK]) for i in range(2)] if kind == "clip" else [xT, xT]
        sq = sb("sq", [P, TT, D]) if kind == "silu" else None
        nrm = sb("nrm", [P, TT, 1])
        L = sb("L", [P, TT, E])
        d2 = sb("d2", [P, TT, E])
        t8 = sb("t8", [P, TT, E])
        greater = sb("greater", [P, TT, E, E])
        equal = sb("equal", [P, TT, E, E])
        rank = sb("rank", [P, TT, E])
        chosen = sb("chosen", [P, TT, E])
        top = sb("top", [P, TT, 1])
        total = sb("total", [P, TT, 1])
        gates = sb("gates", [P, TT, E])
        gT = sb("gT", [E, TOK])
        gB = [sb(f"gB{i}", [P, TOK]) for i in range(2)]
        A = [sb(f"A{i}", [FP, TOK]) for i in range(3)]
        C = [sb(f"C{i}", [FP, TOK]) for i in range(3)] if kind == "clip" else None
        Cm = [sb(f"Cm{i}", [FP, TOK]) for i in range(3)] if kind == "clip" else None
        T = [sb(f"T{i}", [FP, TOK]) for i in range(3)] if two else None
        Hg = [sb(f"Hg{i}", [FP, TOK]) for i in range(3)]
        yo = sb("yo", [P, TOK]) if kind == "clip" else None
        yg = sb("yg", [P, TOK]) if kind == "clip" else None
        yT = sb("yT", [P, TOK])
        out = sb("out", [P, TT, D])
        up1 = [ps(f"up1_{i}", [P, TOK]) for i in range(2)]
        upg = [ps(f"upg_{i}", [P, TOK]) for i in range(2)]
        Y = [ps(f"Y{i}", [P, TOK]) for i in range(2)]
        GB = ps("GB", [P, TOK])
        misc = ps("misc", [P, TOK])

        names = ("setup consts_in csq_ready x_in chain_v xn_ready xT_done xT_ready xc_ready logits_done shifted gate_exp gates_ready gT_done "
                 "gT_ready gb_done gb_ready e_ready up_done pre_done low_done act_done prod_done gated down_done y_done y_taken acc_step yT_ready "
                 "out_done out_ready out_sent").split()
        S = {n: sem(n) for n in names}

        with nc.Block() as block:
            @block.sync
            def _(sp):
                loads = [(ident[:, :], consts["ident"]), (tri[:, :, :], consts["tri8"]), (onehot[:, :, :], consts["onehot"]),
                         (W1[:, :, :], w["W1"]), (W2[:, :, :, :], w["W2"]), (b1[:, :], w["b1"])]
                if two:
                    loads += [(Wg[:, :, :], w["Wg"]), (bg[:, :], w["bg"])]
                if kind == "clip":
                    loads += [(bo[:, :], w["bo"]), (eg[:, :], w["eg"]), (eb[:, :], w["eb"])]
                    loads += [(t[:, :], w[n].rearrange("(o n) -> o n", o=1).broadcast_to([P, D])) for t, n in ((lng, "lng"), (lnb, "lnb"))]
                else:
                    loads += [(b2[:, :], w["b2"])]
                if kind == "relu":
                    loads += [(t[:, :], w[n].rearrange("(p o) -> p o", o=1)) for t, n in ((lng, "lng"), (lnb, "lnb"))]
                    loads += [(gb[:, :], w["gb"].rearrange("(o n) -> o n", o=1).broadcast_to([P, E]))]
                sp.dma_start(gw[:, :], w["gw"]).then_inc(S["consts_in"], 16)
                for dst, src in loads:
                    sp.dma_start(dst, src).then_inc(S["setup"], 16)
                sp.wait_ge(S["setup"], 16 * len(loads))

            @block.vector
            def _(dve):
                dve.wait_ge(S["consts_in"], 16)
                if kind == "silu":
                    dve.memset(ones[:, :], 1.0)
                    dve.tensor_tensor(csq[:, :], gw[:, :], gw[:, :], ALU.mult).then_inc(S["csq_ready"], 1)
                    dve.wait_ge(S["csq_ready"], 1)
                    dve.tensor_scalar(gw[:, :], gw[:, :], -2.0, None, ALU.mult)
        ph.barrier()

        with nc.Fori(0, CHUNKS) as i:
            rows = x_in.rearrange("b s c -> (b s) c").rearrange("(n t p) c -> n p t c", t=TT, p=P)
            rows_out = x_out.rearrange("b s c -> (b s) c").rearrange("(n t p) c -> n p t c", t=TT, p=P)
            with nc.Block() as block:
                @block.sync
                def _(sp):
                    sp.dma_start(x_sb[:, :, :], rows[i]).then_inc(S["x_in"], 16)
                    if kind == "relu":
                        sp.dma_start(r_sb[:, :, :], extra.rearrange("b s c -> (b s) c").rearrange("(n t p) c -> n p t c", t=TT, p=P)[i]
                                     ).then_inc(S["x_in"], 16)
                    sp.wait_ge(S["out_ready"], 1)
                    sp.dma_start(rows_out[i], out[:, :, :]).then_inc(S["out_sent"], 16)
                    sp.wait_ge(S["out_sent"], 16)

                @block.gpsimd
                def _(pool):
                    def low(s):
                        pool.wait_ge(S["pre_done"], s + 1)
                        if s >= 3:
                            pool.wait_ge(S["act_done"], s - 2)
                        pool.tensor_scalar(Cm[s % 3][:, :], C[s % 3][:, :], -20.0, None, ALU.max).then_inc(S["low_done"], 1)

                    if kind == "clip":
                        low(0)
                    if two:
                        for s in range(STEPS):
                            if kind == "clip" and s + 1 < STEPS:
                                low(s + 1)
                            pool.wait_ge(S["prod_done"], s + 1)
                            if s >= 3:
                                pool.wait_ge(S["down_done"], s - 2)
                            if kind == "clip":
                                ins = pool.tensor_scalar(Hg[s % 3][:, :], T[s % 3][:, :], 1e4, -1e4, ALU.min, ALU.max)
                            else:
                                if s % FT == 0:
                                    pool.wait_ge(S["gb_ready"], s // FT + 1)
                                ins = pool.tensor_tensor(Hg[s % 3][:, :], T[s % 3][:, :], gB[s // FT % 2][0:FP, :], ALU.mult)
                            ins.then_inc(S["gated"], 1)

                @block.scalar
                def _(act):
                    act.wait_ge(S["shifted"], 1)
                    act.activation(t8[:, :, :], L[:, :, :], ACT.Exp).then_inc(S["gate_exp"], 1)
                    for s in range(STEPS):
                        if kind == "clip":
                            act.wait_ge(S["low_done"], s + 1)
                            src, bias = Cm[s % 3][:, :], 0.0
                        else:
                            act.wait_ge(S["up_done"], s + 1)
                            src = (upg if two else up1)[s % 2][0:FP, :]
                            bias = (bg if two else b1)[:, s:s + 1]
                        if s >= 3:
                            act.wait_ge(S["prod_done" if two else "gated"], s - 2)
                        act.activation(A[s % 3][:, :], src, ACT.Silu if two else ACT.Relu, bias=bias).then_inc(S["act_done"], 1)

                @block.tensor
                def _(pe):
                    pe.wait_ge(S["xn_ready"], 1)
                    for t in range(TT):
                        ins = pe.transpose(misc[:, t * P:(t + 1) * P], xn[:, t, :], ident[:, :])
                    ins.then_inc(S["xT_done"], 1)
                    if kind == "clip":
                        pe.wait_ge(S["xn_ready"], 2)
                        for t in range(TT):
                            ins = pe.transpose(GB[:, t * P:(t + 1) * P], xm[:, t, :], ident[:, :])
                        ins.then_inc(S["xT_done"], 1)
                        pe.wait_ge(S["xc_ready"], 1)
                    pe.wait_ge(S["xT_ready"], 1)
                    for t in range(TT):
                        o = misc[:, t * E:(t + 1) * E]
                        if kind == "silu":
                            pe.matmul(o, ones[:, :], csq[:, :], start=(t == 0), stop=False, skip_group_check=True)
                        ins = pe.matmul(o, xT[:, t * P:(t + 1) * P], gw[:, :], start=(t == 0 and kind != "silu"), stop=True, skip_group_check=True)
                    ins.then_inc(S["logits_done"], 1)
                    pe.wait_ge(S["gates_ready"], 1)
                    for t in range(TT):
                        ins = pe.transpose(misc[0:E, t * P:(t + 1) * P], gates[:, t, :], ident[:, :])
                    ins.then_inc(S["gT_done"], 1)
                    pe.wait_ge(S["gT_ready"], 1)

                    def spread(e):
                        if e:
                            pe.wait_ge(S["gb_ready"], e)
                        pe.matmul(GB[:, :], onehot[:, e, :], gT[:, :], start=True, stop=True).then_inc(S["gb_done"], 1)

                    def up(s):
                        e, f = divmod(s, FT)
                        if kind == "clip" and f == 0:
                            pe.wait_ge(S["e_ready"], e + 1)
                        if s >= 2:
                            if kind == "relu":
                                pe.wait_ge(S["act_done"], s - 1)
                            else:
                                pe.wait_ge(S["prod_done"], s - 1)
                        x = eT[e % 2]
                        if two:
                            pe.matmul(upg[s % 2][0:FP, :], Wg[:, e, f * FP:(f + 1) * FP], x[:, :], start=True, stop=True)
                        pe.matmul(up1[s % 2][0:FP, :], W1[:, e, f * FP:(f + 1) * FP], x[:, :], start=True, stop=True).then_inc(S["up_done"], 1)

                    def down(s):
                        e, f = divmod(s, FT)
                        pe.wait_ge(S["gated"], s + 1)
                        if kind == "clip":
                            if f == 0 and e >= 2:
                                pe.wait_ge(S["y_taken"], e - 1)
                            pe.matmul(Y[e % 2][:, :], W2[:, e, f, :], Hg[s % 3][:, :], start=(f == 0), stop=(f == FT - 1)).then_inc(S["down_done"], 1)
                        else:
                            pe.matmul(Y[0][:, :], W2[:, e, f, :], Hg[s % 3][:, :], start=False, stop=(s == STEPS - 1)).then_inc(S["down_done"], 1)

                    if kind != "clip":
                        pe.matmul(Y[0][:, :], b2[:, :], gT[:, :], start=True, stop=False)
                    spread(0)
                    up(0)
                    up(1)
                    for s in range(STEPS):
                        if s % FT == FT - 2 and s // FT + 1 < E:
                            spread(s // FT + 1)
                        down(s)
                        if s + 2 < STEPS:
                            up(s + 2)
                    pe.wait_ge(S["yT_ready"], 1)
                    for t in range(TT):
                        ins = pe.transpose(misc[:, t * P:(t + 1) * P], yT[:, t * P:(t + 1) * P], ident[:, :])
                    ins.then_inc(S["out_done"], 1)

                @block.vector
                def _(dve):
                    chain = Chain(dve, S["chain_v"])

                    def normalise(src, dst):
                        for t in range(TT):
                            ins = dve.bn_stats(stats[:, t, :], src[:, t, :])
                        chain(ins)
                        for t in range(TT):
                            ins = dve.bn_aggr(mv[:, t, :], stats[:, t, :])
                        chain(ins)
                        inverse_root(dve, chain, rstd[:, :, :], mv[:, :, 1:2], var, root)
                        for t in range(TT):
                            ins = dve.tensor_scalar(dst[:, t, :], src[:, t, :], mv[:, t, 0:1], rstd[:, t, :], ALU.subtract, ALU.mult)
                        return ins

                    dve.wait_ge(S["x_in"], 32 if kind == "relu" else 16)
                    ins = normalise(r_sb if kind == "relu" else x_sb, xn)
                    if kind == "clip":
                        chain(ins)
                        chain(normalise(xn, xm))
                        for t in range(TT):
                            ins = dve.tensor_tensor(xn[:, t, :], xm[:, t, :], lng[:, :], ALU.mult)
                        chain(ins)
                        for t in range(TT):
                            ins = dve.tensor_tensor(xn[:, t, :], xn[:, t, :], lnb[:, :], ALU.add)
                    ins.then_inc(S["xn_ready"], 1)
                    if kind == "clip":
                        dve.wait_ge(S["xn_ready"], 1)
                        normalise(xn, xm).then_inc(S["xn_ready"], 1)
                    dve.wait_ge(S["xT_done"], 1)
                    if kind == "relu":
                        dve.tensor_scalar(xT[:, :], misc[:, :], lng[:, :], lnb[:, :], ALU.mult, ALU.add).then_inc(S["xT_ready"], 1)
                    else:
                        dve.tensor_copy(xT[:, :], misc[:, :]).then_inc(S["xT_ready"], 1)
                    if kind == "clip":
                        dve.wait_ge(S["xT_done"], 2)
                        dve.tensor_copy(cT[:, :], GB[:, :]).then_inc(S["xc_ready"], 1)
                        dve.wait_ge(S["xc_ready"], 1)
                    if kind == "silu":
                        chain(dve.tensor_tensor(sq[:, :, :], xn[:, :, :], xn[:, :, :], ALU.mult))
                        chain(dve.tensor_reduce(nrm[:, :, :], sq[:, :, :], AX.X, ALU.add))
                    dve.wait_ge(S["logits_done"], 1)
                    raw = misc[:, 0:TT * E].rearrange("p (t e) -> p t e", e=E)
                    if kind == "relu":
                        chain(dve.tensor_tensor(L[:, :, :], raw, gb[:, :].unsqueeze(1).broadcast_to([P, TT, E]), ALU.add))
                    elif kind == "clip":
                        chain(dve.tensor_copy(L[:, :, :], raw))
                    else:
                        chain(dve.tensor_tensor(d2[:, :, :], raw, nrm[:, :, :].broadcast_to([P, TT, E]), ALU.add))
                        chain(dve.tensor_scalar(d2[:, :, :], d2[:, :, :], 1e-12, None, ALU.max))
                        inverse_root(dve, chain, L[:, :, :], d2[:, :, :], rank, t8, eps=0.0)
                        chain(dve.tensor_tensor(L[:, :, :], L[:, :, :], d2[:, :, :], ALU.mult))
                    top_k(dve, chain, L[:, :, :], 2, tri[:, :, :], greater[:, :, :, :], equal[:, :, :, :], rank[:, :, :], chosen[:, :, :])
                    chain(dve.tensor_reduce(top[:, :, :], L[:, :, :], AX.X, ALU.max))
                    dve.tensor_tensor(L[:, :, :], L[:, :, :], top[:, :, :].broadcast_to([P, TT, E]), ALU.subtract).then_inc(S["shifted"], 1)
                    dve.wait_ge(S["gate_exp"], 1)
                    chain(dve.tensor_tensor(t8[:, :, :], t8[:, :, :], chosen[:, :, :], ALU.mult))
                    chain(dve.tensor_reduce(total[:, :, :], t8[:, :, :], AX.X, ALU.add))
                    chain(dve.reciprocal(total[:, :, :], total[:, :, :]))
                    dve.tensor_tensor(gates[:, :, :], t8[:, :, :], total[:, :, :].broadcast_to([P, TT, E]), ALU.mult).then_inc(S["gates_ready"], 1)
                    dve.wait_ge(S["gT_done"], 1)
                    dve.tensor_copy(gT[:, :], misc[0:E, :]).then_inc(S["gT_ready"], 1)

                    def take_gate(e):
                        dve.wait_ge(S["gb_done"], e + 1)
                        if kind == "silu" and e >= 2:
                            dve.wait_ge(S["gated"], (e - 1) * FT)
                        dve.tensor_copy(gB[e % 2][:, :], GB[:, :]).then_inc(S["gb_ready"], 1)

                    def expert_input(e):
                        if e >= 2:
                            dve.wait_ge(S["up_done"], (e - 1) * FT)
                        dve.tensor_scalar(eT[e % 2][:, :], cT[:, :], eg[:, e:e + 1], eb[:, e:e + 1], ALU.mult, ALU.add).then_inc(S["e_ready"], 1)

                    def pre(s):
                        dve.wait_ge(S["up_done"], s + 1)
                        if s >= 3:
                            dve.wait_ge(S["low_done"], s - 2)
                        dve.tensor_scalar(C[s % 3][:, :], upg[s % 2][:, :], bg[:, s:s + 1], 20.0, ALU.add, ALU.min).then_inc(S["pre_done"], 1)

                    if kind == "clip":
                        expert_input(0)
                        dve.memset(yT[:, :], 0.0).then_inc(S["acc_step"], 1)
                        pre(0)
                    for s in range(STEPS):
                        e, f = divmod(s, FT)
                        if f == 0:
                            take_gate(e)
                            if kind == "clip" and e + 1 < E:
                                expert_input(e + 1)
                        if kind == "relu":
                            if f == 0:
                                dve.wait_ge(S["gb_ready"], e + 1)
                            dve.wait_ge(S["act_done"], s + 1)
                            if s >= 3:
                                dve.wait_ge(S["down_done"], s - 2)
                            dve.tensor_tensor(Hg[s % 3][:, :], A[s % 3][:, :], gB[e % 2][:, :], ALU.mult).then_inc(S["gated"], 1)
                            continue
                        if kind == "clip" and s + 1 < STEPS:
                            pre(s + 1)
                        dve.wait_ge(S["act_done"], s + 1)
                        if s >= 3:
                            dve.wait_ge(S["gated"], s - 2)
                        dve.scalar_tensor_tensor(T[s % 3][:, :], up1[s % 2][0:FP, :], b1[:, s:s + 1], A[s % 3][:, :], ALU.add, ALU.mult
                                                 ).then_inc(S["prod_done"], 1)
                        if kind == "clip" and (f == 1 and e or s == STEPS - 1):
                            for k in ([e - 1] if s < STEPS - 1 else [e]):
                                dve.wait_ge(S["down_done"], (k + 1) * FT)
                                dve.tensor_scalar(yo[:, :], Y[k % 2][:, :], bo[:, k:k + 1], 1e4, ALU.add, ALU.min).then_inc(S["y_taken"], 1)
                                dve.wait_ge(S["y_taken"], k + 1)
                                dve.wait_ge(S["gb_ready"], k + 1)
                                chain(dve.scalar_tensor_tensor(yg[:, :], yo[:, :], -1e4, gB[k % 2][:, :], ALU.max, ALU.mult))
                                ins = dve.tensor_tensor(yT[:, :], yT[:, :], yg[:, :], ALU.add)
                                if k == E - 1:
                                    ins.then_inc(S["yT_ready"], 1)
                                else:
                                    chain(ins)
                    if kind != "clip":
                        dve.wait_ge(S["down_done"], STEPS)
                        dve.tensor_copy(yT[:, :], Y[0][:, :]).then_inc(S["yT_ready"], 1)
                    dve.wait_ge(S["out_done"], 1)
                    ins = dve.tensor_tensor(out[:, :, :], misc[:, :].rearrange("p (t c) -> p t c", t=TT), x_sb[:, :, :], ALU.add)
                    if kind == "relu":
                        chain(ins)
                        ins = dve.tensor_tensor(out[:, :, :], out[:, :, :], r_sb[:, :, :], ALU.add)
                    ins.then_inc(S["out_ready"], 1)
            ph.barrier()


def switch_phase(nc, tag, x_in, x_out, w, consts):
    H, E, K, DH = 8, 5, 3, 64
    HD_ALL = H * DH
    ZT_TILES = ceil(E * DH, P)
    USES = [(j, e, t) for j in range(3) for e in range(E) for t in range(QT)]

    with ExitStack() as ctx:
        ph = Phase(nc, ctx, tag)
        sb, ps, sem = ph.sb, ph.ps, ph.sem
        ident = sb("ident", [P, P])
        tri = sb("tri", [P, E, E])
        W = sb("W", [P, 3, E, HD_ALL])
        Wr = sb("Wr", [P, 2, H * E])
        Wo = sb("Wo", [P, ZT_TILES, DIM])
        x_sb = sb("x_sb", [P, QT, DIM])
        stats = sb("stats", [P, QT, 6])
        mv = sb("mv", [P, QT, 2])
        rstd = sb("rstd", [P, QT, 1])
        var = sb("var", [P, QT, 1])
        root = sb("root", [P, QT, 1])
        xn = sb("xn", [P, QT, DIM])
        xT = sb("xT", [P, SEQ])
        G = QT * 2 * H
        sig = sb("sig", [P, G, E])
        greater = sb("greater", [P, G, E, E])
        equal = sb("equal", [P, G, E, E])
        rank = sb("rank", [P, G, E])
        chosen = sb("chosen", [P, G, E])
        gate = sb("gate", [P, G, E])
        prod = [sb(f"prod{i}", [P, HD_ALL]) for i in range(3)]
        acc = sb("acc", [P, 3, QT, HD_ALL])
        qT = sb("qT", [P, H // 2, SEQ])
        kT = sb("kT", [P, H // 2, SEQ])
        mx = sb("mx", [P, H, QT])
        sums = sb("sums", [P, QT, H])
        pr = [sb(f"pr{i}", [P, QT, SEQ]) for i in range(3)]
        pT = [sb(f"pT{i}", [P, QT, SEQ]) for i in range(3)]
        pick = sb("pick", [P, QT, H, E])
        zp = [sb(f"zp{i}", [P, H, DH]) for i in range(2)]
        Z = sb("Z", [P, QT, E, DH])
        ZT = sb("ZT", [P, QT, ZT_TILES, P])
        out = sb("out", [P, QT, DIM])
        bank = [ps(f"bank{i}", [P, 512]) for i in range(8)]

        names = ("setup x_in chain_v xn_ready xT_done xT_ready logits_done sig_exp neg_done gate_ready proj_done prod_done acc_done "
                 "qk_done qk_ready s_done max_ready exp_done pt_done pt_ready pv_done zp_done z_ready zt_done zt_ready out_done "
                 "out_ready out_sent").split()
        S = {n: sem(n) for n in names}

        with nc.Block() as block:
            @block.sync
            def _(sp):
                loads = [(ident[:, :], consts["ident"]), (tri[:, :, :], consts["tri5"]), (W[:, :, :, :], w["W"]), (Wr[:, :, :], w["Wr"]),
                         (Wo[:, 0:2, :], w["Wo"][0:2 * P].rearrange("(t p) n -> p t n", p=P)), (Wo[0:DH, 2, :], w["Wo"][2 * P:])]
                for dst, src in loads:
                    sp.dma_start(dst, src).then_inc(S["setup"], 16)
                sp.wait_ge(S["setup"], 16 * len(loads))
        ph.barrier()

        with nc.Fori(0, LOOPS) as b:
            with nc.Block() as block:
                @block.sync
                def _(sp):
                    sp.dma_start(x_sb[:, :, :], x_in[b].rearrange("(t p) c -> p t c", p=P)).then_inc(S["x_in"], 16)
                    sp.wait_ge(S["out_ready"], 1)
                    sp.dma_start(x_out[b].rearrange("(t p) c -> p t c", p=P), out[:, :, :]).then_inc(S["out_sent"], 16)
                    sp.wait_ge(S["out_sent"], 16)

                @block.gpsimd
                def _(pool):
                    for u, (j, e, t) in enumerate(USES):
                        if e == 0:
                            continue
                        pool.wait_ge(S["prod_done"], u + 1)
                        n = sum(v[1] > 0 for v in USES[:u])
                        if e > 1:
                            pool.wait_ge(S["acc_done"], n - QT + 1)
                        pool.tensor_tensor(acc[:, j, t, :], acc[:, j, t, :], prod[u % 3][:, :], ALU.add).then_inc(S["acc_done"], 1)

                def turn_out(act, h):
                    act.wait_ge(S["pt_done"], h + 1)
                    if h >= 3:
                        act.wait_ge(S["pv_done"], h - 2)
                    act.copy(pT[h % 3][:, :, :], bank[3 + h % 2][:, :].rearrange("p (t q) -> p t q", t=QT)).then_inc(S["pt_ready"], 1)

                @block.scalar
                def _(act):
                    act.wait_ge(S["logits_done"], 1)
                    act.activation(sig[:, :, :], bank[7][:, 0:G * E].rearrange("p (g e) -> p g e", e=E), ACT.Exp, scale=-1.0).then_inc(S["sig_exp"], 1)
                    for h in range(H):
                        act.wait_ge(S["max_ready"], h + 1)
                        if h >= 3:
                            act.wait_ge(S["pt_done"], h - 2)
                        for qt in range(QT):
                            ins = act.activation(pr[h % 3][:, qt, :], bank[h % 3][:, qt * SEQ:(qt + 1) * SEQ], ACT.Exp,
                                                 bias=mx[:, h, qt:qt + 1], accum_out=sums[:, qt, h:h + 1])
                        ins.then_inc(S["exp_done"], 1)
                        if h:
                            turn_out(act, h - 1)
                    turn_out(act, H - 1)

                @block.tensor
                def _(pe):
                    pe.wait_ge(S["xn_ready"], 1)
                    for t in range(QT):
                        ins = pe.transpose(bank[6][:, t * P:(t + 1) * P], xn[:, t, :], ident[:, :])
                    ins.then_inc(S["xT_done"], 1)
                    pe.wait_ge(S["xT_ready"], 1)
                    for t in range(QT):
                        ins = pe.matmul(bank[7][:, t * 2 * H * E:(t + 1) * 2 * H * E], xT[:, t * P:(t + 1) * P],
                                        Wr[:, :, :].rearrange("p r n -> p (r n)"), start=(t == 0), stop=True, skip_group_check=True)
                    ins.then_inc(S["logits_done"], 1)
                    for u, (j, e, t) in enumerate(USES):
                        if u >= 4:
                            pe.wait_ge(S["prod_done"], u - 3)
                        pe.matmul(bank[u % 4][:, :], xT[:, t * P:(t + 1) * P], W[:, j, e, :], start=True, stop=True).then_inc(S["proj_done"], 1)
                        if j == 2 and e == 1 and t == 0:
                            pe.wait_ge(S["acc_done"], 2 * QT * (E - 1))
                            for jj in range(2):
                                for c in range(H // 2):
                                    for tt in range(QT):
                                        ins = pe.transpose(bank[4 + 2 * jj + c // 2][:, c % 2 * SEQ + tt * P:c % 2 * SEQ + (tt + 1) * P],
                                                           acc[:, jj, tt, c * P:(c + 1) * P], ident[:, :])
                                ins.then_inc(S["qk_done"], 1)

                    def scores(h):
                        if h >= 3:
                            pe.wait_ge(S["exp_done"], h - 2)
                        at = DH * (h % 2)
                        for qt in range(QT):
                            ins = pe.matmul(bank[h % 3][:, qt * SEQ:(qt + 1) * SEQ], qT[at:at + DH, h // 2, qt * P:(qt + 1) * P],
                                            kT[at:at + DH, h // 2, :], start=(qt == 0), stop=True, skip_group_check=True)
                        ins.then_inc(S["s_done"], 1)

                    def turn(h):
                        pe.wait_ge(S["exp_done"], h + 1)
                        if h >= 2:
                            pe.wait_ge(S["pt_ready"], h - 1)
                        for kt in range(QT):
                            for qt in range(QT):
                                ins = pe.transpose(bank[3 + h % 2][:, kt * SEQ + qt * P:kt * SEQ + (qt + 1) * P],
                                                   pr[h % 3][:, qt, kt * P:(kt + 1) * P], ident[:, :])
                        ins.then_inc(S["pt_done"], 1)

                    def weigh(h):
                        pe.wait_ge(S["pt_ready"], h + 1)
                        for qt in range(QT):
                            for kt in range(QT):
                                ins = pe.matmul(bank[5 + qt][:, h * DH:(h + 1) * DH], pT[h % 3][:, kt, qt * P:(qt + 1) * P],
                                                acc[:, 2, kt, h * DH:(h + 1) * DH], start=(h == 0 and kt == 0), stop=(kt == QT - 1),
                                                skip_group_check=True)
                        ins.then_inc(S["pv_done"], 1)

                    pe.wait_ge(S["qk_ready"], 4)
                    pe.wait_ge(S["prod_done"], len(USES))
                    pe.wait_ge(S["acc_done"], 3 * QT * (E - 1))
                    scores(0)
                    scores(1)
                    for h in range(H):
                        turn(h)
                        if h + 2 < H:
                            scores(h + 2)
                        if h:
                            weigh(h - 1)
                    weigh(H - 1)
                    for qt in range(QT):
                        pe.wait_ge(S["z_ready"], E * (qt + 1))
                        for c in range(ZT_TILES):
                            n = min(P, E * DH - c * P)
                            ins = pe.transpose(bank[qt][0:n, c * P:(c + 1) * P],
                                               Z[:, qt, :, :].rearrange("p e d -> p (e d)")[:, c * P:c * P + n], ident[:, :])
                        ins.then_inc(S["zt_done"], 1)
                    for qt in range(QT):
                        pe.wait_ge(S["zt_ready"], 2 * (qt + 1))
                        for c in range(ZT_TILES):
                            n = min(P, E * DH - c * P)
                            ins = pe.matmul(bank[7][:, qt * P:(qt + 1) * P], ZT[0:n, qt, c, :], Wo[0:n, c, :],
                                            start=(qt == 0 and c == 0), stop=(c == ZT_TILES - 1), skip_group_check=True)
                    ins.then_inc(S["out_done"], 1)

                @block.vector
                def _(dve):
                    chain = Chain(dve, S["chain_v"])
                    dve.wait_ge(S["x_in"], 16)
                    for t in range(QT):
                        ins = dve.bn_stats(stats[:, t, :], x_sb[:, t, :])
                    chain(ins)
                    for t in range(QT):
                        ins = dve.bn_aggr(mv[:, t, :], stats[:, t, :])
                    chain(ins)
                    inverse_root(dve, chain, rstd[:, :, :], mv[:, :, 1:2], var, root)
                    for t in range(QT):
                        ins = dve.tensor_scalar(xn[:, t, :], x_sb[:, t, :], mv[:, t, 0:1], rstd[:, t, :], ALU.subtract, ALU.mult)
                    ins.then_inc(S["xn_ready"], 1)
                    dve.wait_ge(S["xT_done"], 1)
                    dve.tensor_copy(xT[:, :], bank[6][:, 0:SEQ]).then_inc(S["xT_ready"], 1)
                    dve.wait_ge(S["sig_exp"], 1)
                    chain(dve.tensor_scalar(sig[:, :, :], sig[:, :, :], 1.0, None, ALU.add))
                    chain(dve.reciprocal(sig[:, :, :], sig[:, :, :]))
                    top_k(dve, chain, sig[:, :, :], K, tri[:, :, :], greater[:, :, :, :], equal[:, :, :, :], rank[:, :, :], chosen[:, :, :])
                    chain(dve.tensor_tensor(gate[:, :, :], sig[:, :, :], chosen[:, :, :], ALU.mult))
                    gv = gate[:, :, :].rearrange("p (t r h) e -> p t r h e", t=QT, r=2)
                    cv = chosen[:, :, :].rearrange("p (t r h) e -> p t r h e", t=QT, r=2)
                    for u, (j, e, t) in enumerate(USES):
                        dve.wait_ge(S["proj_done"], u + 1)
                        g = gv[:, t, 1 if j == 0 else 0, :, e:e + 1].broadcast_to([P, H, DH])
                        src = bank[u % 4][:, :].rearrange("p (h d) -> p h d", d=DH)
                        if e == 0:
                            dst = acc[:, j, t, :]
                        else:
                            dst = prod[u % 3][:, :]
                            before = [i for i in range(u) if i % 3 == u % 3 and USES[i][1]]
                            if before:
                                dve.wait_ge(S["acc_done"], sum(v[1] > 0 for v in USES[:before[-1] + 1]))
                        dve.tensor_tensor(dst.rearrange("p (h d) -> p h d", d=DH), src, g, ALU.mult).then_inc(S["prod_done"], 1)
                        if j == 2 and e == 2 and t == 0:
                            for jj in range(2):
                                dve.wait_ge(S["qk_done"], jj + 1)
                                for c in range(2):
                                    dst, src = (qT, kT)[jj][:, 2 * c:2 * c + 2, :], bank[4 + 2 * jj + c][:, :].rearrange("p (c t) -> p c t", c=2)
                                    dve.tensor_scalar(dst, src, DH ** -0.5 if jj == 0 else 1.0, None, ALU.mult).then_inc(S["qk_ready"], 1)
                    for h in range(H):
                        dve.wait_ge(S["s_done"], h + 1)
                        chain(dve.tensor_reduce(mx[:, h, :], bank[h % 3][:, :].rearrange("p (t k) -> p t k", t=QT), AX.X, ALU.max))
                        dve.tensor_scalar(mx[:, h, :], mx[:, h, :], -1.0, None, ALU.mult).then_inc(S["max_ready"], 1)
                    dve.wait_ge(S["exp_done"], H)
                    chain(dve.reciprocal(sums[:, :, :], sums[:, :, :]))
                    for t in range(QT):
                        ins = dve.tensor_tensor(pick[:, t, :, :], cv[:, t, 1, :, :], sums[:, t, :].unsqueeze(2).broadcast_to([P, H, E]), ALU.mult)
                    chain(ins)
                    dve.wait_ge(S["pv_done"], H)
                    for k in range(QT * E):
                        qt, e = divmod(k, E)
                        src = bank[5 + qt][:, :].rearrange("p (h d) -> p h d", d=DH)
                        if k >= 2:
                            dve.wait_ge(S["z_ready"], k - 1)
                        dve.tensor_tensor(zp[k % 2][:, :, :], src, pick[:, qt, :, e:e + 1].broadcast_to([P, H, DH]), ALU.mult).then_inc(S["zp_done"], 1)
                        dve.wait_ge(S["zp_done"], k + 1)
                        dve.tensor_reduce(Z[:, qt, e, :], zp[k % 2][:, :, :].rearrange("p h d -> p d h"), AX.X, ALU.add).then_inc(S["z_ready"], 1)
                    for qt in range(QT):
                        dve.wait_ge(S["zt_done"], qt + 1)
                        dve.tensor_copy(ZT[:, qt, 0:2, :], bank[qt][:, 0:2 * P].rearrange("p (c q) -> p c q", c=2)).then_inc(S["zt_ready"], 1)
                        dve.tensor_copy(ZT[0:DH, qt, 2, :], bank[qt][0:DH, 2 * P:3 * P]).then_inc(S["zt_ready"], 1)
                    dve.wait_ge(S["out_done"], 1)
                    dve.tensor_tensor(out[:, :, :], bank[7][:, 0:SEQ].rearrange("p (t c) -> p t c", t=QT), x_sb[:, :, :], ALU.add
                                      ).then_inc(S["out_ready"], 1)
            ph.barrier()


def lay_out(inputs):
    import numpy as np

    a = {k: np.asarray(v) for k, v in inputs.items()}
    head = np.array([[[2 * s + par for s in range(PAIRS)] for _ in range(HD)] for par in range(2)]).reshape(-1)
    d = np.array([[[k] * PAIRS for k in range(HD)] for _ in range(2)]).reshape(-1)
    packed = head * HD + d
    o = {"x": a["x"]}
    o["ctxT"] = np.ascontiguousarray(a["ctx_1024"].transpose(0, 2, 1))
    o["ctx_rows"] = a["ctx_1024"].reshape(BATCH * CTX, DIM)
    for n, m in (("mask8", a["mask_Bx1xSxS2_ik1"]), ("mask1", a["mask_1x1xSxS2_ik1"])):
        o[n] = m
        o[n + "T"] = np.ascontiguousarray(m[:, 0].transpose(0, 2, 1))
    o["a0_wq"], o["a0_wk"] = a["L0_xattn_wq"].T[:, packed], a["L0_xattn_wk"].T[:, packed]
    o["a0_wv"], o["a0_wo"] = a["L0_xattn_wv"].T, a["L0_xattn_wo"].T
    o["a0_bq"], o["a0_bk"] = a["L0_xattn_bq"][packed], a["L0_xattn_bk"][packed]
    o["a0_bv"], o["a0_bo"] = a["L0_xattn_bv"], a["L0_xattn_bo"]
    wqkv, bqkv = a["L0_ffn_w_qkv"], a["L0_ffn_b_qkv"]
    o["s0_wq"], o["s0_wk"], o["s0_wv"] = wqkv[:, 0:128][:, packed], wqkv[:, 128:256][:, packed], wqkv[:, 256:384]
    o["s0_bq"], o["s0_bk"], o["s0_bv"] = bqkv[0:128][packed], bqkv[128:256][packed], bqkv[256:384]
    o["s0_wo"], o["s0_bo"] = a["L0_ffn_w_o"], a["L0_ffn_b_o"]
    o["s0_lng"], o["s0_lnb"] = a["L0_ffn_ln1_g"], a["L0_ffn_ln1_b"]

    def diagonal(m):
        out = np.zeros((DIM, DIM), m.dtype)
        for h in range(HEADS):
            out[h * HD:(h + 1) * HD, h * HD:(h + 1) * HD] = m.T
        return out
    o["a1_wq"], o["a1_wk"] = diagonal(a["L1_xattn_Wq"])[:, packed], diagonal(a["L1_xattn_Wk"])[:, packed]
    o["a1_wv"], o["a1_wo"], o["a1_bo"] = diagonal(a["L1_xattn_Wv"]), a["L1_xattn_Wo"].T, a["L1_xattn_bo"]
    o["a2_wq"], o["a2_wqn"] = a["L2_xattn_Wq"].T[:, packed], a["L2_xattn_Wq"].T
    o["a2_wk"] = a["L2_xattn_Wkv"].T[:, d]
    o["a2_wv"] = a["L2_xattn_Wkv"].T[:, np.tile(np.arange(HD), HEADS) + HD]
    o["a2_wo"] = a["L2_xattn_Wc"].T
    for k in "qk":
        o["a3_w" + k], o["a3_b" + k] = a["L3_xattn_W" + k][:, packed], a["L3_xattn_b" + k][packed]
    o["a3_wv"], o["a3_bv"], o["a3_wo"], o["a3_bo"] = (a["L3_xattn_" + k] for k in ("Wv", "bv", "Wo", "bo"))

    def experts(tag, up, down, biases, tiles):
        for n, m in up.items():
            o[f"{tag}_{n}"] = m.transpose(1, 0, 2)
        E, F, D = down.shape
        o[f"{tag}_W2"] = down.reshape(E, tiles, F // tiles, D).transpose(2, 0, 1, 3)
        for n, m in biases.items():
            o[f"{tag}_{n}"] = m.reshape(E * tiles, F // tiles).T
    experts("m0", {"W1": a["L0_ffn_W1"]}, a["L0_ffn_W2"], {"b1": a["L0_ffn_b1"]}, 4)
    o["m0_b2"], o["m0_gw"], o["m0_gb"] = a["L0_ffn_b2"], a["L0_ffn_gate_w"], a["L0_ffn_gate_b"]
    o["m0_lng"], o["m0_lnb"] = a["L0_ffn_ln2_g"], a["L0_ffn_ln2_b"]
    experts("m1", {"W1": a["L1_ffn_W1"], "Wg": a["L1_ffn_Wg"]}, a["L1_ffn_W2"], {"b1": a["L1_ffn_b1"], "bg": a["L1_ffn_bg"]}, 3)
    o["m1_b2"], o["m1_gw"] = a["L1_ffn_b2"], a["L1_ffn_centroid"].T
    experts("m2", {"W1": a["L2_ffn_W1"], "Wg": a["L2_ffn_W2"]}, a["L2_ffn_Wo"], {"b1": a["L2_ffn_b1"], "bg": a["L2_ffn_b2"]}, 4)
    o["m2_gw"], o["m2_lng"], o["m2_lnb"] = a["L2_ffn_router_w"], a["L2_ffn_ln_g"], a["L2_ffn_ln_b"]
    o["m2_bo"], o["m2_eg"], o["m2_eb"] = a["L2_ffn_bo"].T, a["L2_ffn_eg"].T, a["L2_ffn_eb"].T
    wq = a["L3_ffn_Wq"].reshape(DIM, 1, 8, 5, 64)
    wkv = a["L3_ffn_Wkv"].reshape(DIM, 2, 8, 5, 64)
    o["m3_W"] = np.concatenate([wq, wkv], axis=1).transpose(0, 1, 3, 2, 4).reshape(DIM, 3, 5, 512)
    o["m3_Wr"] = np.stack([a["L3_ffn_Ws"], a["L3_ffn_Wd"]], axis=1)
    o["m3_Wo"] = a["L3_ffn_Wo"].reshape(64, 5, DIM).transpose(1, 0, 2).reshape(320, DIM)
    for e in (5, 8):
        o[f"tri{e}"] = np.broadcast_to(np.triu(np.ones((e, e), np.float32), 1), (P, e, e))
    o["onehot"] = np.broadcast_to(np.eye(8, dtype=np.float32)[:, :, None], (8, 8, P))
    o["ident"] = np.eye(P, dtype=np.float32)
    pick = np.zeros((P, 2, HD + 1), np.float32)
    for tile in range(2):
        for par in range(2):
            for k in range(HD + 1):
                pick[32 * (2 * tile + par) + k, par, k] = 1.0
    o["pick"] = pick.reshape(P, -1)
    sel = np.zeros((P, P), np.float32)
    for par in range(2):
        sel[HALF * par + SHIFT:HALF * par + SHIFT + 2] = 1.0
    o["shiftsel"] = sel
    o["rowbase"] = np.repeat(np.arange(BATCH, dtype=np.float32)[:, None] * CTX, P, axis=1)
    return {k: np.ascontiguousarray(v) for k, v in o.items()}


def build(nc, t, phases=("a0", "s0", "m0", "a1", "m1", "a2", "m2", "a3", "m3")):
    def weights(tag, *names):
        return {n: t[f"{tag}_{n}"] for n in names}

    consts = {k: t[k] for k in ("ident", "pick", "shiftsel", "rowbase", "tri5", "tri8", "onehot")}
    ROOT8 = float(HD) ** -0.5
    cur = before = t["x"]
    if phases[0] == "m0":
        cur = t["y0"]

    def nxt(tag):
        if tag == phases[-1]:
            return t["out"]
        return nc.dram_tensor(f"x_after_{tag}", [BATCH, SEQ, DIM], F32).ap()
    for tag in phases:
        dst = nxt(tag)
        if tag == "a0":
            attention_phase(nc, tag, cur, dst, weights(tag, "wq", "wk", "wv", "wo", "bq", "bk", "bv", "bo"), consts, ctxT=t["ctxT"],
                            mask=t["mask8"], maskT=t["mask8T"], scale=ROOT8, clip=100.0)
        elif tag == "s0":
            attention_phase(nc, tag, cur, dst, weights(tag, "wq", "wk", "wv", "wo", "bq", "bk", "bv", "bo", "lng", "lnb"), consts,
                            scale=ROOT8, self_ln=True)
        elif tag == "a1":
            attention_phase(nc, tag, cur, dst, weights(tag, "wq", "wk", "wv", "wo", "bo"), consts, ctxT=t["ctxT"],
                            mask=t["mask1"], maskT=t["mask1T"], scale=float(DIM) ** -0.5)
        elif tag == "a2":
            attention_phase(nc, tag, cur, dst, weights(tag, "wq", "wqn", "wk", "wv", "wo"), consts, ctxT=t["ctxT"],
                            ctx_rows=t["ctx_rows"], scale=ROOT8)
        elif tag == "a3":
            attention_phase(nc, tag, cur, dst, weights(tag, "wq", "wk", "wv", "wo", "bq", "bk", "bv", "bo"), consts, ctxT=t["ctxT"],
                            scale=ROOT8)
        elif tag == "m0":
            experts_phase(nc, tag, "relu", before, dst, weights(tag, "W1", "W2", "b1", "b2", "gw", "gb", "lng", "lnb"), consts, extra=cur)
        elif tag == "m1":
            experts_phase(nc, tag, "silu", cur, dst, weights(tag, "W1", "Wg", "W2", "b1", "bg", "b2", "gw"), consts)
        elif tag == "m2":
            experts_phase(nc, tag, "clip", cur, dst, weights(tag, "W1", "Wg", "W2", "b1", "bg", "bo", "eg", "eb", "gw", "lng", "lnb"), consts)
        elif tag == "m3":
            switch_phase(nc, tag, cur, dst, weights(tag, "W", "Wr", "Wo"), consts)
        before, cur = cur, dst


def kernel(**inputs):
    import numpy as _np
    import concourse.bacc as _bacc
    from concourse.bass_utils import run_bass_kernel_spmd as _run

    nc = _bacc.Bacc("TRN2", target_bir_lowering=False, num_devices=1)
    arrays, t = {}, {}
    for name, a in lay_out(inputs).items():
        arrays[f"in_{name}"] = a
        t[name] = nc.dram_tensor(f"in_{name}", a.shape, mybir.dt.from_np(a.dtype), kind="ExternalInput").ap()
    t["out"] = nc.dram_tensor("out_x", [BATCH, SEQ, DIM], F32, kind="ExternalOutput").ap()
    build(nc, t)
    return _run(nc, [arrays], core_ids=[0]).results[0]["out_x"]
```

```python
from contextlib import ExitStack

import concourse.bass as bass
from concourse import mybir

P = 128
F32 = mybir.dt.float32
BF16 = mybir.dt.bfloat16
I32 = mybir.dt.int32
U32 = mybir.dt.uint32
ALU = mybir.AluOpType
ACT = mybir.ActivationFunctionType
AX = mybir.AxisListType

BATCH, SEQ, DIM = 8, 256, 128
LOOPS = BATCH
FIRST_SEMAPHORE = 120
CTX = 1601
HEADS, HD = 16, 8
PAIRS = HEADS // 2
QT = SEQ // P
EPS = 1e-5
MASKED = -1e30
HALF = 64
PARTS = 6 * HD
SHIFT = PARTS


class Phase:

    def __init__(self, nc, ctx, tag):
        self.nc, self.ctx, self.tag, self.sems = nc, ctx, tag, []

    def sb(self, name, shape, dt=F32):
        return self.ctx.enter_context(self.nc.sbuf_tensor(f"{self.tag}_{name}", shape, dt))

    def ps(self, name, shape, dt=F32):
        return self.ctx.enter_context(self.nc.psum_tensor(f"{self.tag}_{name}", shape, dt))

    def sem(self, name):
        num = self.sems[-1].num + 1 if self.sems else FIRST_SEMAPHORE
        s = self.ctx.enter_context(self.nc.semaphore(f"{self.tag}_{name}", num=num))
        self.sems.append(s)
        return s

    def barrier(self):
        self.nc.all_engine_barrier(sems_to_clear=range(self.sems[0].num, self.sems[-1].num + 1))


class Chain:

    def __init__(self, eng, sem):
        self.eng, self.sem, self.n = eng, sem, 0

    def __call__(self, ins):
        self.n += 1
        ins.then_inc(self.sem, 1)
        self.eng.wait_ge(self.sem, self.n)


def ceil(a, b):
    return -(-a // b)


def inverse_root(dve, chain, out, variance, var, tmp, eps=EPS):
    chain(dve.tensor_scalar(var[:], variance, eps, None, ALU.add))
    chain(dve.tensor_scalar(tmp[:].bitcast(I32), var[:].bitcast(I32), 1, None, ALU.arith_shift_right))
    chain(dve.tensor_scalar(out.bitcast(I32), tmp[:].bitcast(I32), -1.0, 1597463007.0, ALU.mult, ALU.add))
    for _ in range(4):
        chain(dve.tensor_tensor(tmp[:], out, out, ALU.mult))
        chain(dve.scalar_tensor_tensor(tmp[:], tmp[:], -0.5, var[:], ALU.mult, ALU.mult))
        chain(dve.scalar_tensor_tensor(out, tmp[:], 1.5, out, ALU.add, ALU.mult))


def attention_phase(nc, tag, x_in, x_out, w, consts, ctxT=None, ctx_rows=None, mask=None, maskT=None,
                    scale=1.0, clip=None, self_ln=None):
    hard = ctx_rows is not None
    NK = CTX if (ctxT is not None and not hard) else SEQ
    KT = ceil(NK, P)
    KP = ceil(KT, 2)
    NC = ceil(NK, 512)
    HC = ceil(CTX, 512)
    VG = ceil(KT, 4)
    AHEAD = 2 if KP > 1 else 3
    N = PAIRS * KP
    ITEMS = 2 * QT * NC
    LAST = KT - 1
    MASK_K = [(0, 6), (6, 12), (12, 13)]
    MASKS = (QT + len(MASK_K)) if mask is not None else 0
    MASK_ONCE = mask is not None and mask.shape[0] == 1

    def keys(kt):
        return min(P, NK - kt * P)

    def chunk(c):
        return min(512, NK - c * 512)

    PREPARE = ["load", "norm", "turn_x", "proj_q"]
    if hard:
        PREPARE += [("hard", t, c) for t in range(QT) for c in range(HC)] + ["gather", "turn_mem"]
    PREPARE += [("proj_k", c) for c in range(NC)] + ["k_high", "k_rest", "k_mid", "k_low"]
    PREPARE += [("proj_v", g) for g in range(VG)]
    masks = [("mask", j) for j in range(MASKS)] if not MASK_ONCE else []
    FINISH = ["divide", "turn_attn", "proj_o"]
    span = (PAIRS - AHEAD) * KP - 1
    plan = [[] for _ in range(N)]
    for k, stage in enumerate(PREPARE):
        plan[min(k * 2, span - 1) if KP > 1 else k * span // len(PREPARE)].append(stage)
    for k, stage in enumerate(masks):
        plan[5 + 6 * k].append(stage)

    def plan_of(n):
        half, k = divmod(n, N)
        out = [(st, half) for st in plan[k]]
        if half and k == min(2, KP):
            out = [(st, 0) for st in FINISH] + out
        return out

    with ExitStack() as ctx:
        ph = Phase(nc, ctx, tag)
        sb, ps, sem = ph.sb, ph.ps, ph.sem
        ident = sb("ident", [P, P])
        identb = sb("identb", [P, P], BF16)
        pick = sb("pick", [P, 2 * (HD + 1)])
        shiftsel_f = sb("shiftsel_f", [P, P]) if clip else None
        shiftsel = sb("shiftsel", [P, P], BF16) if clip else None
        wsb = {k: sb("w_" + k, list(w[k].shape)) for k in ("wq", "wk", "wv", "wo", "wqn") if k in w}
        cols = {k: sb("c_" + k, [P, 1]) for k in ("bq", "bk", "lng", "lnb") if k in w}
        rows = {k: sb("r_" + k, [P, P]) for k in ("bv", "bo") if k in w}
        x_p = sb("x_p", [P, QT, DIM])
        stats = sb("stats", [P, QT, 6])
        mv = sb("mv", [P, QT, 2])
        rstd = sb("rstd", [P, QT, 1])
        var = sb("var", [P, QT, 1])
        root = sb("root", [P, QT, 1])
        xn = sb("xn", [P, QT, DIM])
        xn2 = sb("xn2", [P, QT, DIM]) if self_ln else None
        xT = sb("xT", [P, SEQ])
        srcT = sb("srcT", [P, CTX]) if ctxT is not None else None
        memT = sb("memT", [P, SEQ]) if hard else None
        kf = sb("kf", [P, NK])
        kr = sb("kr", [P, NK])
        kparts = sb("kparts", [P, 3, NK], BF16)
        qf = sb("qf", [P, SEQ])
        qr = sb("qr", [P, SEQ])
        qparts = sb("qparts", [P, 3, SEQ], BF16)
        if mask is not None:
            stage_i = sb("stage_i", [P, 6 * SEQ + P], I32)
        if hard:
            hs = sb("hs", [P, QT, CTX])
            hmax = sb("hmax", [P, QT, 8])
            hidx = sb("hidx", [P, QT, 8], U32)
            rowbase = sb("rowbase", [P, 1])
            mem = sb("mem", [P, QT, DIM])
            qpT = sb("qpT", [P, SEQ])
        KS = [sb(f"KS{i}", [P, PAIRS, NK], BF16) for i in range(2)]
        QS = [sb(f"QS{i}", [P, PAIRS, 2, SEQ], BF16) for i in range(2)]
        V = [sb(f"V{i}", [P, KT, HEADS, HD + 1]) for i in range(2)]
        nm = 1 if MASK_ONCE else 2
        maskq = [sb(f"maskq{i}", [P, QT, CTX], BF16) for i in range(nm)] * (3 - nm) if mask is not None else None
        maskk = [sb(f"maskk{i}", [P, KT, SEQ], BF16) for i in range(nm)] * (3 - nm) if mask is not None else None
        PT = [sb(f"PT{i}", [P, 2, 512]) for i in range(3)]
        mx = sb("mx", [P, 2 * PAIRS, QT * 2, NC])
        mm = sb("mm", [P, 2 * PAIRS, QT * 2])
        MB = sb("MB", [P, 2 * PAIRS, QT * 2, 2], BF16)
        MT = [sb(f"MT{i}", [4, SEQ], BF16) for i in range(2)]
        junk = [sb(f"junk{i}", [P, 512], BF16) for i in range(2)] if mask is not None else None
        osb = [sb(f"osb{i}", [P, SEQ]) for i in range(2)]
        oc = [sb(f"oc{i}", [P, QT, HEADS, HD + 1]) for i in range(2)]
        rec = sb("rec", [P, QT, HEADS, 1])
        attn = sb("attn", [P, QT, DIM])
        attnT = sb("attnT", [P, SEQ])
        base = [sb(f"base{i}", [P, QT, DIM]) for i in range(2)]
        y = [sb(f"y{i}", [P, QT, DIM]) for i in range(2)]
        ST = [ps(f"ST{i}", [P, 2, 512]) for i in range(2)]
        SQ = [ps(f"SQ{i}", [P, 512]) for i in range(2)]
        O = ps("O", [P, 512])
        misc = ps("misc", [P, 512])
        miscb = misc[:, :].bitcast(BF16)
        base_dram = nc.dram_tensor(f"{tag}_base", [BATCH, SEQ, DIM], F32).ap() if self_ln else x_in

        names = ("consts_in x_in ctx_in setup chain_v xn_ready xn_out xT_done xT_ready pq_done q_read q_split pk_done kf_ready "
                 "k_hi kr_ready k_mid k_lo qs_in ks_in pv_proj v_ready mask_in mask_raw mask_ready sq_done max_done mb_ready "
                 "mt_done mtc_done pair_done st_raw clipped st_done exp_done pv_done o_copied fin_done base_in "
                 "attn_ready at_done at_ready po_done y_ready y_out hs_done hs_copied idx_ready rowbase_in mem_ready memT_done "
                 "memT_ready").split()
        S = {n: sem(n) for n in names}
        mem_in = ctx.enter_context(nc.semaphore(f"{tag}_mem_in")) if hard else None
        m_in = [sem(f"m_in{p}") for p in range(PAIRS)]

        QPROD = (0, 1, 0, 1, 2, 0)
        KPROD = (0, 0, 1, 1, 0, 2)

        def mask_source(b, j):
            if j < QT:
                return mask[b, 0, j * P:(j + 1) * P, :], stage_i[:, 0:CTX], lambda m, k: m[:, j, :]
            a, z = MASK_K[j - QT]
            if keys(z - 1) == P:
                st = stage_i[:, 0:(z - a) * SEQ].rearrange("p (t q) -> p t q", q=SEQ)
                return maskT[b, a * P:z * P].rearrange("(t p) q -> p t q", p=P), st, lambda m, k: k[:, a:z, :]
            n = keys(a)
            return maskT[b, a * P:a * P + n], stage_i[0:n, 0:SEQ], lambda m, k: k[0:n, a, :]

        with nc.Block() as block:
            @block.sync
            def _(sp):
                loads = [(ident, consts["ident"]), (pick, consts["pick"])] + ([(shiftsel_f, consts["shiftsel"])] if clip else [])
                for dst, src in loads:
                    sp.dma_start(dst[:, :], src).then_inc(S["consts_in"], 16)
                for k in wsb:
                    sp.dma_start(wsb[k][:, :], w[k]).then_inc(S["setup"], 16)
                for k in cols:
                    sp.dma_start(cols[k][:, :], w[k].rearrange("(p o) -> p o", o=1)).then_inc(S["setup"], 16)
                for k in rows:
                    sp.dma_start(rows[k][:, :], w[k].rearrange("(o n) -> o n", o=1).broadcast_to([P, P])).then_inc(S["setup"], 16)
                sp.wait_ge(S["setup"], 16 * (len(wsb) + len(cols) + len(rows)))

            @block.gpsimd
            def _(pool):
                for i in range(2):
                    pool.memset(KS[i][:, :, :], 0.0 if clip else 1.0)

            @block.vector
            def _(dve):
                dve.memset(O[:, :], 0.0)
                for i in range(2):
                    dve.memset(V[i][:, :, :, :], 1.0)
                    dve.memset(QS[i][:, :, :, :].rearrange("p a b q -> p (a b q)").bitcast(F32), 0.0)
                dve.wait_ge(S["consts_in"], 48 if clip else 32)
                dve.tensor_copy(identb[:, :], ident[:, :])
                if clip:
                    dve.tensor_copy(shiftsel[:, :], shiftsel_f[:, :])
        ph.barrier()

        def prepare_sp(sp, stage, r, nb, b):
            used = r == 1
            if stage == "load":
                if r:
                    sp.wait_ge(S["xn_ready"], r)
                sp.dma_start(x_p[:, :, :], x_in[b].rearrange("(t p) c -> p t c", p=P)).then_inc(S["x_in"], 16)
                if ctxT is not None:
                    if r:
                        sp.wait_ge(S["pv_proj"], VG * r)
                    sp.dma_start(srcT[:, :], ctxT[b]).then_inc(S["ctx_in"], 16)
                if hard:
                    if r:
                        sp.wait_ge(S["idx_ready"], r)
                    sp.dma_start(rowbase[:, :], consts["rowbase"][b].rearrange("(p o) -> p o", o=1)).then_inc(S["rowbase_in"], 16)
            elif stage == "norm" and self_ln:
                sp.wait_ge(S["xn_ready"], r + 1)
                sp.dma_start(base_dram[b].rearrange("(t p) c -> p t c", p=P), xn[:, :, :]).then_inc(S["xn_out"], 16)
            elif stage == "proj_q":
                sp.wait_ge(S["q_split"], 3 * (r + 1))
                if used:
                    sp.wait_ge(S["pv_done"], N)
                for par in range(2):
                    for k, part in enumerate(QPROD):
                        at = HALF * par + HD * k
                        sp.dma_start(QS[nb][at:at + HD, :, par, :], qparts[HALF * par:HALF * par + HALF, part, :]).then_inc(S["qs_in"], 16)
            elif stage == "k_low":
                sp.wait_ge(S["k_lo"], r + 1)
                if used:
                    sp.wait_ge(S["pv_done"], N)
                for par in range(2):
                    for k, part in enumerate(KPROD):
                        at = HALF * par + HD * k
                        sp.dma_start(KS[nb][at:at + HD, :, :], kparts[HALF * par:HALF * par + HALF, part, :]).then_inc(S["ks_in"], 16)
            elif stage[0] == "mask":
                j = stage[1]
                src, st, _ = mask_source(b, j)
                if r * MASKS + j:
                    sp.wait_ge(S["mask_ready"], r * MASKS + j)
                sp.dma_start(st, src).then_inc(S["mask_in"], 16)

        def prepare_pool(pool, stage, r, nb, b):
            if stage[0] == "mask":
                j = stage[1]
                _, st, place = mask_source(b, j)
                pool.wait_ge(S["mask_in"], 16 * (r * MASKS + j + 1))
                if r == 1 and j == 0:
                    pool.wait_ge(S["pv_done"], N)
                if r * MASKS + j:
                    pool.wait_ge(S["mask_ready"], r * MASKS + j)
                to = place(maskq[nb], maskk[nb])
                if clip and j >= QT:
                    pool.tensor_scalar(to, st, 0, MASKED, ALU.is_equal, ALU.mult).then_inc(S["mask_raw"], 1)
                    pool.wait_ge(S["mask_raw"], r * (MASKS - QT) + j - QT + 1)
                    pool.tensor_scalar(to, to, clip, None, ALU.add).then_inc(S["mask_ready"], 1)
                else:
                    pool.tensor_scalar(to, st, 0, MASKED, ALU.is_equal, ALU.mult).then_inc(S["mask_ready"], 1)
            elif stage == "gather":
                pool.wait_ge(S["idx_ready"], r + 1)
                if r:
                    pool.wait_ge(S["memT_done"], r)
                for t in range(QT):
                    pool.indirect_dma_start(mem[:, t, :], None, ctx_rows,
                                            bass.IndirectOffsetOnAxis(ap=hidx[:, t, 0:1], axis=0)).then_inc(mem_in, 16)
                pool.wait_ge(mem_in, (pool_batches(r)) * (16 * QT))
                pool.sem_inc(S["mem_ready"], 1)

        def prepare_act(act, stage, r, nb):
            if stage[0] == "proj_k":
                c = stage[1]
                act.wait_ge(S["pk_done"], NC * r + c + 1)
                if r:
                    act.wait_ge(S["kr_ready"], r)
                dst, src = kf[:, c * 512:c * 512 + chunk(c)], misc[:, 0:chunk(c)]
                ins = act.activation(dst, src, ACT.Identity, bias=cols["bk"][:, :]) if "bk" in w else act.copy(dst, src)
                ins.then_inc(S["kf_ready"], 1)
            elif stage == "k_high":
                act.wait_ge(S["kf_ready"], NC * (r + 1))
                if r:
                    act.wait_ge(S["ks_in"], 16 * 12 * r)
                act.copy(kparts[:, 0, :], kf[:, :]).then_inc(S["k_hi"], 1)
            elif stage == "k_mid":
                act.wait_ge(S["kr_ready"], r + 1)
                act.copy(kparts[:, 1, :], kr[:, :]).then_inc(S["k_mid"], 1)
            elif stage[0] == "proj_v":
                g = stage[1]
                act.wait_ge(S["pv_proj"], VG * r + g + 1)
                if r and g == 0:
                    act.wait_ge(S["pv_done"], N)
                group = range(4 * g, min(4 * g + 4, KT))
                full = [kt for kt in group if keys(kt) == P]
                if full:
                    ins = act.copy(V[nb][:, full[0]:full[-1] + 1, :, 0:HD],
                                   misc[:, 0:P * len(full)].rearrange("p (t h d) -> p t h d", t=len(full), d=HD))
                for kt in group:
                    if keys(kt) < P:
                        k = kt - 4 * g
                        ins = act.copy(V[nb][0:keys(kt), kt, :, 0:HD],
                                       misc[0:keys(kt), k * P:(k + 1) * P].rearrange("p (h d) -> p h d", d=HD))
                ins.then_inc(S["v_ready"], 1)
            elif stage[0] == "hard":
                t, c = stage[1:]
                k = HC * (QT * r + t) + c
                n = min(512, CTX - 512 * c)
                act.wait_ge(S["hs_done"], k + 1)
                if r:
                    act.wait_ge(S["idx_ready"], r)
                act.copy(hs[:, t, c * 512:c * 512 + n], misc[:, 0:n]).then_inc(S["hs_copied"], 1)

        def prepare_pe(pe, take_misc, stage, r):
            if stage == "turn_x":
                pe.wait_ge(S["xn_ready"], r + 1)
                take_misc("xT_ready", r + 1)
                for t in range(QT):
                    ins = pe.transpose(misc[:, t * P:(t + 1) * P], (xn2 if self_ln else xn)[:, t, :], ident[:, :])
                ins.then_inc(S["xT_done"], 1)
            elif stage == "proj_q":
                pe.wait_ge(S["xT_ready"], r + 1)
                take_misc("q_read", r + 1)
                ins = pe.matmul(misc[:, 0:SEQ], wsb["wq"][:, :], xT[:, :], start=True, stop=True)
                if hard:
                    ins = pe.matmul(misc[:, SEQ:2 * SEQ], wsb["wqn"][:, :], xT[:, :], start=False, stop=True, skip_group_check=True)
                ins.then_inc(S["pq_done"], 1)
            elif stage[0] == "hard":
                t, c = stage[1:]
                n = min(512, CTX - 512 * c)
                pe.wait_ge(S["ctx_in"], 16 * (r + 1))
                take_misc("hs_copied", HC * (QT * r + t) + c + 1)
                pe.matmul(misc[:, 0:n], qpT[:, t * P:(t + 1) * P], srcT[:, c * 512:c * 512 + n],
                          start=True, stop=True).then_inc(S["hs_done"], 1)
            elif stage == "turn_mem":
                pe.wait_ge(S["mem_ready"], r + 1)
                take_misc("memT_ready", r + 1)
                for t in range(QT):
                    ins = pe.transpose(misc[:, t * P:(t + 1) * P], mem[:, t, :], ident[:, :])
                ins.then_inc(S["memT_done"], 1)
            elif stage[0] == "proj_k":
                c = stage[1]
                if hard:
                    pe.wait_ge(S["memT_ready"], r + 1)
                elif ctxT is not None:
                    pe.wait_ge(S["ctx_in"], 16 * (r + 1))
                take_misc("kf_ready", NC * r + c + 1)
                pe.matmul(misc[:, 0:chunk(c)], wsb["wk"][:, :], source[:, c * 512:c * 512 + chunk(c)],
                          start=True, stop=True).then_inc(S["pk_done"], 1)
            elif stage[0] == "proj_v":
                g = stage[1]
                take_misc("v_ready", VG * r + g + 1)
                for kt in range(4 * g, min(4 * g + 4, KT)):
                    ins = pe.matmul(misc[0:keys(kt), kt % 4 * P:(kt % 4 + 1) * P], source[:, kt * P:kt * P + keys(kt)], wsb["wv"][:, :],
                                    start=(kt % 4 == 0), stop=True, skip_group_check=True)
                ins.then_inc(S["pv_proj"], 1)
        source = memT if hard else (srcT if ctxT is not None else xT)

        def prepare_dve(dve, chain, stage, r):
            def normalise(src, dst):
                for t in range(QT):
                    ins = dve.bn_stats(stats[:, t, :], src[:, t, :])
                chain(ins)
                for t in range(QT):
                    ins = dve.bn_aggr(mv[:, t, :], stats[:, t, :])
                chain(ins)
                inverse_root(dve, chain, rstd[:, :, :], mv[:, :, 1:2], var, root)
                for t in range(QT):
                    ins = dve.tensor_scalar(dst[:, t, :], src[:, t, :], mv[:, t, 0:1], rstd[:, t, :], ALU.subtract, ALU.mult)
                return ins

            if stage == "norm":
                dve.wait_ge(S["x_in"], 16 * (r + 1))
                if r:
                    dve.wait_ge(S["xT_done"], r)
                    if self_ln:
                        dve.wait_ge(S["xn_out"], 16 * r)
                ins = normalise(x_p, xn)
                if self_ln:
                    chain(ins)
                    ins = normalise(xn, xn2)
                ins.then_inc(S["xn_ready"], 1)
            elif stage == "turn_x":
                dve.wait_ge(S["xT_done"], r + 1)
                if r:
                    dve.wait_ge(S["pq_done"], r)
                    if self_ln:
                        dve.wait_ge(S["pv_proj"], VG * r)
                if self_ln:
                    ins = dve.tensor_scalar(xT[:, :], misc[:, 0:SEQ], cols["lng"][:, :], cols["lnb"][:, :], ALU.mult, ALU.add)
                else:
                    ins = dve.tensor_copy(xT[:, :], misc[:, 0:SEQ])
                ins.then_inc(S["xT_ready"], 1)
            elif stage == "proj_q":
                dve.wait_ge(S["pq_done"], r + 1)
                if hard:
                    if r:
                        dve.wait_ge(S["hs_done"], QT * HC * r)
                    dve.tensor_copy(qpT[:, :], misc[:, SEQ:2 * SEQ])
                if "bq" in w:
                    ins = dve.tensor_scalar(qf[:, :], misc[:, 0:SEQ], cols["bq"][:, :], scale, ALU.add, ALU.mult)
                else:
                    ins = dve.tensor_scalar(qf[:, :], misc[:, 0:SEQ], scale, None, ALU.mult)
                ins.then_inc(S["q_read"], 1)
                dve.wait_ge(S["q_read"], r + 1)
                if r:
                    dve.wait_ge(S["qs_in"], 16 * 12 * r)
                dve.tensor_copy(qparts[:, 0, :], qf[:, :]).then_inc(S["q_split"], 1)
                dve.wait_ge(S["q_split"], 3 * r + 1)
                chain(dve.tensor_tensor(qr[:, :], qf[:, :], qparts[:, 0, :], ALU.subtract))
                dve.tensor_copy(qparts[:, 1, :], qr[:, :]).then_inc(S["q_split"], 1)
                dve.wait_ge(S["q_split"], 3 * r + 2)
                dve.tensor_tensor(qparts[:, 2, :], qr[:, :], qparts[:, 1, :], ALU.subtract).then_inc(S["q_split"], 1)
            elif stage[0] == "hard" and stage[2] == HC - 1:
                t = stage[1]
                dve.wait_ge(S["hs_copied"], HC * (QT * r + t + 1))
                if r and t == 0:
                    dve.wait_ge(S["mem_ready"], r)
                chain(dve.max(hmax[:, t, :], hs[:, t, :]))
                chain(dve.max_index(hidx[:, t, :], hmax[:, t, :], hs[:, t, :]))
                if t == QT - 1:
                    dve.wait_ge(S["rowbase_in"], 16 * (r + 1))
                    dve.tensor_scalar(hidx[:, :, 0:1], hidx[:, :, 0:1], rowbase[:, :], None, ALU.add).then_inc(S["idx_ready"], 1)
            elif stage == "turn_mem":
                dve.wait_ge(S["memT_done"], r + 1)
                if r:
                    dve.wait_ge(S["pv_proj"], VG * r)
                dve.tensor_copy(memT[:, :], misc[:, 0:SEQ]).then_inc(S["memT_ready"], 1)
            elif stage == "k_rest":
                dve.wait_ge(S["k_hi"], r + 1)
                dve.tensor_tensor(kr[:, :], kf[:, :], kparts[:, 0, :], ALU.subtract).then_inc(S["kr_ready"], 1)
            elif stage == "k_low":
                dve.wait_ge(S["k_mid"], r + 1)
                dve.tensor_tensor(kparts[:, 2, :], kr[:, :], kparts[:, 1, :], ALU.subtract).then_inc(S["k_lo"], 1)

        def take_misc_of(pe):
            last_reader = []

            def take_misc(name, count):
                if last_reader:
                    pe.wait_ge(S[last_reader[-1][0]], last_reader[-1][1])
                last_reader.append((name, count))
            return take_misc

        def pool_batches(r):
            return 1
        ALL = PREPARE + [("mask", j) for j in range(MASKS)]
        with nc.Block() as block:
            @block.sync
            def _(sp):
                for stage in ALL:
                    prepare_sp(sp, stage, 0, 0, 0)
                sp.wait_ge(S["qs_in"], 16 * 12)
                sp.wait_ge(S["ks_in"], 16 * 12)
                if self_ln:
                    sp.wait_ge(S["xn_out"], 16)

            @block.gpsimd
            def _(pool):
                for stage in ALL:
                    prepare_pool(pool, stage, 0, 0, 0)

            @block.scalar
            def _(act):
                for stage in ALL:
                    prepare_act(act, stage, 0, 0)

            @block.tensor
            def _(pe):
                take_misc = take_misc_of(pe)
                for stage in ALL:
                    prepare_pe(pe, take_misc, stage, 0)

            @block.vector
            def _(dve):
                chain = Chain(dve, S["chain_v"])
                for stage in ALL:
                    prepare_dve(dve, chain, stage, 0)
        ph.barrier()

        def item(i):
            g, r = divmod(i, ITEMS)
            col, c = divmod(r, NC)
            return g, col, col // 2, col % 2, c

        def items_of_slot(n):
            g, kp = divmod(n, KP)
            if g + AHEAD >= 2 * PAIRS:
                return range(0)
            a, z = ITEMS * kp // KP, ITEMS * (kp + 1) // KP
            return range((g + AHEAD) * ITEMS + a, (g + AHEAD) * ITEMS + z)

        with nc.Fori(0, LOOPS // 2) as it:
            def batch(r):
                return it * 2 + 1 if r == 0 else (it * 2 + 2) % LOOPS

            def pool_batches(r):
                return it * 2 + (2 + r)

            with nc.Block() as block:
                @block.sync
                def _(sp):
                    for bb in range(2):
                        if not (self_ln and bb):
                            sp.dma_start(base[bb][:, :, :], base_dram[it * 2 + bb].rearrange("(t p) c -> p t c", p=P)).then_inc(S["base_in"], 16)

                    def pack_maxima(g):
                        sp.wait_ge(S["mtc_done"], g + 1)
                        bb, p = divmod(g, PAIRS)
                        for par in range(2):
                            at = HALF * par + SHIFT
                            sp.dma_start(QS[bb][at:at + 2, p, par, :], MT[g % 2][2 * par:2 * par + 2, :]).then_inc(m_in[p], 16)

                    def store(bb):
                        sp.wait_ge(S["y_ready"], bb + 1)
                        sp.dma_start(x_out[it * 2 + bb].rearrange("(t p) c -> p t c", p=P), y[bb][:, :, :]).then_inc(S["y_out"], 16)

                    for g in range(AHEAD - 1):
                        pack_maxima(g)
                    for n in range(2 * N):
                        g, kp = divmod(n, KP)
                        if kp == 0 and g + AHEAD - 1 < 2 * PAIRS:
                            pack_maxima(g + AHEAD - 1)
                        for stage, r in plan_of(n):
                            if stage == "proj_o":
                                store(r)
                            else:
                                prepare_sp(sp, stage, r, 1 - r, batch(r))
                        if n == N and self_ln:
                            sp.wait_ge(S["xn_out"], 16)
                            sp.dma_start(base[1][:, :, :], base_dram[it * 2 + 1].rearrange("(t p) c -> p t c", p=P)).then_inc(S["base_in"], 16)
                    store(1)
                    sp.wait_ge(S["y_out"], 32)
                    sp.wait_ge(S["qs_in"], 2 * 16 * 12)
                    sp.wait_ge(S["ks_in"], 2 * 16 * 12)
                    if self_ln:
                        sp.wait_ge(S["xn_out"], 32)

                @block.gpsimd
                def _(pool):
                    for n in range(2 * N):
                        for stage, r in plan_of(n):
                            prepare_pool(pool, stage, r, 1 - r, batch(r))

                @block.scalar
                def _(act):
                    for n in range(2 * N):
                        kp = n % KP
                        act.wait_ge(S["st_done"], n + 1)
                        if n >= 3:
                            act.wait_ge(S["pv_done"], n - 2)
                        tiles = min(2, KT - 2 * kp)
                        k = keys(2 * kp)
                        act.activation(PT[n % 3][0:k, 0:tiles, :], ST[n % 2][0:k, 0:tiles, :], ACT.Exp).then_inc(S["exp_done"], 1)
                        for stage, r in plan_of(n - 1) if n else ():
                            prepare_act(act, stage, r, 1 - r)

                @block.tensor
                def _(pe):
                    take_misc = take_misc_of(pe)

                    def sq(i):
                        g, col, qt, par, c = item(i)
                        bb, p = divmod(g, PAIRS)
                        if i >= 2:
                            pe.wait_ge(S["max_done"], i - 1)
                        if i == PAIRS * ITEMS:
                            pe.wait_ge(S["qs_in"], 16 * 12)
                            pe.wait_ge(S["ks_in"], 16 * 12)
                        at = HALF * par
                        pe.matmul(SQ[i % 2][:, 0:chunk(c)], QS[bb][at:at + PARTS, p, par, qt * P:(qt + 1) * P],
                                  KS[bb][at:at + PARTS, p, c * 512:c * 512 + chunk(c)], start=True, stop=True).then_inc(S["sq_done"], 1)

                    def turn_maxima(g):
                        pe.wait_ge(S["mb_ready"], g + 1)
                        take_misc("mtc_done", g + 1)
                        for qt in range(QT):
                            ins = pe.transpose(miscb[0:4, qt * P:(qt + 1) * P], MB[:, g, 2 * qt:2 * qt + 2, :].rearrange("p a b -> p (a b)"),
                                               identb[:, :])
                        ins.then_inc(S["mt_done"], 1)

                    def key_tiles(n):
                        kp = n % KP
                        return range(2 * kp, min(2 * kp + 2, KT))

                    def add_mask(n, kt, start):
                        pe.matmul(ST[n % 2][0:keys(kt), kt % 2, :], identb[0:keys(kt), 0:keys(kt)],
                                  maskk[n // N][0:keys(kt), kt, :].unsqueeze(1).broadcast_to([keys(kt), 2, SEQ]),
                                  start=start, stop=False, skip_group_check=True)

                    def scores(n):
                        bb, p, kp = n // N, n // KP % PAIRS, n % KP
                        if n >= 2:
                            pe.wait_ge(S["exp_done"], n - 1)
                        if kp == 0:
                            pe.wait_ge(m_in[p], 32 * (bb + 1))
                        if n == N and mask is not None and not MASK_ONCE:
                            pe.wait_ge(S["mask_ready"], MASKS)
                        masked = mask is not None and not clip
                        for kt in key_tiles(n):
                            if masked:
                                add_mask(n, kt, True)
                            ins = pe.matmul(ST[n % 2][0:keys(kt), kt % 2, :], KS[bb][:, p, kt * P:kt * P + keys(kt)],
                                            QS[bb][:, p, :, :].rearrange("p a q -> p (a q)"), start=not masked, stop=True, skip_group_check=True)
                        ins.then_inc(S["st_raw" if clip else "st_done"], 1)

                    def shift(n):
                        bb, p, kp = n // N, n // KP % PAIRS, n % KP
                        pe.wait_ge(S["clipped"], n + 1)
                        for kt in key_tiles(n):
                            ins = pe.matmul(ST[n % 2][0:keys(kt), kt % 2, :], shiftsel[:, 0:keys(kt)],
                                            QS[bb][:, p, :, :].rearrange("p a q -> p (a q)"), start=False, stop=True, skip_group_check=True)
                        ins.then_inc(S["st_done"], 1)

                    def weigh(n, between=()):
                        between = list(between)
                        bb, p, kp = n // N, n // KP % PAIRS, n % KP
                        pe.wait_ge(S["exp_done"], n + 1)
                        if kp == 0 and n:
                            pe.wait_ge(S["o_copied"], n // KP)
                        if n == N:
                            pe.wait_ge(S["v_ready"], VG)
                        for kt in key_tiles(n):
                            for par in range(2):
                                at = 32 * (2 * (kt % 2) + par)
                                ins = pe.matmul(O[at:at + HD + 1, 0:SEQ], V[bb][0:keys(kt), kt, 2 * p + par, :],
                                                PT[n % 3][0:keys(kt), kt % 2, par * SEQ:(par + 1) * SEQ],
                                                start=(kt < 2), stop=(kt + 2 >= KT), skip_group_check=True)
                            if kt == 2 * kp and between:
                                if keys(kt) == P and kt != LAST:
                                    sq(between.pop(0))
                        ins.then_inc(S["pv_done"], 1)
                        for i in between:
                            sq(i)

                    def gather_pair(g):
                        pe.wait_ge(S["o_copied"], g + 1)
                        take_misc("pair_done", g + 1)
                        for qt in range(QT):
                            ins = pe.matmul(misc[:, qt * 18:(qt + 1) * 18], osb[g % 2][:, qt * P:(qt + 1) * P], pick[:, :],
                                            start=(qt == 0), stop=True, skip_group_check=True)
                        ins.then_inc(S["fin_done"], 1)

                    def finish(stage, bb):
                        if stage == "turn_attn":
                            pe.wait_ge(S["attn_ready"], bb + 1)
                            take_misc("at_ready", bb + 1)
                            for t in range(QT):
                                ins = pe.transpose(misc[:, t * P:(t + 1) * P], attn[:, t, :], ident[:, :])
                            ins.then_inc(S["at_done"], 1)
                        elif stage == "proj_o":
                            pe.wait_ge(S["at_ready"], bb + 1)
                            take_misc("y_ready", bb + 1)
                            for t in range(QT):
                                ins = pe.matmul(misc[:, t * P:(t + 1) * P], attnT[:, t * P:(t + 1) * P], wsb["wo"][:, :],
                                                start=(t == 0), stop=True, skip_group_check=True)
                            ins.then_inc(S["po_done"], 1)

                    for i in range(AHEAD * ITEMS):
                        sq(i)
                    for g in range(AHEAD - 1):
                        turn_maxima(g)
                    scores(0)
                    for n in range(2 * N):
                        g, kp = divmod(n, KP)
                        items = items_of_slot(n)
                        if n + 1 < 2 * N:
                            scores(n + 1)
                        for i in items[:1]:
                            sq(i)
                        if clip:
                            shift(n)
                        if n:
                            weigh(n - 1, items[1:])
                        else:
                            for i in items[1:]:
                                sq(i)
                        if kp == 0 and g + AHEAD - 1 < 2 * PAIRS:
                            turn_maxima(g + AHEAD - 1)
                        if kp == min(1, KP - 1) and g:
                            gather_pair(g - 1)
                        for stage, r in plan_of(n):
                            if stage in FINISH:
                                finish(stage, r)
                            else:
                                prepare_pe(pe, take_misc, stage, r)
                    weigh(2 * N - 1)
                    gather_pair(2 * PAIRS - 1)
                    for stage in FINISH:
                        finish(stage, 1)

                @block.vector
                def _(dve):
                    chain = Chain(dve, S["chain_v"])

                    def maximum(i):
                        g, col, qt, par, c = item(i)
                        dve.wait_ge(S["sq_done"], i + 1)
                        if i == PAIRS * ITEMS and mask is not None and not MASK_ONCE:
                            dve.wait_ge(S["mask_ready"], MASKS)
                        n = chunk(c)
                        if mask is not None:
                            if i >= 2:
                                dve.wait_ge(S["max_done"], i - 1)
                            dve.tensor_tensor_reduce(out=junk[i % 2][:, 0:n], in0=SQ[i % 2][:, 0:n],
                                                     in1=maskq[g // PAIRS][:, qt, c * 512:c * 512 + n],
                                                     scale=1.0, scalar=-3e38, op0=ALU.add, op1=ALU.max,
                                                     accum_out=mx[:, g, col, c:c + 1]).then_inc(S["max_done"], 1)
                        else:
                            dve.tensor_reduce(mx[:, g, col, c:c + 1], SQ[i % 2][:, 0:n], AX.X, ALU.max).then_inc(S["max_done"], 1)

                    def split_maxima(g):
                        dve.wait_ge(S["max_done"], (g + 1) * ITEMS)
                        if NC > 1:
                            chain(dve.tensor_reduce(mm[:, g, :], mx[:, g, :, :], AX.X, ALU.max))
                            m = mm
                        else:
                            m = mx[:, :, :, 0]
                        if clip:
                            chain(dve.tensor_scalar(mm[:, g, :], m[:, g, :], clip, -clip, ALU.min, ALU.max))
                            m = mm
                        chain(dve.tensor_scalar(MB[:, g, :, 0], m[:, g, :], -1.0, None, ALU.mult))
                        dve.scalar_tensor_tensor(MB[:, g, :, 1], m[:, g, :], -1.0, MB[:, g, :, 0], ALU.mult, ALU.subtract).then_inc(S["mb_ready"], 1)

                    def copy_maxima(g):
                        dve.wait_ge(S["mt_done"], g + 1)
                        if g >= 2:
                            bb, p = divmod(g - 2, PAIRS)
                            dve.wait_ge(m_in[p], 32 * (bb + 1))
                        dve.tensor_copy(MT[g % 2][:, :], miscb[0:4, 0:SEQ]).then_inc(S["mtc_done"], 1)

                    def copy_pair(g):
                        dve.wait_ge(S["pv_done"], (g + 1) * KP)
                        if g >= 2:
                            dve.wait_ge(S["fin_done"], g - 1)
                        dve.tensor_copy(osb[g % 2][:, :], O[:, 0:SEQ]).then_inc(S["o_copied"], 1)

                    def collect_pair(g):
                        bb, p = divmod(g, PAIRS)
                        dve.wait_ge(S["fin_done"], g + 1)
                        dve.tensor_copy(oc[bb][:, :, 2 * p:2 * p + 2, :],
                                        misc[:, 0:36].rearrange("p (t h d) -> p t h d", t=QT, d=HD + 1)).then_inc(S["pair_done"], 1)

                    def clip_scores(n):
                        kp = n % KP
                        dve.wait_ge(S["st_raw"], n + 1)
                        if n == N:
                            dve.wait_ge(S["mask_ready"], MASKS)
                        for kt in range(2 * kp, min(2 * kp + 2, KT)):
                            v = ST[n % 2][0:keys(kt), kt % 2, :].rearrange("p (a q) -> p a q", a=2)
                            ins = dve.scalar_tensor_tensor(v, v, -clip, maskk[n // N][0:keys(kt), kt, :].unsqueeze(1).broadcast_to([keys(kt), 2, SEQ]),
                                                           ALU.max, ALU.min)
                        ins.then_inc(S["clipped"], 1)

                    def finish(stage, bb):
                        if stage == "divide":
                            dve.wait_ge(S["pair_done"], PAIRS * (bb + 1))
                            chain(dve.reciprocal(rec[:, :, :, :], oc[bb][:, :, :, HD:HD + 1]))
                            if bb:
                                dve.wait_ge(S["at_done"], bb)
                            av = attn[:, :, :].rearrange("p t (h d) -> p t h d", d=HD)
                            for t in range(QT):
                                ins = dve.tensor_tensor(av[:, t], oc[bb][:, t, :, 0:HD], rec[:, t, :, :].broadcast_to([P, HEADS, HD]), ALU.mult)
                                if "bv" in w:
                                    chain(ins)
                                    ins = dve.tensor_tensor(attn[:, t, :], attn[:, t, :], rows["bv"][:, :], ALU.add)
                            ins.then_inc(S["attn_ready"], 1)
                        elif stage == "turn_attn":
                            dve.wait_ge(S["at_done"], bb + 1)
                            if bb:
                                dve.wait_ge(S["po_done"], bb)
                            dve.tensor_copy(attnT[:, :], misc[:, 0:SEQ]).then_inc(S["at_ready"], 1)
                        else:
                            dve.wait_ge(S["po_done"], bb + 1)
                            dve.wait_ge(S["base_in"], 32 if not self_ln else 16 * (bb + 1))
                            ins = dve.tensor_tensor(y[bb][:, :, :], misc[:, 0:SEQ].rearrange("p (t c) -> p t c", t=QT), base[bb][:, :, :], ALU.add)
                            if "bo" in w:
                                chain(ins)
                                for t in range(QT):
                                    ins = dve.tensor_tensor(y[bb][:, t, :], y[bb][:, t, :], rows["bo"][:, :], ALU.add)
                            ins.then_inc(S["y_ready"], 1)

                    for g in range(AHEAD):
                        for i in range(g * ITEMS, (g + 1) * ITEMS):
                            maximum(i)
                        split_maxima(g)
                    for g in range(AHEAD - 1):
                        copy_maxima(g)
                    if clip:
                        clip_scores(0)
                    for n in range(2 * N):
                        g, kp = divmod(n, KP)
                        if clip and n + 1 < 2 * N:
                            clip_scores(n + 1)
                        items = items_of_slot(n)
                        for i in items[:1]:
                            maximum(i)
                        if kp == 0 and g:
                            copy_pair(g - 1)
                        for i in items[1:]:
                            maximum(i)
                        if kp == KP - 1 and g + AHEAD < 2 * PAIRS:
                            split_maxima(g + AHEAD)
                        if kp == 0 and g + AHEAD - 1 < 2 * PAIRS:
                            copy_maxima(g + AHEAD - 1)
                        if kp == min(1, KP - 1) and g:
                            collect_pair(g - 1)
                        for stage, r in plan_of(n):
                            if stage in FINISH:
                                finish(stage, r)
                            else:
                                prepare_dve(dve, chain, stage, r)
                    copy_pair(2 * PAIRS - 1)
                    collect_pair(2 * PAIRS - 1)
                    for stage in FINISH:
                        finish(stage, 1)
            ph.barrier()


def top_k(dve, chain, values, k, tri, greater, equal, rank, chosen):
    _, T, E = values.shape
    a = values.unsqueeze(3).broadcast_to([P, T, E, E])
    b = values.unsqueeze(2).broadcast_to([P, T, E, E])
    dve.tensor_tensor(greater, a, b, ALU.is_gt)
    chain(dve.tensor_tensor(equal, a, b, ALU.is_equal))
    chain(dve.tensor_tensor(equal, equal, tri.unsqueeze(1).broadcast_to([P, T, E, E]), ALU.mult))
    chain(dve.tensor_tensor(greater, greater, equal, ALU.add))
    chain(dve.tensor_reduce(rank, greater.rearrange("p t a b -> p t b a"), AX.X, ALU.add))
    chain(dve.tensor_scalar(chosen, rank, float(k), None, ALU.is_lt))


def experts_phase(nc, tag, kind, x_in, x_out, w, consts, extra=None):
    E, TT, D = 8, 4, DIM
    TOK = TT * P
    FT = 3 if kind == "silu" else 4
    FP = 114 if kind == "silu" else P
    STEPS = E * FT
    CHUNKS = LOOPS * SEQ // TOK
    TA = CHUNKS * TT
    two = kind != "relu"

    with ExitStack() as ctx:
        ph = Phase(nc, ctx, tag)
        sb, ps, sem = ph.sb, ph.ps, ph.sem
        ident = sb("ident", [P, P])
        tri = sb("tri", [P, E, E])
        onehot = sb("onehot", [E, E, P])
        W1 = sb("W1", [P, E, FT * FP])
        Wg = sb("Wg", [P, E, FT * FP]) if two else None
        W2 = sb("W2", [FP, E, FT, D])
        b1 = sb("b1", [FP, STEPS])
        bg = sb("bg", [FP, STEPS]) if two else None
        b2 = sb("b2", [E, D]) if kind != "clip" else None
        bo = sb("bo", [P, E]) if kind == "clip" else None
        eg = sb("eg", [P, E]) if kind == "clip" else None
        eb = sb("eb", [P, E]) if kind == "clip" else None
        gw = sb("gw", [P, E])
        gb = sb("gb", [P, E]) if kind == "relu" else None
        lng = sb("lng", [P, D]) if kind == "clip" else (sb("lng", [P, 1]) if kind == "relu" else None)
        lnb = sb("lnb", [P, D]) if kind == "clip" else (sb("lnb", [P, 1]) if kind == "relu" else None)
        ones = sb("ones", [P, P]) if kind == "silu" else None
        csq = sb("csq", [P, E]) if kind == "silu" else None
        x_sb = sb("x_sb", [P, TA, D])
        r_sb = sb("r_sb", [P, TA, D]) if kind == "relu" else None
        stats = sb("stats", [P, TA, 6])
        mv = sb("mv", [P, TA, 2])
        rstd = sb("rstd", [P, TA, 1])
        var = sb("var", [P, TA, 1])
        root = sb("root", [P, TA, 1])
        xn = sb("xn", [P, TA, D])
        xm = sb("xm", [P, TA, D]) if kind == "clip" else None
        xT = sb("xT", [P, TA * P])
        cT = sb("cT", [P, TA * P]) if kind == "clip" else None
        eT = [sb(f"eT{i}", [P, TOK]) for i in range(2)] if kind == "clip" else None
        sq = sb("sq", [P, TA, D]) if kind == "silu" else None
        nrm = sb("nrm", [P, TA, 1])
        L = sb("L", [P, TA, E])
        d2 = sb("d2", [P, TA, E])
        t8 = sb("t8", [P, TA, E])
        greater = sb("greater", [P, TT, E, E])
        equal = sb("equal", [P, TT, E, E])
        rank = sb("rank", [P, TA, E])
        chosen = sb("chosen", [P, TA, E])
        top = sb("top", [P, TA, 1])
        total = sb("total", [P, TA, 1])
        gates = sb("gates", [P, TA, E])
        gT = sb("gT", [E, TA * P])
        gB = [sb(f"gB{i}", [P, TOK]) for i in range(2)]
        A = [sb(f"A{i}", [FP, TOK]) for i in range(3)]
        C = [sb(f"C{i}", [FP, TOK]) for i in range(3)] if kind == "clip" else None
        T = [sb(f"T{i}", [FP, TOK]) for i in range(3)] if two else None
        Hg = [sb(f"Hg{i}", [FP, TOK]) for i in range(3)]
        yo = sb("yo", [P, TOK]) if kind == "clip" else None
        yg = sb("yg", [P, TOK]) if kind == "clip" else None
        yT = sb("yT", [P, TOK])
        out = sb("out", [P, TT, D])
        up1 = [ps(f"up1_{i}", [P, TOK]) for i in range(2)]
        upg = [ps(f"upg_{i}", [P, TOK]) for i in range(2)]
        Y = [ps(f"Y{i}", [P, TOK]) for i in range(2)]
        GB = ps("GB", [P, TOK])
        misc = ps("misc", [P, TOK])
        first = [misc, GB] + Y
        second = up1 + upg

        names = ("setup consts_in csq_ready x_in chain_v xn_ready xm_ready xT_done cT_done xT_ready logits_done shifted gate_exp gates_ready gT_done "
                 "gT_ready gb_done gb_ready e_ready upg_done up_done pre_done clipped act_done prod_done gated down_done y_done y_taken acc_step yT_ready "
                 "out_done out_ready out_sent").split()
        S = {n: sem(n) for n in names}
        x_in_sem = [sem(f"x_in{c}") for c in range(CHUNKS)]

        with nc.Block() as block:
            @block.sync
            def _(sp):
                loads = [(ident[:, :], consts["ident"]), (tri[:, :, :], consts["tri8"]), (onehot[:, :, :], consts["onehot"]),
                         (W1[:, :, :], w["W1"]), (W2[:, :, :, :], w["W2"]), (b1[:, :], w["b1"])]
                if two:
                    loads += [(Wg[:, :, :], w["Wg"]), (bg[:, :], w["bg"])]
                if kind == "clip":
                    loads += [(bo[:, :], w["bo"]), (eg[:, :], w["eg"]), (eb[:, :], w["eb"])]
                    loads += [(t[:, :], w[n].rearrange("(o n) -> o n", o=1).broadcast_to([P, D])) for t, n in ((lng, "lng"), (lnb, "lnb"))]
                else:
                    loads += [(b2[:, :], w["b2"])]
                if kind == "relu":
                    loads += [(t[:, :], w[n].rearrange("(p o) -> p o", o=1)) for t, n in ((lng, "lng"), (lnb, "lnb"))]
                    loads += [(gb[:, :], w["gb"].rearrange("(o n) -> o n", o=1).broadcast_to([P, E]))]
                sp.dma_start(gw[:, :], w["gw"]).then_inc(S["consts_in"], 16)
                for dst, src in loads:
                    sp.dma_start(dst, src).then_inc(S["setup"], 16)
                sp.wait_ge(S["setup"], 16 * len(loads))

            @block.vector
            def _(dve):
                dve.wait_ge(S["consts_in"], 16)
                if kind == "silu":
                    dve.memset(ones[:, :], 1.0)
                    dve.tensor_tensor(csq[:, :], gw[:, :], gw[:, :], ALU.mult).then_inc(S["csq_ready"], 1)
                    dve.wait_ge(S["csq_ready"], 1)
                    dve.tensor_scalar(gw[:, :], gw[:, :], -2.0, None, ALU.mult)
        ph.barrier()

        rows = x_in.rearrange("b s c -> (b s) c")[0:TA * P].rearrange("(t p) c -> p t c", p=P)
        with nc.Block() as block:
            @block.sync
            def _(sp):
                if kind == "relu":
                    more = extra.rearrange("b s c -> (b s) c")[0:TA * P].rearrange("(t p) c -> p t c", p=P)
                for c in range(CHUNKS):
                    tiles = slice(c * TT, (c + 1) * TT)
                    if kind == "relu":
                        sp.dma_start(r_sb[:, tiles, :], more[:, tiles, :]).then_inc(x_in_sem[c], 16)
                    else:
                        sp.dma_start(x_sb[:, tiles, :], rows[:, tiles, :]).then_inc(x_in_sem[c], 16)
                if kind == "relu":
                    sp.dma_start(x_sb[:, :, :], rows).then_inc(S["x_in"], 16)
                    sp.wait_ge(S["x_in"], 16)

            @block.scalar
            def _(act):
                act.wait_ge(S["shifted"], 1)
                act.activation(t8[:, :, :], L[:, :, :], ACT.Exp).then_inc(S["gate_exp"], 1)

            @block.tensor
            def _(pe):
                for c in range(CHUNKS):
                    pe.wait_ge(S["xn_ready"], c + 1)
                    for t in range(TT):
                        ins = pe.transpose(first[c][:, t * P:(t + 1) * P], xn[:, c * TT + t, :], ident[:, :])
                    ins.then_inc(S["xT_done"], 1)
                    if kind == "clip":
                        pe.wait_ge(S["xm_ready"], c + 1)
                        for t in range(TT):
                            ins = pe.transpose(second[c][:, t * P:(t + 1) * P], xm[:, c * TT + t, :], ident[:, :])
                        ins.then_inc(S["cT_done"], 1)
                pe.wait_ge(S["xT_ready"], CHUNKS)
                for t in range(TA):
                    o = misc[:, t * E:(t + 1) * E]
                    if kind == "silu":
                        pe.matmul(o, ones[:, :], csq[:, :], start=(t == 0), stop=False, skip_group_check=True)
                    ins = pe.matmul(o, xT[:, t * P:(t + 1) * P], gw[:, :], start=(t == 0 and kind != "silu"), stop=True, skip_group_check=True)
                ins.then_inc(S["logits_done"], 1)
                pe.wait_ge(S["gates_ready"], 1)
                for t in range(TA):
                    ins = pe.transpose(first[t // TT][0:E, t % TT * P:(t % TT + 1) * P], gates[:, t, :], ident[:, :])
                ins.then_inc(S["gT_done"], 1)

            @block.vector
            def _(dve):
                chain = Chain(dve, S["chain_v"])

                def normalise(src, dst, tiles):
                    a, z = tiles[0], tiles[-1] + 1
                    for t in tiles:
                        ins = dve.bn_stats(stats[:, t, :], src[:, t, :])
                    chain(ins)
                    for t in tiles:
                        ins = dve.bn_aggr(mv[:, t, :], stats[:, t, :])
                    chain(ins)
                    inverse_root(dve, chain, rstd[:, a:z, :], mv[:, a:z, 1:2], var[:, a:z], root[:, a:z])
                    for t in tiles:
                        ins = dve.tensor_scalar(dst[:, t, :], src[:, t, :], mv[:, t, 0:1], rstd[:, t, :], ALU.subtract, ALU.mult)
                    return ins

                for c in range(CHUNKS):
                    tiles = range(c * TT, (c + 1) * TT)
                    whole = slice(c * TT, (c + 1) * TT)
                    dve.wait_ge(x_in_sem[c], 16)
                    ins = normalise(r_sb if kind == "relu" else x_sb, xn, tiles)
                    if kind == "clip":
                        chain(ins)
                        chain(normalise(xn, xm, tiles))
                        chain(dve.tensor_tensor(xn[:, whole, :], xm[:, whole, :], lng[:, :].unsqueeze(1).broadcast_to([P, TT, D]), ALU.mult))
                        ins = dve.tensor_tensor(xn[:, whole, :], xn[:, whole, :], lnb[:, :].unsqueeze(1).broadcast_to([P, TT, D]), ALU.add)
                    ins.then_inc(S["xn_ready"], 1)
                    if kind == "clip":
                        dve.wait_ge(S["xn_ready"], c + 1)
                        normalise(xn, xm, tiles).then_inc(S["xm_ready"], 1)
                for c in range(CHUNKS):
                    cols = slice(c * TOK, (c + 1) * TOK)
                    dve.wait_ge(S["xT_done"], c + 1)
                    if kind == "relu":
                        dve.tensor_scalar(xT[:, cols], first[c][:, :], lng[:, :], lnb[:, :], ALU.mult, ALU.add).then_inc(S["xT_ready"], 1)
                    else:
                        dve.tensor_copy(xT[:, cols], first[c][:, :]).then_inc(S["xT_ready"], 1)
                    if kind == "clip":
                        dve.wait_ge(S["cT_done"], c + 1)
                        dve.tensor_copy(cT[:, cols], second[c][:, :])
                if kind == "silu":
                    chain(dve.tensor_tensor(sq[:, :, :], xn[:, :, :], xn[:, :, :], ALU.mult))
                    chain(dve.tensor_reduce(nrm[:, :, :], sq[:, :, :], AX.X, ALU.add))
                dve.wait_ge(S["logits_done"], 1)
                raw = misc[:, 0:TA * E].rearrange("p (t e) -> p t e", e=E)
                if kind == "relu":
                    chain(dve.tensor_tensor(L[:, :, :], raw, gb[:, :].unsqueeze(1).broadcast_to([P, TA, E]), ALU.add))
                elif kind == "clip":
                    chain(dve.tensor_copy(L[:, :, :], raw))
                else:
                    chain(dve.tensor_tensor(d2[:, :, :], raw, nrm[:, :, :].broadcast_to([P, TA, E]), ALU.add))
                    chain(dve.tensor_scalar(d2[:, :, :], d2[:, :, :], 1e-12, None, ALU.max))
                    inverse_root(dve, chain, L[:, :, :], d2[:, :, :], rank, t8, eps=0.0)
                    chain(dve.tensor_tensor(L[:, :, :], L[:, :, :], d2[:, :, :], ALU.mult))
                for c in range(CHUNKS):
                    whole = slice(c * TT, (c + 1) * TT)
                    top_k(dve, chain, L[:, whole, :], 2, tri[:, :, :], greater[:, :, :, :], equal[:, :, :, :], rank[:, whole, :], chosen[:, whole, :])
                chain(dve.tensor_reduce(top[:, :, :], L[:, :, :], AX.X, ALU.max))
                dve.tensor_tensor(L[:, :, :], L[:, :, :], top[:, :, :].broadcast_to([P, TA, E]), ALU.subtract).then_inc(S["shifted"], 1)
                dve.wait_ge(S["gate_exp"], 1)
                chain(dve.tensor_tensor(t8[:, :, :], t8[:, :, :], chosen[:, :, :], ALU.mult))
                chain(dve.tensor_reduce(total[:, :, :], t8[:, :, :], AX.X, ALU.add))
                chain(dve.reciprocal(total[:, :, :], total[:, :, :]))
                dve.tensor_tensor(gates[:, :, :], t8[:, :, :], total[:, :, :].broadcast_to([P, TA, E]), ALU.mult).then_inc(S["gates_ready"], 1)
                dve.wait_ge(S["gT_done"], 1)
                for c in range(CHUNKS):
                    dve.tensor_copy(gT[:, c * TOK:(c + 1) * TOK], first[c][0:E, :])
        ph.barrier()

        with nc.Fori(0, CHUNKS) as i:
            rows_out = x_out.rearrange("b s c -> (b s) c").rearrange("(n t p) c -> n p t c", t=TT, p=P)
            now = bass.ds(i * TOK, TOK)
            with nc.Block() as block:
                @block.sync
                def _(sp):
                    sp.wait_ge(S["out_ready"], 1)
                    sp.dma_start(rows_out[i], out[:, :, :]).then_inc(S["out_sent"], 16)
                    sp.wait_ge(S["out_sent"], 16)

                @block.gpsimd
                def _(pool):
                    if kind == "silu":
                        for s in range(STEPS):
                            pool.wait_ge(S["prod_done"], s + 1)
                            if s >= 3:
                                pool.wait_ge(S["down_done"], s - 2)
                            if s % FT == 0:
                                pool.wait_ge(S["gb_ready"], s // FT + 1)
                            pool.tensor_tensor(Hg[s % 3][:, :], T[s % 3][:, :], gB[s // FT % 2][0:FP, :], ALU.mult).then_inc(S["gated"], 1)

                @block.scalar
                def _(act):
                    def pre(s):
                        act.wait_ge(S["upg_done"], s + 1)
                        if s >= 3:
                            act.wait_ge(S["act_done"], s - 2)
                        act.activation(C[s % 3][:, :], upg[s % 2][:, :], ACT.Identity, bias=bg[:, s:s + 1]).then_inc(S["pre_done"], 1)

                    if kind == "clip":
                        pre(0)
                    for s in range(STEPS):
                        if kind == "clip":
                            if s + 1 < STEPS:
                                pre(s + 1)
                            act.wait_ge(S["clipped"], s + 1)
                            src, bias = C[s % 3][:, :], 0.0
                        else:
                            act.wait_ge(S["upg_done" if two else "up_done"], s + 1)
                            src = (upg if two else up1)[s % 2][0:FP, :]
                            bias = (bg if two else b1)[:, s:s + 1]
                        if s >= 3:
                            act.wait_ge(S["prod_done" if two else "gated"], s - 2)
                        act.activation(A[s % 3][:, :], src, ACT.Silu if two else ACT.Relu, bias=bias).then_inc(S["act_done"], 1)

                @block.tensor
                def _(pe):
                    def spread(e):
                        if e:
                            pe.wait_ge(S["gb_ready"], e)
                        pe.matmul(GB[:, :], onehot[:, e, :], gT[:, now], start=True, stop=True).then_inc(S["gb_done"], 1)

                    def up(s):
                        e, f = divmod(s, FT)
                        if kind == "clip" and f == 0:
                            pe.wait_ge(S["e_ready"], e + 1)
                        if s >= 2:
                            if two:
                                pe.wait_ge(S["pre_done" if kind == "clip" else "act_done"], s - 1)
                            else:
                                pe.wait_ge(S["act_done"], s - 1)
                        x = eT[e % 2][:, :] if kind == "clip" else xT[:, now]
                        if two:
                            pe.matmul(upg[s % 2][0:FP, :], Wg[:, e, f * FP:(f + 1) * FP], x, start=True, stop=True).then_inc(S["upg_done"], 1)
                            if s >= 2:
                                pe.wait_ge(S["prod_done"], s - 1)
                        pe.matmul(up1[s % 2][0:FP, :], W1[:, e, f * FP:(f + 1) * FP], x, start=True, stop=True).then_inc(S["up_done"], 1)

                    def down(s):
                        e, f = divmod(s, FT)
                        pe.wait_ge(S["gated"], s + 1)
                        if kind == "clip":
                            if f == 0 and e >= 2:
                                pe.wait_ge(S["y_taken"], e - 1)
                            pe.matmul(Y[e % 2][:, :], W2[:, e, f, :], Hg[s % 3][:, :], start=(f == 0), stop=(f == FT - 1)).then_inc(S["down_done"], 1)
                        else:
                            pe.matmul(Y[0][:, :], W2[:, e, f, :], Hg[s % 3][:, :], start=False, stop=(s == STEPS - 1)).then_inc(S["down_done"], 1)

                    spread(0)
                    up(0)
                    up(1)
                    if kind != "clip":
                        pe.matmul(Y[0][:, :], b2[:, :], gT[:, now], start=True, stop=False)
                    for s in range(STEPS):
                        if s % FT == FT - 2 and s // FT + 1 < E:
                            spread(s // FT + 1)
                        if s + 2 < STEPS:
                            up(s + 2)
                        down(s)
                    pe.wait_ge(S["yT_ready"], 1)
                    for t in range(TT):
                        ins = pe.transpose(misc[:, t * P:(t + 1) * P], yT[:, t * P:(t + 1) * P], ident[:, :])
                    ins.then_inc(S["out_done"], 1)

                @block.vector
                def _(dve):
                    chain = Chain(dve, S["chain_v"])

                    def take_gate(e):
                        dve.wait_ge(S["gb_done"], e + 1)
                        if kind == "silu" and e >= 2:
                            dve.wait_ge(S["gated"], (e - 1) * FT)
                        dve.tensor_copy(gB[e % 2][:, :], GB[:, :]).then_inc(S["gb_ready"], 1)

                    def expert_input(e):
                        if e >= 2:
                            dve.wait_ge(S["up_done"], (e - 1) * FT)
                        dve.tensor_scalar(eT[e % 2][:, :], cT[:, now], eg[:, e:e + 1], eb[:, e:e + 1], ALU.mult, ALU.add).then_inc(S["e_ready"], 1)

                    def clip_gate(s):
                        dve.wait_ge(S["pre_done"], s + 1)
                        dve.tensor_scalar(C[s % 3][:, :], C[s % 3][:, :], 20.0, -20.0, ALU.min, ALU.max).then_inc(S["clipped"], 1)

                    if kind == "clip":
                        expert_input(0)
                        dve.memset(yT[:, :], 0.0).then_inc(S["acc_step"], 1)
                        clip_gate(0)
                    for s in range(STEPS):
                        e, f = divmod(s, FT)
                        if f == 0:
                            take_gate(e)
                            if kind == "clip" and e + 1 < E:
                                expert_input(e + 1)
                        if kind == "relu":
                            if f == 0:
                                dve.wait_ge(S["gb_ready"], e + 1)
                            dve.wait_ge(S["act_done"], s + 1)
                            if s >= 3:
                                dve.wait_ge(S["down_done"], s - 2)
                            dve.tensor_tensor(Hg[s % 3][:, :], A[s % 3][:, :], gB[e % 2][:, :], ALU.mult).then_inc(S["gated"], 1)
                            continue
                        if kind == "clip" and s + 1 < STEPS:
                            clip_gate(s + 1)
                        dve.wait_ge(S["act_done"], s + 1)
                        dve.wait_ge(S["up_done"], s + 1)
                        if s >= 3:
                            dve.wait_ge(S["gated"], s - 2)
                        dve.scalar_tensor_tensor(T[s % 3][:, :], up1[s % 2][0:FP, :], b1[:, s:s + 1], A[s % 3][:, :], ALU.add, ALU.mult
                                                 ).then_inc(S["prod_done"], 1)
                        if kind == "silu":
                            continue
                        dve.wait_ge(S["prod_done"], s + 1)
                        if s >= 3:
                            dve.wait_ge(S["down_done"], s - 2)
                        dve.tensor_scalar(Hg[s % 3][:, :], T[s % 3][:, :], 1e4, -1e4, ALU.min, ALU.max).then_inc(S["gated"], 1)
                        if f == 2 and e or s == STEPS - 1:
                            for k in ([e - 1] if s < STEPS - 1 else [e]):
                                dve.wait_ge(S["down_done"], (k + 1) * FT)
                                dve.tensor_scalar(yo[:, :], Y[k % 2][:, :], bo[:, k:k + 1], 1e4, ALU.add, ALU.min).then_inc(S["y_taken"], 1)
                                dve.wait_ge(S["y_taken"], k + 1)
                                dve.wait_ge(S["gb_ready"], k + 1)
                                chain(dve.scalar_tensor_tensor(yg[:, :], yo[:, :], -1e4, gB[k % 2][:, :], ALU.max, ALU.mult))
                                ins = dve.tensor_tensor(yT[:, :], yT[:, :], yg[:, :], ALU.add)
                                if k == E - 1:
                                    ins.then_inc(S["yT_ready"], 1)
                                else:
                                    chain(ins)
                    if kind != "clip":
                        dve.wait_ge(S["down_done"], STEPS)
                        dve.tensor_copy(yT[:, :], Y[0][:, :]).then_inc(S["yT_ready"], 1)
                    dve.wait_ge(S["out_done"], 1)
                    these = bass.ds(i * TT, TT)
                    ins = dve.tensor_tensor(out[:, :, :], misc[:, :].rearrange("p (t c) -> p t c", t=TT), x_sb[:, these, :], ALU.add)
                    if kind == "relu":
                        chain(ins)
                        ins = dve.tensor_tensor(out[:, :, :], out[:, :, :], r_sb[:, these, :], ALU.add)
                    ins.then_inc(S["out_ready"], 1)
            ph.barrier()


def switch_phase(nc, tag, x_in, x_out, w, consts):
    H, E, K, DH = 8, 5, 3, 64
    HD_ALL = H * DH
    ZT_TILES = ceil(E * DH, P)
    USES = [(j, e, t) for j in range(3) for e in range(E) for t in range(QT)]

    with ExitStack() as ctx:
        ph = Phase(nc, ctx, tag)
        sb, ps, sem = ph.sb, ph.ps, ph.sem
        ident = sb("ident", [P, P])
        tri = sb("tri", [P, E, E])
        W = sb("W", [P, 3, E, HD_ALL])
        Wr = sb("Wr", [P, 2, H * E])
        Wo = sb("Wo", [P, ZT_TILES, DIM])
        x_sb = sb("x_sb", [P, QT, DIM])
        stats = sb("stats", [P, QT, 6])
        mv = sb("mv", [P, QT, 2])
        rstd = sb("rstd", [P, QT, 1])
        var = sb("var", [P, QT, 1])
        root = sb("root", [P, QT, 1])
        xn = sb("xn", [P, QT, DIM])
        xT = sb("xT", [P, SEQ])
        G = QT * 2 * H
        sig = sb("sig", [P, G, E])
        greater = sb("greater", [P, G, E, E])
        equal = sb("equal", [P, G, E, E])
        rank = sb("rank", [P, G, E])
        chosen = sb("chosen", [P, G, E])
        gate = sb("gate", [P, G, E])
        prod = [sb(f"prod{i}", [P, HD_ALL]) for i in range(3)]
        acc = sb("acc", [P, 3, QT, HD_ALL])
        qT = sb("qT", [P, H // 2, SEQ])
        kT = sb("kT", [P, H // 2, SEQ])
        mx = sb("mx", [P, H, QT])
        sums = sb("sums", [P, QT, H])
        pr = [sb(f"pr{i}", [P, QT, SEQ]) for i in range(3)]
        pT = [sb(f"pT{i}", [P, QT, SEQ]) for i in range(3)]
        pick = sb("pick", [P, QT, H, E])
        zp = [sb(f"zp{i}", [P, H, DH]) for i in range(2)]
        Z = sb("Z", [P, QT, E, DH])
        ZT = sb("ZT", [P, QT, ZT_TILES, P])
        out = sb("out", [P, QT, DIM])
        bank = [ps(f"bank{i}", [P, 512]) for i in range(8)]

        names = ("setup x_in chain_v xn_ready xT_done xT_ready logits_done sig_exp neg_done gate_ready proj_done prod_done acc_done "
                 "qk_done qk_ready s_done max_ready exp_done pt_done pt_ready pv_done zp_done z_ready zt_done zt_ready out_done "
                 "out_ready out_sent").split()
        S = {n: sem(n) for n in names}

        with nc.Block() as block:
            @block.sync
            def _(sp):
                loads = [(ident[:, :], consts["ident"]), (tri[:, :, :], consts["tri5"]), (W[:, :, :, :], w["W"]), (Wr[:, :, :], w["Wr"]),
                         (Wo[:, 0:2, :], w["Wo"][0:2 * P].rearrange("(t p) n -> p t n", p=P)), (Wo[0:DH, 2, :], w["Wo"][2 * P:])]
                for dst, src in loads:
                    sp.dma_start(dst, src).then_inc(S["setup"], 16)
                sp.wait_ge(S["setup"], 16 * len(loads))
        ph.barrier()

        with nc.Fori(0, LOOPS) as b:
            with nc.Block() as block:
                @block.sync
                def _(sp):
                    sp.dma_start(x_sb[:, :, :], x_in[b].rearrange("(t p) c -> p t c", p=P)).then_inc(S["x_in"], 16)
                    sp.wait_ge(S["out_ready"], 1)
                    sp.dma_start(x_out[b].rearrange("(t p) c -> p t c", p=P), out[:, :, :]).then_inc(S["out_sent"], 16)
                    sp.wait_ge(S["out_sent"], 16)

                @block.gpsimd
                def _(pool):
                    for u, (j, e, t) in enumerate(USES):
                        if e == 0:
                            continue
                        pool.wait_ge(S["prod_done"], u + 1)
                        n = sum(v[1] > 0 for v in USES[:u])
                        if e > 1:
                            pool.wait_ge(S["acc_done"], n - QT + 1)
                        pool.tensor_tensor(acc[:, j, t, :], acc[:, j, t, :], prod[u % 3][:, :], ALU.add).then_inc(S["acc_done"], 1)

                def turn_out(act, h):
                    act.wait_ge(S["pt_done"], h + 1)
                    if h >= 3:
                        act.wait_ge(S["pv_done"], h - 2)
                    act.copy(pT[h % 3][:, :, :], bank[3 + h % 2][:, :].rearrange("p (t q) -> p t q", t=QT)).then_inc(S["pt_ready"], 1)

                @block.scalar
                def _(act):
                    act.wait_ge(S["logits_done"], 1)
                    act.activation(sig[:, :, :], bank[7][:, 0:G * E].rearrange("p (g e) -> p g e", e=E), ACT.Exp, scale=-1.0).then_inc(S["sig_exp"], 1)
                    for h in range(H):
                        act.wait_ge(S["max_ready"], h + 1)
                        if h >= 3:
                            act.wait_ge(S["pt_done"], h - 2)
                        for qt in range(QT):
                            ins = act.activation(pr[h % 3][:, qt, :], bank[h % 3][:, qt * SEQ:(qt + 1) * SEQ], ACT.Exp,
                                                 bias=mx[:, h, qt:qt + 1], accum_out=sums[:, qt, h:h + 1])
                        ins.then_inc(S["exp_done"], 1)
                        if h:
                            turn_out(act, h - 1)
                    turn_out(act, H - 1)

                @block.tensor
                def _(pe):
                    pe.wait_ge(S["xn_ready"], 1)
                    for t in range(QT):
                        ins = pe.transpose(bank[6][:, t * P:(t + 1) * P], xn[:, t, :], ident[:, :])
                    ins.then_inc(S["xT_done"], 1)
                    pe.wait_ge(S["xT_ready"], 1)
                    for t in range(QT):
                        ins = pe.matmul(bank[7][:, t * 2 * H * E:(t + 1) * 2 * H * E], xT[:, t * P:(t + 1) * P],
                                        Wr[:, :, :].rearrange("p r n -> p (r n)"), start=(t == 0), stop=True, skip_group_check=True)
                    ins.then_inc(S["logits_done"], 1)
                    for u, (j, e, t) in enumerate(USES):
                        if u >= 4:
                            pe.wait_ge(S["prod_done"], u - 3)
                        pe.matmul(bank[u % 4][:, :], xT[:, t * P:(t + 1) * P], W[:, j, e, :], start=True, stop=True).then_inc(S["proj_done"], 1)
                        if j == 2 and e == 1 and t == 0:
                            pe.wait_ge(S["acc_done"], 2 * QT * (E - 1))
                            for jj in range(2):
                                for c in range(H // 2):
                                    for tt in range(QT):
                                        ins = pe.transpose(bank[4 + 2 * jj + c // 2][:, c % 2 * SEQ + tt * P:c % 2 * SEQ + (tt + 1) * P],
                                                           acc[:, jj, tt, c * P:(c + 1) * P], ident[:, :])
                                ins.then_inc(S["qk_done"], 1)

                    def scores(h):
                        if h >= 3:
                            pe.wait_ge(S["exp_done"], h - 2)
                        at = DH * (h % 2)
                        for qt in range(QT):
                            ins = pe.matmul(bank[h % 3][:, qt * SEQ:(qt + 1) * SEQ], qT[at:at + DH, h // 2, qt * P:(qt + 1) * P],
                                            kT[at:at + DH, h // 2, :], start=(qt == 0), stop=True, skip_group_check=True)
                        ins.then_inc(S["s_done"], 1)

                    def turn(h):
                        pe.wait_ge(S["exp_done"], h + 1)
                        if h >= 2:
                            pe.wait_ge(S["pt_ready"], h - 1)
                        for kt in range(QT):
                            for qt in range(QT):
                                ins = pe.transpose(bank[3 + h % 2][:, kt * SEQ + qt * P:kt * SEQ + (qt + 1) * P],
                                                   pr[h % 3][:, qt, kt * P:(kt + 1) * P], ident[:, :])
                        ins.then_inc(S["pt_done"], 1)

                    def weigh(h):
                        pe.wait_ge(S["pt_ready"], h + 1)
                        for qt in range(QT):
                            for kt in range(QT):
                                ins = pe.matmul(bank[5 + qt][:, h * DH:(h + 1) * DH], pT[h % 3][:, kt, qt * P:(qt + 1) * P],
                                                acc[:, 2, kt, h * DH:(h + 1) * DH], start=(h == 0 and kt == 0), stop=(kt == QT - 1),
                                                skip_group_check=True)
                        ins.then_inc(S["pv_done"], 1)

                    pe.wait_ge(S["qk_ready"], 4)
                    pe.wait_ge(S["prod_done"], len(USES))
                    pe.wait_ge(S["acc_done"], 3 * QT * (E - 1))
                    scores(0)
                    scores(1)
                    for h in range(H):
                        turn(h)
                        if h + 2 < H:
                            scores(h + 2)
                        if h:
                            weigh(h - 1)
                    weigh(H - 1)
                    for qt in range(QT):
                        pe.wait_ge(S["z_ready"], E * (qt + 1))
                        for c in range(ZT_TILES):
                            n = min(P, E * DH - c * P)
                            ins = pe.transpose(bank[qt][0:n, c * P:(c + 1) * P],
                                               Z[:, qt, :, :].rearrange("p e d -> p (e d)")[:, c * P:c * P + n], ident[:, :])
                        ins.then_inc(S["zt_done"], 1)
                    for qt in range(QT):
                        pe.wait_ge(S["zt_ready"], 2 * (qt + 1))
                        for c in range(ZT_TILES):
                            n = min(P, E * DH - c * P)
                            ins = pe.matmul(bank[7][:, qt * P:(qt + 1) * P], ZT[0:n, qt, c, :], Wo[0:n, c, :],
                                            start=(qt == 0 and c == 0), stop=(c == ZT_TILES - 1), skip_group_check=True)
                    ins.then_inc(S["out_done"], 1)

                @block.vector
                def _(dve):
                    chain = Chain(dve, S["chain_v"])
                    dve.wait_ge(S["x_in"], 16)
                    for t in range(QT):
                        ins = dve.bn_stats(stats[:, t, :], x_sb[:, t, :])
                    chain(ins)
                    for t in range(QT):
                        ins = dve.bn_aggr(mv[:, t, :], stats[:, t, :])
                    chain(ins)
                    inverse_root(dve, chain, rstd[:, :, :], mv[:, :, 1:2], var, root)
                    for t in range(QT):
                        ins = dve.tensor_scalar(xn[:, t, :], x_sb[:, t, :], mv[:, t, 0:1], rstd[:, t, :], ALU.subtract, ALU.mult)
                    ins.then_inc(S["xn_ready"], 1)
                    dve.wait_ge(S["xT_done"], 1)
                    dve.tensor_copy(xT[:, :], bank[6][:, 0:SEQ]).then_inc(S["xT_ready"], 1)
                    dve.wait_ge(S["sig_exp"], 1)
                    chain(dve.tensor_scalar(sig[:, :, :], sig[:, :, :], 1.0, None, ALU.add))
                    chain(dve.reciprocal(sig[:, :, :], sig[:, :, :]))
                    top_k(dve, chain, sig[:, :, :], K, tri[:, :, :], greater[:, :, :, :], equal[:, :, :, :], rank[:, :, :], chosen[:, :, :])
                    chain(dve.tensor_tensor(gate[:, :, :], sig[:, :, :], chosen[:, :, :], ALU.mult))
                    gv = gate[:, :, :].rearrange("p (t r h) e -> p t r h e", t=QT, r=2)
                    cv = chosen[:, :, :].rearrange("p (t r h) e -> p t r h e", t=QT, r=2)
                    for u, (j, e, t) in enumerate(USES):
                        dve.wait_ge(S["proj_done"], u + 1)
                        g = gv[:, t, 1 if j == 0 else 0, :, e:e + 1].broadcast_to([P, H, DH])
                        src = bank[u % 4][:, :].rearrange("p (h d) -> p h d", d=DH)
                        if e == 0:
                            dst = acc[:, j, t, :]
                        else:
                            dst = prod[u % 3][:, :]
                            before = [i for i in range(u) if i % 3 == u % 3 and USES[i][1]]
                            if before:
                                dve.wait_ge(S["acc_done"], sum(v[1] > 0 for v in USES[:before[-1] + 1]))
                        dve.tensor_tensor(dst.rearrange("p (h d) -> p h d", d=DH), src, g, ALU.mult).then_inc(S["prod_done"], 1)
                        if j == 2 and e == 2 and t == 0:
                            for jj in range(2):
                                dve.wait_ge(S["qk_done"], jj + 1)
                                for c in range(2):
                                    dst, src = (qT, kT)[jj][:, 2 * c:2 * c + 2, :], bank[4 + 2 * jj + c][:, :].rearrange("p (c t) -> p c t", c=2)
                                    dve.tensor_scalar(dst, src, DH ** -0.5 if jj == 0 else 1.0, None, ALU.mult).then_inc(S["qk_ready"], 1)
                    for h in range(H):
                        dve.wait_ge(S["s_done"], h + 1)
                        chain(dve.tensor_reduce(mx[:, h, :], bank[h % 3][:, :].rearrange("p (t k) -> p t k", t=QT), AX.X, ALU.max))
                        dve.tensor_scalar(mx[:, h, :], mx[:, h, :], -1.0, None, ALU.mult).then_inc(S["max_ready"], 1)
                    dve.wait_ge(S["exp_done"], H)
                    chain(dve.reciprocal(sums[:, :, :], sums[:, :, :]))
                    for t in range(QT):
                        ins = dve.tensor_tensor(pick[:, t, :, :], cv[:, t, 1, :, :], sums[:, t, :].unsqueeze(2).broadcast_to([P, H, E]), ALU.mult)
                    chain(ins)
                    dve.wait_ge(S["pv_done"], H)
                    for k in range(QT * E):
                        qt, e = divmod(k, E)
                        src = bank[5 + qt][:, :].rearrange("p (h d) -> p h d", d=DH)
                        if k >= 2:
                            dve.wait_ge(S["z_ready"], k - 1)
                        dve.tensor_tensor(zp[k % 2][:, :, :], src, pick[:, qt, :, e:e + 1].broadcast_to([P, H, DH]), ALU.mult).then_inc(S["zp_done"], 1)
                        dve.wait_ge(S["zp_done"], k + 1)
                        dve.tensor_reduce(Z[:, qt, e, :], zp[k % 2][:, :, :].rearrange("p h d -> p d h"), AX.X, ALU.add).then_inc(S["z_ready"], 1)
                    for qt in range(QT):
                        dve.wait_ge(S["zt_done"], qt + 1)
                        dve.tensor_copy(ZT[:, qt, 0:2, :], bank[qt][:, 0:2 * P].rearrange("p (c q) -> p c q", c=2)).then_inc(S["zt_ready"], 1)
                        dve.tensor_copy(ZT[0:DH, qt, 2, :], bank[qt][0:DH, 2 * P:3 * P]).then_inc(S["zt_ready"], 1)
                    dve.wait_ge(S["out_done"], 1)
                    dve.tensor_tensor(out[:, :, :], bank[7][:, 0:SEQ].rearrange("p (t c) -> p t c", t=QT), x_sb[:, :, :], ALU.add
                                      ).then_inc(S["out_ready"], 1)
            ph.barrier()


def lay_out(inputs):
    import numpy as np

    a = {k: np.asarray(v) for k, v in inputs.items()}
    head = np.array([[[2 * s + par for s in range(PAIRS)] for _ in range(HD)] for par in range(2)]).reshape(-1)
    d = np.array([[[k] * PAIRS for k in range(HD)] for _ in range(2)]).reshape(-1)
    packed = head * HD + d
    o = {"x": a["x"]}
    o["ctxT"] = np.ascontiguousarray(a["ctx_1024"].transpose(0, 2, 1))
    o["ctx_rows"] = a["ctx_1024"].reshape(BATCH * CTX, DIM)
    for n, m in (("mask8", a["mask_Bx1xSxS2_ik1"]), ("mask1", a["mask_1x1xSxS2_ik1"])):
        o[n] = m
        o[n + "T"] = np.ascontiguousarray(m[:, 0].transpose(0, 2, 1))
    o["a0_wq"], o["a0_wk"] = a["L0_xattn_wq"].T[:, packed], a["L0_xattn_wk"].T[:, packed]
    o["a0_wv"], o["a0_wo"] = a["L0_xattn_wv"].T, a["L0_xattn_wo"].T
    o["a0_bq"], o["a0_bk"] = a["L0_xattn_bq"][packed], a["L0_xattn_bk"][packed]
    o["a0_bv"], o["a0_bo"] = a["L0_xattn_bv"], a["L0_xattn_bo"]
    wqkv, bqkv = a["L0_ffn_w_qkv"], a["L0_ffn_b_qkv"]
    o["s0_wq"], o["s0_wk"], o["s0_wv"] = wqkv[:, 0:128][:, packed], wqkv[:, 128:256][:, packed], wqkv[:, 256:384]
    o["s0_bq"], o["s0_bk"], o["s0_bv"] = bqkv[0:128][packed], bqkv[128:256][packed], bqkv[256:384]
    o["s0_wo"], o["s0_bo"] = a["L0_ffn_w_o"], a["L0_ffn_b_o"]
    o["s0_lng"], o["s0_lnb"] = a["L0_ffn_ln1_g"], a["L0_ffn_ln1_b"]

    def diagonal(m):
        out = np.zeros((DIM, DIM), m.dtype)
        for h in range(HEADS):
            out[h * HD:(h + 1) * HD, h * HD:(h + 1) * HD] = m.T
        return out
    o["a1_wq"], o["a1_wk"] = diagonal(a["L1_xattn_Wq"])[:, packed], diagonal(a["L1_xattn_Wk"])[:, packed]
    o["a1_wv"], o["a1_wo"], o["a1_bo"] = diagonal(a["L1_xattn_Wv"]), a["L1_xattn_Wo"].T, a["L1_xattn_bo"]
    o["a2_wq"], o["a2_wqn"] = a["L2_xattn_Wq"].T[:, packed], a["L2_xattn_Wq"].T
    o["a2_wk"] = a["L2_xattn_Wkv"].T[:, d]
    o["a2_wv"] = a["L2_xattn_Wkv"].T[:, np.tile(np.arange(HD), HEADS) + HD]
    o["a2_wo"] = a["L2_xattn_Wc"].T
    for k in "qk":
        o["a3_w" + k], o["a3_b" + k] = a["L3_xattn_W" + k][:, packed], a["L3_xattn_b" + k][packed]
    o["a3_wv"], o["a3_bv"], o["a3_wo"], o["a3_bo"] = (a["L3_xattn_" + k] for k in ("Wv", "bv", "Wo", "bo"))

    def experts(tag, up, down, biases, tiles):
        for n, m in up.items():
            o[f"{tag}_{n}"] = m.transpose(1, 0, 2)
        E, F, D = down.shape
        o[f"{tag}_W2"] = down.reshape(E, tiles, F // tiles, D).transpose(2, 0, 1, 3)
        for n, m in biases.items():
            o[f"{tag}_{n}"] = m.reshape(E * tiles, F // tiles).T
    experts("m0", {"W1": a["L0_ffn_W1"]}, a["L0_ffn_W2"], {"b1": a["L0_ffn_b1"]}, 4)
    o["m0_b2"], o["m0_gw"], o["m0_gb"] = a["L0_ffn_b2"], a["L0_ffn_gate_w"], a["L0_ffn_gate_b"]
    o["m0_lng"], o["m0_lnb"] = a["L0_ffn_ln2_g"], a["L0_ffn_ln2_b"]
    experts("m1", {"W1": a["L1_ffn_W1"], "Wg": a["L1_ffn_Wg"]}, a["L1_ffn_W2"], {"b1": a["L1_ffn_b1"], "bg": a["L1_ffn_bg"]}, 3)
    o["m1_b2"], o["m1_gw"] = a["L1_ffn_b2"], a["L1_ffn_centroid"].T
    experts("m2", {"W1": a["L2_ffn_W1"], "Wg": a["L2_ffn_W2"]}, a["L2_ffn_Wo"], {"b1": a["L2_ffn_b1"], "bg": a["L2_ffn_b2"]}, 4)
    o["m2_gw"], o["m2_lng"], o["m2_lnb"] = a["L2_ffn_router_w"], a["L2_ffn_ln_g"], a["L2_ffn_ln_b"]
    o["m2_bo"], o["m2_eg"], o["m2_eb"] = a["L2_ffn_bo"].T, a["L2_ffn_eg"].T, a["L2_ffn_eb"].T
    wq = a["L3_ffn_Wq"].reshape(DIM, 1, 8, 5, 64)
    wkv = a["L3_ffn_Wkv"].reshape(DIM, 2, 8, 5, 64)
    o["m3_W"] = np.concatenate([wq, wkv], axis=1).transpose(0, 1, 3, 2, 4).reshape(DIM, 3, 5, 512)
    o["m3_Wr"] = np.stack([a["L3_ffn_Ws"], a["L3_ffn_Wd"]], axis=1)
    o["m3_Wo"] = a["L3_ffn_Wo"].reshape(64, 5, DIM).transpose(1, 0, 2).reshape(320, DIM)
    for e in (5, 8):
        o[f"tri{e}"] = np.broadcast_to(np.triu(np.ones((e, e), np.float32), 1), (P, e, e))
    o["onehot"] = np.broadcast_to(np.eye(8, dtype=np.float32)[:, :, None], (8, 8, P))
    o["ident"] = np.eye(P, dtype=np.float32)
    pick = np.zeros((P, 2, HD + 1), np.float32)
    for tile in range(2):
        for par in range(2):
            for k in range(HD + 1):
                pick[32 * (2 * tile + par) + k, par, k] = 1.0
    o["pick"] = pick.reshape(P, -1)
    sel = np.zeros((P, P), np.float32)
    for par in range(2):
        sel[HALF * par + SHIFT:HALF * par + SHIFT + 2] = 1.0
    o["shiftsel"] = sel
    o["rowbase"] = np.repeat(np.arange(BATCH, dtype=np.float32)[:, None] * CTX, P, axis=1)
    return {k: np.ascontiguousarray(v) for k, v in o.items()}


def build(nc, t, phases=("a0", "s0", "m0", "a1", "m1", "a2", "m2", "a3", "m3")):
    def weights(tag, *names):
        return {n: t[f"{tag}_{n}"] for n in names}

    consts = {k: t[k] for k in ("ident", "pick", "shiftsel", "rowbase", "tri5", "tri8", "onehot")}
    ROOT8 = float(HD) ** -0.5
    cur = before = t["x"]
    if phases[0] == "m0":
        cur = t["y0"]

    def nxt(tag):
        if tag == phases[-1]:
            return t["out"]
        return nc.dram_tensor(f"x_after_{tag}", [BATCH, SEQ, DIM], F32).ap()
    for tag in phases:
        dst = nxt(tag)
        if tag == "a0":
            attention_phase(nc, tag, cur, dst, weights(tag, "wq", "wk", "wv", "wo", "bq", "bk", "bv", "bo"), consts, ctxT=t["ctxT"],
                            mask=t["mask8"], maskT=t["mask8T"], scale=ROOT8, clip=100.0)
        elif tag == "s0":
            attention_phase(nc, tag, cur, dst, weights(tag, "wq", "wk", "wv", "wo", "bq", "bk", "bv", "bo", "lng", "lnb"), consts,
                            scale=ROOT8, self_ln=True)
        elif tag == "a1":
            attention_phase(nc, tag, cur, dst, weights(tag, "wq", "wk", "wv", "wo", "bo"), consts, ctxT=t["ctxT"],
                            mask=t["mask1"], maskT=t["mask1T"], scale=float(DIM) ** -0.5)
        elif tag == "a2":
            attention_phase(nc, tag, cur, dst, weights(tag, "wq", "wqn", "wk", "wv", "wo"), consts, ctxT=t["ctxT"],
                            ctx_rows=t["ctx_rows"], scale=ROOT8)
        elif tag == "a3":
            attention_phase(nc, tag, cur, dst, weights(tag, "wq", "wk", "wv", "wo", "bq", "bk", "bv", "bo"), consts, ctxT=t["ctxT"],
                            scale=ROOT8)
        elif tag == "m0":
            experts_phase(nc, tag, "relu", before, dst, weights(tag, "W1", "W2", "b1", "b2", "gw", "gb", "lng", "lnb"), consts, extra=cur)
        elif tag == "m1":
            experts_phase(nc, tag, "silu", cur, dst, weights(tag, "W1", "Wg", "W2", "b1", "bg", "b2", "gw"), consts)
        elif tag == "m2":
            experts_phase(nc, tag, "clip", cur, dst, weights(tag, "W1", "Wg", "W2", "b1", "bg", "bo", "eg", "eb", "gw", "lng", "lnb"), consts)
        elif tag == "m3":
            switch_phase(nc, tag, cur, dst, weights(tag, "W", "Wr", "Wo"), consts)
        before, cur = cur, dst


def kernel(**inputs):
    import numpy as _np
    import concourse.bacc as _bacc
    from concourse.bass_utils import run_bass_kernel_spmd as _run

    nc = _bacc.Bacc("TRN2", target_bir_lowering=False, num_devices=1)
    arrays, t = {}, {}
    for name, a in lay_out(inputs).items():
        arrays[f"in_{name}"] = a
        t[name] = nc.dram_tensor(f"in_{name}", a.shape, mybir.dt.from_np(a.dtype), kind="ExternalInput").ap()
    t["out"] = nc.dram_tensor("out_x", [BATCH, SEQ, DIM], F32, kind="ExternalOutput").ap()
    build(nc, t)
    return _run(nc, [arrays], core_ids=[0]).results[0]["out_x"]
```

```python
from contextlib import ExitStack

import concourse.bass as bass
from concourse import mybir

P = 128
F32 = mybir.dt.float32
BF16 = mybir.dt.bfloat16
I32 = mybir.dt.int32
U32 = mybir.dt.uint32
ALU = mybir.AluOpType
ACT = mybir.ActivationFunctionType
AX = mybir.AxisListType

BATCH, SEQ, DIM = 8, 256, 128
LOOPS = BATCH
FIRST_SEMAPHORE = 120
CTX = 1601
HEADS, HD = 16, 8
PAIRS = HEADS // 2
QT = SEQ // P
EPS = 1e-5
MASKED = -1e30
HALF = 64
PARTS = 6 * HD
TWO_ONES = 1.0 + 0x3F80 / 2.0 ** 23
SHIFT = 2 * PARTS


class Phase:

    def __init__(self, nc, ctx, tag):
        self.nc, self.ctx, self.tag, self.sems = nc, ctx, tag, []

    def sb(self, name, shape, dt=F32):
        return self.ctx.enter_context(self.nc.sbuf_tensor(f"{self.tag}_{name}", shape, dt))

    def ps(self, name, shape, dt=F32):
        return self.ctx.enter_context(self.nc.psum_tensor(f"{self.tag}_{name}", shape, dt))

    def sem(self, name):
        num = self.sems[-1].num + 1 if self.sems else FIRST_SEMAPHORE
        s = self.ctx.enter_context(self.nc.semaphore(f"{self.tag}_{name}", num=num))
        self.sems.append(s)
        return s

    def barrier(self):
        self.nc.all_engine_barrier(sems_to_clear=range(self.sems[0].num, self.sems[-1].num + 1))


class Chain:

    def __init__(self, eng, sem):
        self.eng, self.sem, self.n = eng, sem, 0

    def __call__(self, ins):
        self.n += 1
        ins.then_inc(self.sem, 1)
        self.eng.wait_ge(self.sem, self.n)


def ceil(a, b):
    return -(-a // b)


def inverse_root(dve, chain, out, variance, var, tmp, eps=EPS):
    chain(dve.tensor_scalar(var[:], variance, eps, None, ALU.add))
    chain(dve.tensor_scalar(tmp[:].bitcast(I32), var[:].bitcast(I32), 1, None, ALU.arith_shift_right))
    chain(dve.tensor_scalar(out.bitcast(I32), tmp[:].bitcast(I32), -1.0, 1597463007.0, ALU.mult, ALU.add))
    for _ in range(4):
        chain(dve.tensor_tensor(tmp[:], out, out, ALU.mult))
        chain(dve.scalar_tensor_tensor(tmp[:], tmp[:], -0.5, var[:], ALU.mult, ALU.mult))
        chain(dve.scalar_tensor_tensor(out, tmp[:], 1.5, out, ALU.add, ALU.mult))


def normalise(dve, chain, src, dst, stats, mv, rstd, var, root, arrived=None, done=None, part=4):
    T = src.shape[1]
    for t in range(T):
        if arrived is not None and t % part == 0:
            dve.wait_ge(arrived[t // part], 16)
        ins = dve.bn_stats(stats[:, t, :], src[:, t, :])
    chain(ins)
    for t in range(T):
        ins = dve.bn_aggr(mv[:, t, :], stats[:, t, :])
    chain(ins)
    inverse_root(dve, chain, rstd[:, :, :], mv[:, :, 1:2], var, root)
    for t in range(T):
        ins = dve.tensor_scalar(dst[:, t, :], src[:, t, :], mv[:, t, 0:1], rstd[:, t, :], ALU.subtract, ALU.mult)
        if done is not None and t % part == part - 1:
            ins.then_inc(done, 1)
    if done is None:
        chain(ins)


def attention_phase(nc, tag, x_in, x_out, w, consts, ctxT, mask=None, maskT=None,
                    scale=1.0, clip=None):
    NK = CTX
    KT = ceil(NK, P)
    KP = ceil(KT, 2)
    NC = ceil(NK, 512)
    VG = ceil(KT, 4)
    AHEAD = 2
    N = PAIRS * KP
    GROUP = 4 if LOOPS % 4 == 0 else 2
    ITEMS = 2 * QT * NC
    LAST = KT - 1
    MASK_K = [(0, 6), (6, 12), (12, 13)]
    MASKS = (QT + len(MASK_K)) if mask is not None else 0
    MASK_ONCE = mask is not None and mask.shape[0] == 1

    def keys(kt):
        return min(P, NK - kt * P)

    def chunk(c):
        return min(512, NK - c * 512)

    PREPARE = ["load", "norm", "turn_x", "proj_q"]
    PREPARE += [("proj_k", c) for c in range(NC)] + ["k_high", "k_rest", "k_mid", "k_low"]
    PREPARE += [("proj_v", g) for g in range(VG)]
    masks = [("mask", j) for j in range(MASKS)] if not MASK_ONCE else []
    FINISH = ["divide", "turn_attn", "proj_o"]
    span = (PAIRS - AHEAD) * KP - 1
    plan = [[] for _ in range(N)]
    for k, stage in enumerate(PREPARE):
        plan[min(k * 2, span - 1)].append(stage)
    for k, stage in enumerate(masks):
        plan[5 + 6 * k].append(stage)

    def plan_of(n):
        half, k = divmod(n, N)
        out = [(st, half) for st in plan[k]]
        if half and k == min(2, KP):
            out = [(st, half - 1) for st in FINISH] + out
        return out

    with ExitStack() as ctx:
        ph = Phase(nc, ctx, tag)
        sb, ps, sem = ph.sb, ph.ps, ph.sem
        ident = sb("ident", [P, P])
        identb = sb("identb", [P, P], BF16)
        pick = sb("pick", [P, 2 * (HD + 1)])
        shiftsel_f = sb("shiftsel_f", [P, P]) if clip else None
        shiftsel = sb("shiftsel", [P, P], BF16) if clip else None
        wsb = {k: sb("w_" + k, list(w[k].shape)) for k in ("wq", "wk", "wv", "wo") if k in w}
        cols = {k: sb("c_" + k, [P, 1]) for k in ("bq", "bk") if k in w}
        rows = {k: sb("r_" + k, [P, P]) for k in ("bv", "bo") if k in w}
        x_p = sb("x_p", [P, QT, DIM])
        stats = sb("stats", [P, QT, 6])
        mv = sb("mv", [P, QT, 2])
        rstd = sb("rstd", [P, QT, 1])
        var = sb("var", [P, QT, 1])
        root = sb("root", [P, QT, 1])
        xn = sb("xn", [P, QT, DIM])
        xT = sb("xT", [P, SEQ])
        srcT = sb("srcT", [P, CTX])
        kf = sb("kf", [P, NK])
        kr = sb("kr", [P, NK])
        kparts = sb("kparts", [P, 3, NK], BF16)
        qf = sb("qf", [P, SEQ])
        qr = sb("qr", [P, SEQ])
        qparts = sb("qparts", [P, 3, SEQ], BF16)
        if mask is not None:
            stage_i = sb("stage_i", [P, 6 * SEQ + P], I32)
        KS_flat = [sb(f"KS{i}", [P, PAIRS * NK], BF16) for i in range(2)]
        KS = [flat[:, :].rearrange("p (a k) -> p a k", a=PAIRS) for flat in KS_flat]
        QS = [sb(f"QS{i}", [P, PAIRS, 2, SEQ], BF16) for i in range(2)]
        V = [sb(f"V{i}", [P, KT, HEADS, HD + 1]) for i in range(2)]
        nm = 1 if MASK_ONCE else 2
        maskq = [sb(f"maskq{i}", [P, QT, CTX], BF16) for i in range(nm)] * (3 - nm) if mask is not None else None
        maskk = [sb(f"maskk{i}", [P, KT, SEQ], BF16) for i in range(nm)] * (3 - nm) if mask is not None else None
        PT = [sb(f"PT{i}", [P, 2, 512]) for i in range(3)]
        mx = sb("mx", [P, GROUP * PAIRS, QT * 2, NC])
        mm = sb("mm", [P, GROUP * PAIRS, QT * 2])
        MB = sb("MB", [P, GROUP * PAIRS, QT * 2, 2], BF16)
        MT = [sb(f"MT{i}", [4, SEQ], BF16) for i in range(2)]
        junk = [sb(f"junk{i}", [P, 512], BF16) for i in range(2)] if mask is not None else None
        osb = [sb(f"osb{i}", [P, SEQ]) for i in range(2)]
        oc = [sb(f"oc{i}", [P, QT, HEADS, HD + 1]) for i in range(2)]
        rec = sb("rec", [P, QT, HEADS, 1])
        attn = sb("attn", [P, QT, DIM])
        attnT = sb("attnT", [P, SEQ])
        base = [sb(f"base{i}", [P, QT, DIM]) for i in range(2)]
        y = [sb(f"y{i}", [P, QT, DIM]) for i in range(2)]
        ST = [ps(f"ST{i}", [P, 2, 512]) for i in range(2)]
        SQ = [ps(f"SQ{i}", [P, 512]) for i in range(2)]
        O = ps("O", [P, 512])
        misc = ps("misc", [P, 512])
        miscb = misc[:, :].bitcast(BF16)

        names = ("consts_in x_in ctx_in setup filled chain_v xn_ready xT_done xT_ready pq_done q_read q_split pk_done kf_ready "
                 "k_hi kr_ready k_mid k_lo qs_in ks_in pv_proj v_ready mask_in mask_raw mask_ready sq_done max_done mb_ready "
                 "mt_done mtc_done pair_done st_raw clipped st_done exp_done pv_done o_copied fin_done base_in "
                 "attn_ready at_done at_ready po_done y_ready y_out").split()
        S = {n: sem(n) for n in names}
        m_in = [sem(f"m_in{p}") for p in range(PAIRS)]

        QPROD = (0, 1, 0, 1, 2, 0)
        KPROD = (0, 0, 1, 1, 0, 2)

        def mask_source(b, j):
            if j < QT:
                return mask[b, 0, j * P:(j + 1) * P, :], stage_i[:, 0:CTX], lambda m, k: m[:, j, :]
            a, z = MASK_K[j - QT]
            if keys(z - 1) == P:
                st = stage_i[:, 0:(z - a) * SEQ].rearrange("p (t q) -> p t q", q=SEQ)
                return maskT[b, a * P:z * P].rearrange("(t p) q -> p t q", p=P), st, lambda m, k: k[:, a:z, :]
            n = keys(a)
            return maskT[b, a * P:a * P + n], stage_i[0:n, 0:SEQ], lambda m, k: k[0:n, a, :]

        def prepare_sp(sp, stage, r, nb, b):
            if stage == "load":
                if r:
                    sp.wait_ge(S["xn_ready"], r)
                sp.dma_start(x_p[:, :, :], x_in[b].rearrange("(t p) c -> p t c", p=P)).then_inc(S["x_in"], 16)
                if r:
                    sp.wait_ge(S["pv_proj"], VG * r)
                sp.dma_start(srcT[:, :], ctxT[b]).then_inc(S["ctx_in"], 16)
            elif stage == "proj_q":
                sp.wait_ge(S["q_split"], 3 * (r + 1))
                if r:
                    sp.wait_ge(S["pv_done"], N * r)
                for par in range(2):
                    for k, part in enumerate(QPROD):
                        at = PARTS * par + HD * k
                        sp.dma_start(QS[nb][at:at + HD, :, par, :], qparts[HALF * par:HALF * par + HALF, part, :]).then_inc(S["qs_in"], 16)
            elif stage == "k_low":
                sp.wait_ge(S["k_lo"], r + 1)
                if r:
                    sp.wait_ge(S["pv_done"], N * r)
                for par in range(2):
                    for k, part in enumerate(KPROD):
                        at = PARTS * par + HD * k
                        sp.dma_start(KS[nb][at:at + HD, :, :], kparts[HALF * par:HALF * par + HALF, part, :]).then_inc(S["ks_in"], 16)
            elif stage[0] == "mask":
                j = stage[1]
                src, st, _ = mask_source(b, j)
                if r * MASKS + j:
                    sp.wait_ge(S["mask_ready"], r * MASKS + j)
                sp.dma_start(st, src).then_inc(S["mask_in"], 16)

        def prepare_keys(eng, stage, r):
            if stage == "k_rest":
                eng.wait_ge(S["k_hi"], r + 1)
                eng.tensor_tensor(kr[:, :], kf[:, :], kparts[:, 0, :], ALU.subtract).then_inc(S["kr_ready"], 1)
            else:
                eng.wait_ge(S["k_mid"], r + 1)
                eng.tensor_tensor(kparts[:, 2, :], kr[:, :], kparts[:, 1, :], ALU.subtract).then_inc(S["k_lo"], 1)

        def prepare_mask(eng, stage, r, nb, b):
            j = stage[1]
            _, st, place = mask_source(b, j)
            eng.wait_ge(S["mask_in"], 16 * (r * MASKS + j + 1))
            if r and j == 0:
                eng.wait_ge(S["pv_done"], N * r)
            if r * MASKS + j:
                eng.wait_ge(S["mask_ready"], r * MASKS + j)
            to = place(maskq[nb], maskk[nb])
            if clip and j >= QT:
                eng.tensor_scalar(to, st, 0, MASKED, ALU.is_equal, ALU.mult).then_inc(S["mask_raw"], 1)
                eng.wait_ge(S["mask_raw"], r * (MASKS - QT) + j - QT + 1)
                eng.tensor_scalar(to, to, clip, None, ALU.add).then_inc(S["mask_ready"], 1)
            else:
                eng.tensor_scalar(to, st, 0, MASKED, ALU.is_equal, ALU.mult).then_inc(S["mask_ready"], 1)

        def prepare_act(act, stage, r, nb):
            if stage[0] == "proj_k":
                c = stage[1]
                act.wait_ge(S["pk_done"], NC * r + c + 1)
                if r:
                    act.wait_ge(S["kr_ready"], r)
                dst, src = kf[:, c * 512:c * 512 + chunk(c)], misc[:, 0:chunk(c)]
                ins = act.activation(dst, src, ACT.Identity, bias=cols["bk"][:, :]) if "bk" in w else act.copy(dst, src)
                ins.then_inc(S["kf_ready"], 1)
            elif stage == "k_high":
                act.wait_ge(S["kf_ready"], NC * (r + 1))
                if r:
                    act.wait_ge(S["ks_in"], 16 * 12 * r)
                act.copy(kparts[:, 0, :], kf[:, :]).then_inc(S["k_hi"], 1)
            elif stage == "k_mid":
                act.wait_ge(S["kr_ready"], r + 1)
                act.copy(kparts[:, 1, :], kr[:, :]).then_inc(S["k_mid"], 1)
            elif stage[0] == "proj_v":
                g = stage[1]
                act.wait_ge(S["pv_proj"], VG * r + g + 1)
                if r and g == 0:
                    act.wait_ge(S["pv_done"], N * r)
                group = range(4 * g, min(4 * g + 4, KT))
                full = [kt for kt in group if keys(kt) == P]
                if full:
                    ins = act.copy(V[nb][:, full[0]:full[-1] + 1, :, 0:HD],
                                   misc[:, 0:P * len(full)].rearrange("p (t h d) -> p t h d", t=len(full), d=HD))
                for kt in group:
                    if keys(kt) < P:
                        k = kt - 4 * g
                        ins = act.copy(V[nb][0:keys(kt), kt, :, 0:HD],
                                       misc[0:keys(kt), k * P:(k + 1) * P].rearrange("p (h d) -> p h d", d=HD))
                ins.then_inc(S["v_ready"], 1)

        def prepare_pe(pe, take_misc, stage, r):
            if stage == "turn_x":
                pe.wait_ge(S["xn_ready"], r + 1)
                take_misc("xT_ready", r + 1)
                for t in range(QT):
                    ins = pe.transpose(misc[:, t * P:(t + 1) * P], xn[:, t, :], ident[:, :])
                ins.then_inc(S["xT_done"], 1)
            elif stage == "proj_q":
                pe.wait_ge(S["xT_ready"], r + 1)
                take_misc("q_read", r + 1)
                ins = pe.matmul(misc[:, 0:SEQ], wsb["wq"][:, :], xT[:, :], start=True, stop=True)
                ins.then_inc(S["pq_done"], 1)
            elif stage[0] == "proj_k":
                c = stage[1]
                pe.wait_ge(S["ctx_in"], 16 * (r + 1))
                take_misc("kf_ready", NC * r + c + 1)
                pe.matmul(misc[:, 0:chunk(c)], wsb["wk"][:, :], srcT[:, c * 512:c * 512 + chunk(c)],
                          start=True, stop=True).then_inc(S["pk_done"], 1)
            elif stage[0] == "proj_v":
                g = stage[1]
                take_misc("v_ready", VG * r + g + 1)
                for kt in range(4 * g, min(4 * g + 4, KT)):
                    ins = pe.matmul(misc[0:keys(kt), kt % 4 * P:(kt % 4 + 1) * P], srcT[:, kt * P:kt * P + keys(kt)], wsb["wv"][:, :],
                                    start=(kt % 4 == 0), stop=True, skip_group_check=True)
                ins.then_inc(S["pv_proj"], 1)

        def prepare_dve(dve, chain, stage, r):
            def normalise(src, dst):
                for t in range(QT):
                    ins = dve.bn_stats(stats[:, t, :], src[:, t, :])
                chain(ins)
                for t in range(QT):
                    ins = dve.bn_aggr(mv[:, t, :], stats[:, t, :])
                chain(ins)
                inverse_root(dve, chain, rstd[:, :, :], mv[:, :, 1:2], var, root)
                for t in range(QT):
                    ins = dve.tensor_scalar(dst[:, t, :], src[:, t, :], mv[:, t, 0:1], rstd[:, t, :], ALU.subtract, ALU.mult)
                return ins

            if stage == "norm":
                dve.wait_ge(S["x_in"], 16 * (r + 1))
                if r:
                    dve.wait_ge(S["xT_done"], r)
                normalise(x_p, xn).then_inc(S["xn_ready"], 1)
            elif stage == "turn_x":
                dve.wait_ge(S["xT_done"], r + 1)
                if r:
                    dve.wait_ge(S["pq_done"], r)
                dve.tensor_copy(xT[:, :], misc[:, 0:SEQ]).then_inc(S["xT_ready"], 1)
            elif stage == "proj_q":
                dve.wait_ge(S["pq_done"], r + 1)
                if "bq" in w:
                    ins = dve.tensor_scalar(qf[:, :], misc[:, 0:SEQ], cols["bq"][:, :], scale, ALU.add, ALU.mult)
                else:
                    ins = dve.tensor_scalar(qf[:, :], misc[:, 0:SEQ], scale, None, ALU.mult)
                ins.then_inc(S["q_read"], 1)
                dve.wait_ge(S["q_read"], r + 1)
                if r:
                    dve.wait_ge(S["qs_in"], 16 * 12 * r)
                dve.tensor_copy(qparts[:, 0, :], qf[:, :]).then_inc(S["q_split"], 1)
                dve.wait_ge(S["q_split"], 3 * r + 1)
                chain(dve.tensor_tensor(qr[:, :], qf[:, :], qparts[:, 0, :], ALU.subtract))
                dve.tensor_copy(qparts[:, 1, :], qr[:, :]).then_inc(S["q_split"], 1)
                dve.wait_ge(S["q_split"], 3 * r + 2)
                dve.tensor_tensor(qparts[:, 2, :], qr[:, :], qparts[:, 1, :], ALU.subtract).then_inc(S["q_split"], 1)

        def take_misc_of(pe):
            last_reader = []

            def take_misc(name, count):
                if last_reader:
                    pe.wait_ge(S[last_reader[-1][0]], last_reader[-1][1])
                last_reader.append((name, count))
            return take_misc

        CONSTS = [(ident, consts["ident"]), (pick, consts["pick"])] + ([(shiftsel_f, consts["shiftsel"])] if clip else [])
        SETUP = len(wsb) + len(cols) + len(rows)
        ALL = list(PREPARE)
        for j in range(MASKS):
            ALL.insert(2 + 3 * j, ("mask", j))
        with nc.Block() as block:
            @block.sync
            def _(sp):
                for stage in ALL:
                    if stage == "proj_q":
                        sp.wait_ge(S["filled"], 1)
                    elif stage == "k_low":
                        sp.wait_ge(S["filled"], 2)
                    prepare_sp(sp, stage, 0, 0, 0)
                    if stage != "load":
                        continue
                    for dst, src in CONSTS:
                        sp.dma_start(dst[:, :], src).then_inc(S["consts_in"], 16)
                    for k in wsb:
                        sp.dma_start(wsb[k][:, :], w[k]).then_inc(S["setup"], 16)
                    for k in cols:
                        sp.dma_start(cols[k][:, :], w[k].rearrange("(p o) -> p o", o=1)).then_inc(S["setup"], 16)
                    for k in rows:
                        sp.dma_start(rows[k][:, :], w[k].rearrange("(o n) -> o n", o=1).broadcast_to([P, P])).then_inc(S["setup"], 16)
                sp.wait_ge(S["qs_in"], 16 * 12)
                sp.wait_ge(S["ks_in"], 16 * 12)

            @block.gpsimd
            def _(pool):
                for i in range(2):
                    pool.memset(QS[i][:, :, :, :].rearrange("p a b q -> p (a b q)").bitcast(F32), 0.0).then_inc(S["filled"], 1)
                    pool.memset(KS_flat[i][:, :].bitcast(F32), 0.0 if clip else TWO_ONES).then_inc(S["filled"], 1)
                    pool.memset(V[i][:, :, :, :], 1.0).then_inc(S["filled"], 1)

            @block.scalar
            def _(act):
                act.wait_ge(S["setup"], 16 * SETUP)
                for stage in ALL:
                    if stage == ("proj_v", 0):
                        act.wait_ge(S["filled"], 3)
                    prepare_act(act, stage, 0, 0)

            @block.tensor
            def _(pe):
                take_misc = take_misc_of(pe)
                pe.wait_ge(S["consts_in"], 16 * len(CONSTS))
                pe.wait_ge(S["setup"], 16 * SETUP)
                for stage in ALL:
                    prepare_pe(pe, take_misc, stage, 0)

            @block.vector
            def _(dve):
                chain = Chain(dve, S["chain_v"])
                dve.memset(O[:, :], 0.0)
                for stage in ALL:
                    if stage[0] == "mask":
                        prepare_mask(dve, stage, 0, 0, 0)
                    elif stage in ("k_rest", "k_low"):
                        prepare_keys(dve, stage, 0)
                    else:
                        prepare_dve(dve, chain, stage, 0)
                    if stage == "norm":
                        dve.wait_ge(S["consts_in"], 16 * len(CONSTS))
                        dve.tensor_copy(identb[:, :], ident[:, :])
                        if clip:
                            dve.tensor_copy(shiftsel[:, :], shiftsel_f[:, :])
                        dve.wait_ge(S["setup"], 16 * SETUP)
        ph.barrier()

        def item(i):
            g, r = divmod(i, ITEMS)
            col, c = divmod(r, NC)
            return g, col, col // 2, col % 2, c

        def items_of_slot(n):
            g, kp = divmod(n, KP)
            if g + AHEAD >= GROUP * PAIRS:
                return range(0)
            a, z = ITEMS * kp // KP, ITEMS * (kp + 1) // KP
            return range((g + AHEAD) * ITEMS + a, (g + AHEAD) * ITEMS + z)

        with nc.Fori(0, LOOPS // GROUP) as it:
            def batch(r):
                return it * GROUP + (r + 1) if r + 1 < GROUP else (it * GROUP + GROUP) % LOOPS

            with nc.Block() as block:
                @block.sync
                def _(sp):
                    def load_base(bb):
                        if bb >= 2:
                            sp.wait_ge(S["y_ready"], bb - 1)
                        sp.dma_start(base[bb % 2][:, :, :], x_in[it * GROUP + bb].rearrange("(t p) c -> p t c", p=P)).then_inc(S["base_in"], 16)

                    load_base(0)
                    load_base(1)

                    def pack_maxima(g):
                        sp.wait_ge(S["mtc_done"], g + 1)
                        bb, p = divmod(g, PAIRS)
                        for par in range(2):
                            at = SHIFT + 2 * par
                            sp.dma_start(QS[bb % 2][at:at + 2, p, par, :], MT[g % 2][2 * par:2 * par + 2, :]).then_inc(m_in[p], 16)

                    def store(bb):
                        sp.wait_ge(S["y_ready"], bb + 1)
                        sp.dma_start(x_out[it * GROUP + bb].rearrange("(t p) c -> p t c", p=P), y[bb % 2][:, :, :]).then_inc(S["y_out"], 16)

                    for g in range(AHEAD - 1):
                        pack_maxima(g)
                    for n in range(GROUP * N):
                        g, kp = divmod(n, KP)
                        if kp == 0 and g + AHEAD - 1 < GROUP * PAIRS:
                            pack_maxima(g + AHEAD - 1)
                        for stage, r in plan_of(n):
                            if stage == "proj_o":
                                store(r)
                                if r + 2 < GROUP:
                                    load_base(r + 2)
                            else:
                                prepare_sp(sp, stage, r, (r + 1) % 2, batch(r))
                    store(GROUP - 1)
                    sp.wait_ge(S["y_out"], 16 * GROUP)
                    sp.wait_ge(S["qs_in"], GROUP * 16 * 12)
                    sp.wait_ge(S["ks_in"], GROUP * 16 * 12)

                @block.gpsimd
                def _(pool):
                    for n in range(GROUP * N):
                        for stage, r in plan_of(n):
                            if stage[0] == "mask":
                                prepare_mask(pool, stage, r, (r + 1) % 2, batch(r))
                            elif stage in ("k_rest", "k_low"):
                                prepare_keys(pool, stage, r)

                @block.scalar
                def _(act):
                    def copy_pair(g):
                        act.wait_ge(S["pv_done"], (g + 1) * KP)
                        if g >= 2:
                            act.wait_ge(S["fin_done"], g - 1)
                        act.copy(osb[g % 2][:, :], O[:, 0:SEQ]).then_inc(S["o_copied"], 1)

                    for n in range(GROUP * N):
                        g, kp = divmod(n, KP)
                        act.wait_ge(S["st_done"], n + 1)
                        if n >= 3:
                            act.wait_ge(S["pv_done"], n - 2)
                        tiles = min(2, KT - 2 * kp)
                        k = keys(2 * kp)
                        act.activation(PT[n % 3][0:k, 0:tiles, :], ST[n % 2][0:k, 0:tiles, :], ACT.Exp).then_inc(S["exp_done"], 1)
                        if kp == 0 and g:
                            copy_pair(g - 1)
                        for stage, r in plan_of(n - 1) if n else ():
                            prepare_act(act, stage, r, (r + 1) % 2)
                    copy_pair(GROUP * PAIRS - 1)

                @block.tensor
                def _(pe):
                    take_misc = take_misc_of(pe)

                    def sq(i):
                        g, col, qt, par, c = item(i)
                        bb, p = divmod(g, PAIRS)
                        if i >= 2:
                            pe.wait_ge(S["max_done"], i - 1)
                        if bb and i % (PAIRS * ITEMS) == 0:
                            pe.wait_ge(S["qs_in"], 16 * 12 * bb)
                            pe.wait_ge(S["ks_in"], 16 * 12 * bb)
                        pe.matmul(SQ[i % 2][:, 0:chunk(c)], QS[bb % 2][0:SHIFT, p, par, qt * P:(qt + 1) * P],
                                  KS[bb % 2][0:SHIFT, p, c * 512:c * 512 + chunk(c)], start=True, stop=True).then_inc(S["sq_done"], 1)

                    def turn_maxima(g):
                        pe.wait_ge(S["mb_ready"], g + 1)
                        take_misc("mtc_done", g + 1)
                        for qt in range(QT):
                            ins = pe.transpose(miscb[0:4, qt * P:(qt + 1) * P], MB[:, g, 2 * qt:2 * qt + 2, :].rearrange("p a b -> p (a b)"),
                                               identb[:, :])
                        ins.then_inc(S["mt_done"], 1)

                    def key_tiles(n):
                        kp = n % KP
                        return range(2 * kp, min(2 * kp + 2, KT))

                    def add_mask(n, kt, start):
                        pe.matmul(ST[n % 2][0:keys(kt), kt % 2, :], identb[0:keys(kt), 0:keys(kt)],
                                  maskk[n // N % 2][0:keys(kt), kt, :].unsqueeze(1).broadcast_to([keys(kt), 2, SEQ]),
                                  start=start, stop=False, skip_group_check=True)

                    def scores(n):
                        bb, p, kp = n // N, n // KP % PAIRS, n % KP
                        if n >= 2:
                            pe.wait_ge(S["exp_done"], n - 1)
                        if kp == 0:
                            pe.wait_ge(m_in[p], 32 * (bb + 1))
                        if n and n % N == 0 and mask is not None and not MASK_ONCE:
                            pe.wait_ge(S["mask_ready"], MASKS * bb)
                        masked = mask is not None and not clip
                        for kt in key_tiles(n):
                            if masked:
                                add_mask(n, kt, True)
                            ins = pe.matmul(ST[n % 2][0:keys(kt), kt % 2, :], KS[bb % 2][:, p, kt * P:kt * P + keys(kt)],
                                            QS[bb % 2][:, p, :, :].rearrange("p a q -> p (a q)"), start=not masked, stop=True, skip_group_check=True)
                        ins.then_inc(S["st_raw" if clip else "st_done"], 1)

                    def shift(n):
                        bb, p, kp = n // N, n // KP % PAIRS, n % KP
                        pe.wait_ge(S["clipped"], n + 1)
                        for kt in key_tiles(n):
                            ins = pe.matmul(ST[n % 2][0:keys(kt), kt % 2, :], shiftsel[:, 0:keys(kt)],
                                            QS[bb % 2][:, p, :, :].rearrange("p a q -> p (a q)"), start=False, stop=True, skip_group_check=True)
                        ins.then_inc(S["st_done"], 1)

                    def weigh(n, between=()):
                        between = list(between)
                        bb, p, kp = n // N, n // KP % PAIRS, n % KP
                        pe.wait_ge(S["exp_done"], n + 1)
                        if kp == 0 and n:
                            pe.wait_ge(S["o_copied"], n // KP)
                        if n and n % N == 0:
                            pe.wait_ge(S["v_ready"], VG * bb)
                        for kt in key_tiles(n):
                            for par in range(2):
                                at = 32 * (2 * (kt % 2) + par)
                                ins = pe.matmul(O[at:at + HD + 1, 0:SEQ], V[bb % 2][0:keys(kt), kt, 2 * p + par, :],
                                                PT[n % 3][0:keys(kt), kt % 2, par * SEQ:(par + 1) * SEQ],
                                                start=(kt < 2), stop=(kt + 2 >= KT), skip_group_check=True)
                            if kt == 2 * kp and between:
                                if keys(kt) == P and kt != LAST:
                                    sq(between.pop(0))
                        ins.then_inc(S["pv_done"], 1)
                        for i in between:
                            sq(i)

                    def gather_pair(g):
                        pe.wait_ge(S["o_copied"], g + 1)
                        take_misc("pair_done", g + 1)
                        for qt in range(QT):
                            ins = pe.matmul(misc[:, qt * 18:(qt + 1) * 18], osb[g % 2][:, qt * P:(qt + 1) * P], pick[:, :],
                                            start=(qt == 0), stop=True, skip_group_check=True)
                        ins.then_inc(S["fin_done"], 1)

                    def finish(stage, bb):
                        if stage == "turn_attn":
                            pe.wait_ge(S["attn_ready"], bb + 1)
                            take_misc("at_ready", bb + 1)
                            for t in range(QT):
                                ins = pe.transpose(misc[:, t * P:(t + 1) * P], attn[:, t, :], ident[:, :])
                            ins.then_inc(S["at_done"], 1)
                        elif stage == "proj_o":
                            pe.wait_ge(S["at_ready"], bb + 1)
                            take_misc("y_ready", bb + 1)
                            for t in range(QT):
                                ins = pe.matmul(misc[:, t * P:(t + 1) * P], attnT[:, t * P:(t + 1) * P], wsb["wo"][:, :],
                                                start=(t == 0), stop=True, skip_group_check=True)
                            ins.then_inc(S["po_done"], 1)

                    for i in range(AHEAD * ITEMS):
                        sq(i)
                    for g in range(AHEAD - 1):
                        turn_maxima(g)
                    scores(0)
                    for n in range(GROUP * N):
                        g, kp = divmod(n, KP)
                        items = items_of_slot(n)
                        if n + 1 < GROUP * N:
                            scores(n + 1)
                        if clip:
                            shift(n)
                        for i in items[:1]:
                            sq(i)
                        if n:
                            weigh(n - 1, items[1:])
                        else:
                            for i in items[1:]:
                                sq(i)
                        if kp == 0 and g + AHEAD - 1 < GROUP * PAIRS:
                            turn_maxima(g + AHEAD - 1)
                        if kp == min(1, KP - 1) and g:
                            gather_pair(g - 1)
                        for stage, r in plan_of(n):
                            if stage in FINISH:
                                finish(stage, r)
                            else:
                                prepare_pe(pe, take_misc, stage, r)
                    weigh(GROUP * N - 1)
                    gather_pair(GROUP * PAIRS - 1)
                    for stage in FINISH:
                        finish(stage, GROUP - 1)

                @block.vector
                def _(dve):
                    chain = Chain(dve, S["chain_v"])

                    def maximum(i):
                        g, col, qt, par, c = item(i)
                        dve.wait_ge(S["sq_done"], i + 1)
                        if i and i % (PAIRS * ITEMS) == 0 and mask is not None and not MASK_ONCE:
                            dve.wait_ge(S["mask_ready"], MASKS * (g // PAIRS))
                        n = chunk(c)
                        if mask is not None:
                            if i >= 2:
                                dve.wait_ge(S["max_done"], i - 1)
                            dve.tensor_tensor_reduce(out=junk[i % 2][:, 0:n], in0=SQ[i % 2][:, 0:n],
                                                     in1=maskq[g // PAIRS % 2][:, qt, c * 512:c * 512 + n],
                                                     scale=1.0, scalar=-3e38, op0=ALU.add, op1=ALU.max,
                                                     accum_out=mx[:, g, col, c:c + 1]).then_inc(S["max_done"], 1)
                        else:
                            dve.tensor_reduce(mx[:, g, col, c:c + 1], SQ[i % 2][:, 0:n], AX.X, ALU.max).then_inc(S["max_done"], 1)

                    def split_maxima(g):
                        dve.wait_ge(S["max_done"], (g + 1) * ITEMS)
                        if NC > 1:
                            chain(dve.tensor_reduce(mm[:, g, :], mx[:, g, :, :], AX.X, ALU.max))
                            m = mm
                        else:
                            m = mx[:, :, :, 0]
                        if clip:
                            chain(dve.tensor_scalar(mm[:, g, :], m[:, g, :], clip, -clip, ALU.min, ALU.max))
                            m = mm
                        chain(dve.tensor_scalar(MB[:, g, :, 0], m[:, g, :], -1.0, None, ALU.mult))
                        dve.scalar_tensor_tensor(MB[:, g, :, 1], m[:, g, :], -1.0, MB[:, g, :, 0], ALU.mult, ALU.subtract).then_inc(S["mb_ready"], 1)

                    def copy_maxima(g):
                        dve.wait_ge(S["mt_done"], g + 1)
                        if g >= 2:
                            bb, p = divmod(g - 2, PAIRS)
                            dve.wait_ge(m_in[p], 32 * (bb + 1))
                        dve.tensor_copy(MT[g % 2][:, :], miscb[0:4, 0:SEQ]).then_inc(S["mtc_done"], 1)

                    def collect_pair(g):
                        bb, p = divmod(g, PAIRS)
                        dve.wait_ge(S["fin_done"], g + 1)
                        dve.tensor_copy(oc[bb % 2][:, :, 2 * p:2 * p + 2, :],
                                        misc[:, 0:36].rearrange("p (t h d) -> p t h d", t=QT, d=HD + 1)).then_inc(S["pair_done"], 1)

                    def clip_scores(n):
                        kp = n % KP
                        dve.wait_ge(S["st_raw"], n + 1)
                        if n and n % N == 0:
                            dve.wait_ge(S["mask_ready"], MASKS * (n // N))
                        for kt in range(2 * kp, min(2 * kp + 2, KT)):
                            v = ST[n % 2][0:keys(kt), kt % 2, :].rearrange("p (a q) -> p a q", a=2)
                            bound = maskk[n // N % 2][0:keys(kt), kt, :].unsqueeze(1).broadcast_to([keys(kt), 2, SEQ])
                            ins = dve.scalar_tensor_tensor(v, v, -clip, bound, ALU.max, ALU.min)
                        ins.then_inc(S["clipped"], 1)

                    def finish(stage, bb):
                        if stage == "divide":
                            dve.wait_ge(S["pair_done"], PAIRS * (bb + 1))
                            chain(dve.reciprocal(rec[:, :, :, :], oc[bb % 2][:, :, :, HD:HD + 1]))
                            if bb:
                                dve.wait_ge(S["at_done"], bb)
                            av = attn[:, :, :].rearrange("p t (h d) -> p t h d", d=HD)
                            for t in range(QT):
                                ins = dve.tensor_tensor(av[:, t], oc[bb % 2][:, t, :, 0:HD], rec[:, t, :, :].broadcast_to([P, HEADS, HD]), ALU.mult)
                                if "bv" in w:
                                    chain(ins)
                                    ins = dve.tensor_tensor(attn[:, t, :], attn[:, t, :], rows["bv"][:, :], ALU.add)
                            ins.then_inc(S["attn_ready"], 1)
                        elif stage == "turn_attn":
                            dve.wait_ge(S["at_done"], bb + 1)
                            if bb:
                                dve.wait_ge(S["po_done"], bb)
                            dve.tensor_copy(attnT[:, :], misc[:, 0:SEQ]).then_inc(S["at_ready"], 1)
                        else:
                            dve.wait_ge(S["po_done"], bb + 1)
                            dve.wait_ge(S["base_in"], max(32, 16 * (bb + 1)))
                            if bb >= 2:
                                dve.wait_ge(S["y_out"], 16 * bb)
                            ins = dve.tensor_tensor(y[bb % 2][:, :, :], misc[:, 0:SEQ].rearrange("p (t c) -> p t c", t=QT), base[bb % 2][:, :, :], ALU.add)
                            if "bo" in w:
                                chain(ins)
                                for t in range(QT):
                                    ins = dve.tensor_tensor(y[bb % 2][:, t, :], y[bb % 2][:, t, :], rows["bo"][:, :], ALU.add)
                            ins.then_inc(S["y_ready"], 1)

                    for g in range(AHEAD):
                        for i in range(g * ITEMS, (g + 1) * ITEMS):
                            maximum(i)
                        split_maxima(g)
                    for g in range(AHEAD - 1):
                        copy_maxima(g)
                    if clip:
                        clip_scores(0)
                    for n in range(GROUP * N):
                        g, kp = divmod(n, KP)
                        if clip and n + 1 < GROUP * N:
                            clip_scores(n + 1)
                        items = items_of_slot(n)
                        for i in items[:1]:
                            maximum(i)
                        for i in items[1:]:
                            maximum(i)
                        if kp == KP - 1 and g + AHEAD < GROUP * PAIRS:
                            split_maxima(g + AHEAD)
                        if kp == 0 and g + AHEAD - 1 < GROUP * PAIRS:
                            copy_maxima(g + AHEAD - 1)
                        if kp == min(1, KP - 1) and g:
                            collect_pair(g - 1)
                        for stage, r in plan_of(n):
                            if stage in FINISH:
                                finish(stage, r)
                            else:
                                prepare_dve(dve, chain, stage, r)
                    collect_pair(GROUP * PAIRS - 1)
                    for stage in FINISH:
                        finish(stage, GROUP - 1)
            ph.barrier()


def short_attention_phase(nc, tag, x_in, x_out, w, consts, ctxT=None, ctx_rows=None, scale=1.0, self_ln=False):
    hard = ctx_rows is not None
    TA, NTOK = LOOPS * QT, LOOPS * SEQ
    CHUNKS = NTOK // 512
    CT = 512 // P
    GROUP = 4 if LOOPS % 4 == 0 else 2
    N = GROUP * PAIRS
    LEAD = PAIRS + 3
    HC = ceil(CTX, 512)
    QPROD = (0, 1, 0, 1, 2, 0)
    KPROD = (0, 0, 1, 1, 0, 2)

    with ExitStack() as ctx:
        ph = Phase(nc, ctx, tag)
        sb, ps, sem = ph.sb, ph.ps, ph.sem
        ident = sb("ident", [P, P])
        identb = sb("identb", [P, P], BF16)
        pick = sb("pick", [P, 2 * (HD + 1)])
        wsb = {k: sb("w_" + k, list(w[k].shape)) for k in ("wq", "wk", "wv", "wo", "wqn") if k in w}
        cols = {k: sb("c_" + k, [P, 1]) for k in ("bq", "bk", "lng", "lnb") if k in w}
        rows = {k: sb("r_" + k, [P, P]) for k in ("bv", "bo") if k in w}
        KS = sb("KS", [P, PAIRS, NTOK], BF16)
        QS = sb("QS", [P, PAIRS, 2, NTOK], BF16)
        V = sb("V", [P, TA, HEADS, HD + 1])
        base = sb("base", [P, TA, DIM])
        names = ("consts_in setup chain_v xs_ready xT_done xT_ready pq_done q_read q_copied q_split pk_done k_read k_split "
                 "qs_in ks_in pv_proj v_ready v_ones filled "
                 "qh_copied hs_done found idx_ready rowbase_in mem_ready memT_done memT_ready "
                 "sq_done max_done mb_ready mt_done mtc_done v_copied st_done exp_done pv_done o_copied fin_done pair_done "
                 "attn_ready at_done at_ready po_done y_ready y_out").split()
        S = {n: sem(n) for n in names}
        chunk_in = [sem(f"chunk_in{c}") for c in range(CHUNKS)]
        ctx_in = [sem(f"ctx_in{i}") for i in range(2)]
        m_in = [sem(f"m_in{r}") for r in range(GROUP)]
        mem_in = ctx.enter_context(nc.semaphore(f"{tag}_mem_in")) if hard else None

        with ExitStack() as early:
            def tmp(name, shape, dt=F32):
                return early.enter_context(nc.sbuf_tensor(f"{tag}_{name}", shape, dt))

            stats, mv = tmp("stats", [P, TA, 6]), tmp("mv", [P, TA, 2])
            rstd, var, root = (tmp(n, [P, TA, 1]) for n in ("rstd", "var", "root"))
            xs = tmp("xs", [P, TA, DIM])
            xT = tmp("xT", [P, NTOK])
            xf = tmp("xf", [P, 512])
            xr = tmp("xr", [P, 512])
            parts = tmp("parts", [P, 3, NTOK], BF16)
            if hard:
                mem = tmp("mem", [P, TA, DIM])
                qpT = tmp("qpT", [P, NTOK])
                rowbase = tmp("rowbase", [P, LOOPS])
            memT = xT

            def split(dve, chain, c, name):
                at = slice(c * 512, (c + 1) * 512)
                chain(dve.tensor_copy(parts[:, 0, at], xf[:, :]))
                chain(dve.tensor_tensor(xr[:, :], xf[:, :], parts[:, 0, at], ALU.subtract))
                chain(dve.tensor_copy(parts[:, 1, at], xr[:, :]))
                ins = dve.tensor_tensor(parts[:, 2, at], xr[:, :], parts[:, 1, at], ALU.subtract)
                chain(ins)
                dve.sem_inc(S[name], 1)

            SETUP = len(wsb) + len(cols) + len(rows)

            with ExitStack() as banks:
                turned = [banks.enter_context(nc.psum_tensor(f"{tag}_turned{c}", [P, 512], F32)) for c in range(2)]
                proj = [banks.enter_context(nc.psum_tensor(f"{tag}_proj{c}", [P, 512], F32)) for c in range(4)]
                with nc.Block() as block:
                    @block.sync
                    def _(sp):
                        flat = x_in.rearrange("b s c -> (b s) c")[0:NTOK].rearrange("(t p) c -> p t c", p=P)
                        x_dst = xs if self_ln else base
                        for c in range(CHUNKS):
                            t = slice(c * CT, (c + 1) * CT)
                            sp.dma_start(x_dst[:, t, :], flat[:, t, :]).then_inc(chunk_in[c], 16)
                        sp.dma_start(ident[:, :], consts["ident"]).then_inc(S["consts_in"], 16)
                        sp.dma_start(pick[:, :], consts["pick"]).then_inc(S["consts_in"], 16)
                        for k in wsb:
                            sp.dma_start(wsb[k][:, :], w[k]).then_inc(S["setup"], 16)
                        for k in cols:
                            sp.dma_start(cols[k][:, :], w[k].rearrange("(p o) -> p o", o=1)).then_inc(S["setup"], 16)
                        for k in rows:
                            sp.dma_start(rows[k][:, :], w[k].rearrange("(o n) -> o n", o=1).broadcast_to([P, P])).then_inc(S["setup"], 16)
                        if hard:
                            sp.dma_start(rowbase[:, :], consts["rowbase"][:, 0:LOOPS]).then_inc(S["rowbase_in"], 16)
                            sp.wait_ge(S["rowbase_in"], 16)
                        sp.wait_ge(S["q_split"], CHUNKS)
                        sp.wait_ge(S["filled"], 1)
                        for par in range(2):
                            for k, part in enumerate(QPROD):
                                at = PARTS * par + HD * k
                                sp.dma_start(QS[at:at + HD, :, par, :], parts[HALF * par:HALF * par + HALF, part, :]).then_inc(S["qs_in"], 16)
                        sp.wait_ge(S["qs_in"], 16 * 12)

                    @block.gpsimd
                    def _(pool):
                        pool.memset(QS[:, :, :, :].rearrange("p a b q -> p (a b q)").bitcast(F32), 0.0).then_inc(S["filled"], 1)
                        pool.memset(V[:, :, :, :], 1.0).then_inc(S["v_ones"], 1)
                        pool.memset(KS[:, :, :], 1.0)

                    @block.scalar
                    def _(act):
                        act.wait_ge(S["setup"], 16 * SETUP)
                        for c in range(CHUNKS):
                            at = slice(c * 512, (c + 1) * 512)
                            if hard:
                                act.wait_ge(S["pq_done"], c + 1)
                                act.copy(qpT[:, at], proj[2 + c % 2][:, :]).then_inc(S["q_copied"], 1)
                            else:
                                if c == 0:
                                    act.wait_ge(S["v_ones"], 1)
                                act.wait_ge(S["pv_proj"], c + 1)
                                act.copy(V[:, c * CT:(c + 1) * CT, :, 0:HD],
                                         proj[2 + c % 2][:, :].rearrange("p (t h d) -> p t h d", t=CT, d=HD)).then_inc(S["v_ready"], 1)

                    @block.tensor
                    def _(pe):
                        pe.wait_ge(S["consts_in"], 32)
                        pe.wait_ge(S["setup"], 16 * SETUP)

                        def turn(c):
                            pe.wait_ge(S["xs_ready"], c + 1)
                            if c >= 2:
                                pe.wait_ge(S["xT_ready"], c - 1)
                            for t in range(CT):
                                ins = pe.transpose(turned[c % 2][:, t * P:(t + 1) * P], xs[:, c * CT + t, :], ident[:, :])
                            ins.then_inc(S["xT_done"], 1)

                        turn(0)
                        for c in range(CHUNKS):
                            at = slice(c * 512, (c + 1) * 512)
                            if c + 1 < CHUNKS:
                                turn(c + 1)
                            pe.wait_ge(S["xT_ready"], c + 1)
                            if c >= 2:
                                pe.wait_ge(S["q_read"], c - 1)
                                pe.wait_ge(S["q_copied" if hard else "v_ready"], c - 1)
                            ins = pe.matmul(proj[c % 2][:, :], wsb["wq"][:, :], xT[:, at], start=True, stop=True)
                            if hard:
                                ins = pe.matmul(proj[2 + c % 2][:, :], wsb["wqn"][:, :], xT[:, at], start=True, stop=True)
                            ins.then_inc(S["pq_done"], 1)
                            if not hard:
                                for t in range(CT):
                                    ins = pe.matmul(proj[2 + c % 2][:, t * P:(t + 1) * P], xT[:, (c * CT + t) * P:(c * CT + t + 1) * P],
                                                    wsb["wv"][:, :], start=(t == 0), stop=True, skip_group_check=True)
                                ins.then_inc(S["pv_proj"], 1)

                    @block.vector
                    def _(dve):
                        chain = Chain(dve, S["chain_v"])

                        scratch = (stats, mv, rstd, var, root)
                        if self_ln:
                            normalise(dve, chain, xs, base, *scratch, arrived=chunk_in)
                        normalise(dve, chain, base, xs, *scratch, arrived=None if self_ln else chunk_in, done=S["xs_ready"])
                        dve.wait_ge(S["consts_in"], 32)
                        dve.tensor_copy(identb[:, :], ident[:, :])
                        dve.wait_ge(S["setup"], 16 * SETUP)
                        for c in range(CHUNKS):
                            at = slice(c * 512, (c + 1) * 512)
                            dve.wait_ge(S["xT_done"], c + 1)
                            if self_ln:
                                ins = dve.tensor_scalar(xT[:, at], turned[c % 2][:, :], cols["lng"][:, :], cols["lnb"][:, :], ALU.mult, ALU.add)
                            else:
                                ins = dve.tensor_copy(xT[:, at], turned[c % 2][:, :])
                            ins.then_inc(S["xT_ready"], 1)
                            dve.wait_ge(S["pq_done"], c + 1)
                            if "bq" in w:
                                ins = dve.tensor_scalar(xf[:, :], proj[c % 2][:, :], cols["bq"][:, :], scale, ALU.add, ALU.mult)
                            else:
                                ins = dve.tensor_scalar(xf[:, :], proj[c % 2][:, :], scale, None, ALU.mult)
                            ins.then_inc(S["q_read"], 1)
                            dve.wait_ge(S["q_read"], c + 1)
                            split(dve, chain, c, "q_split")
                ph.barrier()

            if hard:
                HB = GROUP
                with ExitStack() as banks:
                    srcT = [banks.enter_context(nc.sbuf_tensor(f"{tag}_srcT{i}", [P, CTX], F32)) for i in range(2)]
                    qh = [banks.enter_context(nc.sbuf_tensor(f"{tag}_qh{i}", [P, SEQ], F32)) for i in range(2)]
                    hmax = banks.enter_context(nc.sbuf_tensor(f"{tag}_hmax", [P, HB * QT, 8], F32))
                    hidx = banks.enter_context(nc.sbuf_tensor(f"{tag}_hidx", [P, HB * QT, 8], U32))
                    picked = banks.enter_context(nc.sbuf_tensor(f"{tag}_picked", [P, HB * QT, DIM], F32))
                    hs = [banks.enter_context(nc.psum_tensor(f"{tag}_hs{i}", [P, HC * 512], F32)) for i in range(2)]
                    with nc.Fori(0, LOOPS // HB) as it:
                        with nc.Block() as block:
                            @block.sync
                            def _(sp):
                                for r in range(HB):
                                    if r >= 2:
                                        sp.wait_ge(S["hs_done"], QT * (r - 1))
                                    sp.dma_start(srcT[r % 2][:, :], ctxT[it * HB + r]).then_inc(ctx_in[r % 2], 16)

                            @block.scalar
                            def _(act):
                                for r in range(HB):
                                    if r >= 2:
                                        act.wait_ge(S["hs_done"], QT * (r - 1))
                                    act.copy(qh[r % 2][:, :], qpT[:, bass.ds((it * HB + r) * SEQ, SEQ)]).then_inc(S["qh_copied"], 1)
                                act.wait_ge(S["mem_ready"], 1)
                                act.copy(mem[:, bass.ds(it * (HB * QT), HB * QT), :], picked[:, :, :])

                            @block.tensor
                            def _(pe):
                                for k in range(HB * QT):
                                    r, t = divmod(k, QT)
                                    if t == 0:
                                        pe.wait_ge(S["qh_copied"], r + 1)
                                        pe.wait_ge(ctx_in[r % 2], 16 * (r // 2 + 1))
                                    if k >= 2:
                                        pe.wait_ge(S["found"], k - 1)
                                    for c in range(HC):
                                        n = min(512, CTX - 512 * c)
                                        ins = pe.matmul(hs[k % 2][:, c * 512:c * 512 + n], qh[r % 2][:, t * P:(t + 1) * P],
                                                        srcT[r % 2][:, c * 512:c * 512 + n], start=True, stop=True)
                                    ins.then_inc(S["hs_done"], 1)

                            @block.vector
                            def _(dve):
                                chain = Chain(dve, S["chain_v"])
                                for k in range(HB * QT):
                                    r, t = divmod(k, QT)
                                    dve.wait_ge(S["hs_done"], k + 1)
                                    chain(dve.max(hmax[:, k, :], hs[k % 2][:, 0:CTX]))
                                    dve.max_index(hidx[:, k, :], hmax[:, k, :], hs[k % 2][:, 0:CTX]).then_inc(S["found"], 1)
                                    dve.wait_ge(S["found"], k + 1)
                                    dve.tensor_scalar(hidx[:, k, 0:1], hidx[:, k, 0:1], rowbase[:, bass.ds(it * HB + r, 1)], None,
                                                      ALU.add).then_inc(S["idx_ready"], 1)

                            @block.gpsimd
                            def _(pool):
                                for k in range(HB * QT):
                                    pool.wait_ge(S["idx_ready"], k + 1)
                                    pool.indirect_dma_start(picked[:, k, :], None, ctx_rows,
                                                            bass.IndirectOffsetOnAxis(ap=hidx[:, k, 0:1], axis=0)).then_inc(mem_in, 16)
                                pool.wait_ge(mem_in, (it + 1) * (16 * HB * QT))
                                pool.sem_inc(S["mem_ready"], 1)
                        ph.barrier()

            with ExitStack() as banks:
                turned = [banks.enter_context(nc.psum_tensor(f"{tag}_mturned{c}", [P, 512], F32)) for c in range(2)]
                proj = [banks.enter_context(nc.psum_tensor(f"{tag}_mproj{c}", [P, 512], F32)) for c in range(4)]
                with nc.Block() as block:
                    @block.sync
                    def _(sp):
                        sp.wait_ge(S["k_split"], CHUNKS)
                        for par in range(2):
                            for k, part in enumerate(KPROD):
                                at = PARTS * par + HD * k
                                sp.dma_start(KS[at:at + HD, :, :], parts[HALF * par:HALF * par + HALF, part, :]).then_inc(S["ks_in"], 16)
                        sp.wait_ge(S["ks_in"], 16 * 12)

                    @block.scalar
                    def _(act):
                        for c in range(CHUNKS):
                            at = slice(c * 512, (c + 1) * 512)
                            if hard:
                                act.wait_ge(S["memT_done"], c + 1)
                                act.copy(memT[:, at], turned[c % 2][:, :]).then_inc(S["memT_ready"], 1)
                                act.wait_ge(S["pv_proj"], c + 1)
                                act.copy(V[:, c * CT:(c + 1) * CT, :, 0:HD],
                                         proj[2 + c % 2][:, :].rearrange("p (t h d) -> p t h d", t=CT, d=HD)).then_inc(S["v_ready"], 1)

                    @block.tensor
                    def _(pe):
                        def turn(c):
                            if c >= 2:
                                pe.wait_ge(S["memT_ready"], c - 1)
                            for t in range(CT):
                                ins = pe.transpose(turned[c % 2][:, t * P:(t + 1) * P], mem[:, c * CT + t, :], ident[:, :])
                            ins.then_inc(S["memT_done"], 1)

                        if hard:
                            turn(0)
                        for c in range(CHUNKS):
                            at = slice(c * 512, (c + 1) * 512)
                            if hard:
                                if c + 1 < CHUNKS:
                                    turn(c + 1)
                                pe.wait_ge(S["memT_ready"], c + 1)
                            if c >= 2:
                                pe.wait_ge(S["k_read"], c - 1)
                            pe.matmul(proj[c % 2][:, :], wsb["wk"][:, :], memT[:, at], start=True, stop=True).then_inc(S["pk_done"], 1)
                            if hard:
                                if c >= 2:
                                    pe.wait_ge(S["v_ready"], c - 1)
                                for t in range(CT):
                                    ins = pe.matmul(proj[2 + c % 2][:, t * P:(t + 1) * P], memT[:, (c * CT + t) * P:(c * CT + t + 1) * P],
                                                    wsb["wv"][:, :], start=(t == 0), stop=True, skip_group_check=True)
                                ins.then_inc(S["pv_proj"], 1)

                    @block.vector
                    def _(dve):
                        chain = Chain(dve, S["chain_v"])
                        for c in range(CHUNKS):
                            dve.wait_ge(S["pk_done"], c + 1)
                            if "bk" in w:
                                ins = dve.tensor_scalar(xf[:, :], proj[c % 2][:, :], cols["bk"][:, :], None, ALU.add)
                            else:
                                ins = dve.tensor_copy(xf[:, :], proj[c % 2][:, :])
                            ins.then_inc(S["k_read"], 1)
                            dve.wait_ge(S["k_read"], c + 1)
                            split(dve, chain, c, "k_split")
                ph.barrier()

        Vb = [sb(f"Vb{i}", [P, QT, HEADS, HD + 1]) for i in range(2)]
        PT = [sb(f"PT{i}", [P, 2, 512]) for i in range(3)]
        mx = sb("mx", [P, GROUP, QT, 2, PAIRS])
        MB = sb("MB", [P, GROUP, QT, 2, 2, PAIRS], BF16)
        MT = [sb(f"MT{i}", [4 * PAIRS, SEQ], BF16) for i in range(2)]
        osb = [sb(f"osb{i}", [P, SEQ]) for i in range(2)]
        oc = [sb(f"oc{i}", [P, QT, HEADS, HD + 1]) for i in range(2)]
        rec = sb("rec", [P, QT, HEADS, 1])
        attn = sb("attn", [P, QT, DIM])
        attnT = sb("attnT", [P, SEQ])
        y = [sb(f"y{i}", [P, QT, DIM]) for i in range(2)]
        ST = [ps(f"ST{i}", [P, 2, 512]) for i in range(2)]
        SQ = [ps(f"SQ{i}", [P, 512]) for i in range(2)]
        O = ps("O", [P, 512])
        misc = ps("misc", [P, 512])
        miscb = misc[:, :].bitcast(BF16)

        with nc.Block() as block:
            @block.vector
            def _(dve):
                dve.memset(O[:, :], 0.0)
        ph.barrier()

        def turn_step(r):
            return PAIRS * (r + 1) - LEAD

        DIVIDE, TURN, PROJECT = PAIRS + 1, PAIRS + 2, PAIRS + 3
        TAIL = PROJECT - PAIRS + 1

        def finishing(n, offset):
            r, k = divmod(n - offset, PAIRS)
            return r if k == 0 and 0 <= r < GROUP else None

        with nc.Fori(0, LOOPS // GROUP) as it:
            def tokens(r, start, n):
                return bass.ds(it * (GROUP * SEQ) + (r * SEQ + start), n)

            with nc.Block() as block:
                @block.sync
                def _(sp):
                    def pack_maxima(r):
                        sp.wait_ge(S["mtc_done"], r + 1)
                        for par in range(2):
                            at = SHIFT + 2 * par
                            sp.dma_start(QS[at:at + 2, :, par, tokens(r, 0, SEQ)],
                                         MT[r % 2][2 * PAIRS * par:2 * PAIRS * (par + 1), :]).then_inc(m_in[r], 16)

                    for n in range(min(turn_step(0), 0), N + TAIL):
                        for r in range(GROUP):
                            if max(turn_step(r), -1) == n:
                                pack_maxima(r)
                        r = finishing(n, PROJECT)
                        if r is not None:
                            sp.wait_ge(S["y_ready"], r + 1)
                            sp.dma_start(x_out[it * GROUP + r].rearrange("(t p) c -> p t c", p=P), y[r % 2][:, :, :]).then_inc(S["y_out"], 16)
                    sp.wait_ge(S["y_out"], 16 * GROUP)

                @block.gpsimd
                def _(pool):
                    for r in range(GROUP):
                        if r >= 2:
                            pool.wait_ge(S["pv_done"], PAIRS * (r - 1))
                        pool.tensor_copy(Vb[r % 2][:, :, :, :], V[:, bass.ds(it * (GROUP * QT) + r * QT, QT), :, :]).then_inc(S["v_copied"], 1)

                @block.scalar
                def _(act):
                    def copy_maxima(r):
                        act.wait_ge(S["mt_done"], r + 1)
                        if r >= 2:
                            act.wait_ge(m_in[r - 2], 32)
                        act.copy(MT[r % 2][:, :], miscb[0:4 * PAIRS, 0:SEQ]).then_inc(S["mtc_done"], 1)

                    copy_maxima(0)
                    for n in range(N + 1):
                        if n < N:
                            act.wait_ge(S["st_done"], n + 1)
                            if n >= 3:
                                act.wait_ge(S["pv_done"], n - 2)
                            act.activation(PT[n % 3][:, :, :], ST[n % 2][:, :, :], ACT.Exp).then_inc(S["exp_done"], 1)
                        if n:
                            act.wait_ge(S["pv_done"], n)
                            if n >= 3:
                                act.wait_ge(S["fin_done"], n - 2)
                            act.copy(osb[(n - 1) % 2][:, :], O[:, 0:SEQ]).then_inc(S["o_copied"], 1)
                        for r in range(1, GROUP):
                            if turn_step(r) == n:
                                copy_maxima(r)

                @block.tensor
                def _(pe):
                    last_reader = []

                    def take_misc(name, count):
                        if last_reader:
                            pe.wait_ge(S[last_reader[-1][0]], last_reader[-1][1])
                        last_reader.append((name, count))

                    def sq(i, par):
                        r, p = divmod(i, PAIRS)
                        k = 2 * i + par
                        if k >= 2:
                            pe.wait_ge(S["max_done"], k - 1)
                        for qt in range(QT):
                            ins = pe.matmul(SQ[k % 2][:, qt * SEQ:(qt + 1) * SEQ], QS[0:SHIFT, p, par, tokens(r, qt * P, P)],
                                            KS[0:SHIFT, p, tokens(r, 0, SEQ)], start=(qt == 0), stop=True, skip_group_check=True)
                        ins.then_inc(S["sq_done"], 1)

                    def turn_maxima(r):
                        pe.wait_ge(S["mb_ready"], r + 1)
                        take_misc("mtc_done", r + 1)
                        for qt in range(QT):
                            ins = pe.transpose(miscb[0:4 * PAIRS, qt * P:(qt + 1) * P],
                                               MB[:, r, qt, :, :, :].rearrange("p a k h -> p (a k h)"), identb[:, :])
                        ins.then_inc(S["mt_done"], 1)

                    def scores(n):
                        r, p = divmod(n, PAIRS)
                        if p == 0:
                            pe.wait_ge(m_in[r], 32)
                        if n >= 2:
                            pe.wait_ge(S["exp_done"], n - 1)
                        for kt in range(QT):
                            ins = pe.matmul(ST[n % 2][:, kt, :], KS[:, p, tokens(r, kt * P, P)], QS[:, p, :, tokens(r, 0, SEQ)],
                                            start=True, stop=True)
                        ins.then_inc(S["st_done"], 1)

                    def weigh(n):
                        r, p = divmod(n, PAIRS)
                        if p == 0:
                            pe.wait_ge(S["v_copied"], r + 1)
                        pe.wait_ge(S["exp_done"], n + 1)
                        if n:
                            pe.wait_ge(S["o_copied"], n)
                        for kt in range(QT):
                            for par in range(2):
                                at = 32 * (2 * kt + par)
                                ins = pe.matmul(O[at:at + HD + 1, 0:SEQ], Vb[r % 2][:, kt, 2 * p + par, :],
                                                PT[n % 3][:, kt, par * SEQ:(par + 1) * SEQ], start=True, stop=True, skip_group_check=True)
                        ins.then_inc(S["pv_done"], 1)

                    def gather_pair(n):
                        pe.wait_ge(S["o_copied"], n + 1)
                        take_misc("pair_done", n + 1)
                        for qt in range(QT):
                            ins = pe.matmul(misc[:, qt * 18:(qt + 1) * 18], osb[n % 2][:, qt * P:(qt + 1) * P], pick[:, :],
                                            start=(qt == 0), stop=True, skip_group_check=True)
                        ins.then_inc(S["fin_done"], 1)

                    for i in range(LEAD):
                        for par in range(2):
                            sq(i, par)
                        if i == PAIRS - 1:
                            turn_maxima(0)
                    scores(0)
                    for n in range(N + TAIL):
                        if n + 1 < N:
                            scores(n + 1)
                        if n + LEAD < N:
                            sq(n + LEAD, 0)
                        if 1 <= n <= N:
                            weigh(n - 1)
                        if n + LEAD < N:
                            sq(n + LEAD, 1)
                        if 2 <= n <= N + 1:
                            gather_pair(n - 2)
                        for r in range(1, GROUP):
                            if turn_step(r) == n:
                                turn_maxima(r)
                        r = finishing(n, TURN)
                        if r is not None:
                            pe.wait_ge(S["attn_ready"], r + 1)
                            take_misc("at_ready", r + 1)
                            for t in range(QT):
                                ins = pe.transpose(misc[:, t * P:(t + 1) * P], attn[:, t, :], ident[:, :])
                            ins.then_inc(S["at_done"], 1)
                        r = finishing(n, PROJECT)
                        if r is not None:
                            pe.wait_ge(S["at_ready"], r + 1)
                            take_misc("y_ready", r + 1)
                            for t in range(QT):
                                ins = pe.matmul(misc[:, t * P:(t + 1) * P], attnT[:, t * P:(t + 1) * P], wsb["wo"][:, :],
                                                start=(t == 0), stop=True, skip_group_check=True)
                            ins.then_inc(S["po_done"], 1)

                @block.vector
                def _(dve):
                    chain = Chain(dve, S["chain_v"])

                    def maximum(i, par):
                        r, p = divmod(i, PAIRS)
                        k = 2 * i + par
                        dve.wait_ge(S["sq_done"], k + 1)
                        dve.tensor_reduce(mx[:, r, :, par, p], SQ[k % 2][:, :].rearrange("p (t k) -> p t k", t=QT), AX.X, ALU.max
                                          ).then_inc(S["max_done"], 1)

                    def split_maxima(r):
                        dve.wait_ge(S["max_done"], 2 * PAIRS * (r + 1))
                        for qt in range(QT):
                            ins = dve.tensor_scalar(MB[:, r, qt, :, 0, :], mx[:, r, qt, :, :], -1.0, None, ALU.mult)
                        chain(ins)
                        for qt in range(QT):
                            ins = dve.scalar_tensor_tensor(MB[:, r, qt, :, 1, :], mx[:, r, qt, :, :], -1.0, MB[:, r, qt, :, 0, :],
                                                           ALU.mult, ALU.subtract)
                        ins.then_inc(S["mb_ready"], 1)

                    for i in range(LEAD):
                        for par in range(2):
                            maximum(i, par)
                        if i == PAIRS - 1:
                            split_maxima(0)
                    for n in range(N + TAIL):
                        if n + LEAD < N:
                            for par in range(2):
                                maximum(n + LEAD, par)
                        for r in range(1, GROUP):
                            if turn_step(r) == n + 1:
                                split_maxima(r)
                        if 2 <= n <= N + 1:
                            g = n - 2
                            r, p = divmod(g, PAIRS)
                            dve.wait_ge(S["fin_done"], g + 1)
                            dve.tensor_copy(oc[r % 2][:, :, 2 * p:2 * p + 2, :],
                                            misc[:, 0:36].rearrange("p (t h d) -> p t h d", t=QT, d=HD + 1)).then_inc(S["pair_done"], 1)
                        r = finishing(n, DIVIDE)
                        if r is not None:
                            dve.wait_ge(S["pair_done"], PAIRS * (r + 1))
                            chain(dve.reciprocal(rec[:, :, :, :], oc[r % 2][:, :, :, HD:HD + 1]))
                            if r:
                                dve.wait_ge(S["at_done"], r)
                            av = attn[:, :, :].rearrange("p t (h d) -> p t h d", d=HD)
                            for t in range(QT):
                                ins = dve.tensor_tensor(av[:, t], oc[r % 2][:, t, :, 0:HD], rec[:, t, :, :].broadcast_to([P, HEADS, HD]), ALU.mult)
                                if "bv" in w:
                                    chain(ins)
                                    ins = dve.tensor_tensor(attn[:, t, :], attn[:, t, :], rows["bv"][:, :], ALU.add)
                            ins.then_inc(S["attn_ready"], 1)
                        r = finishing(n, TURN)
                        if r is not None:
                            dve.wait_ge(S["at_done"], r + 1)
                            if r:
                                dve.wait_ge(S["po_done"], r)
                            dve.tensor_copy(attnT[:, :], misc[:, 0:SEQ]).then_inc(S["at_ready"], 1)
                        r = finishing(n, PROJECT)
                        if r is not None:
                            dve.wait_ge(S["po_done"], r + 1)
                            if r >= 2:
                                dve.wait_ge(S["y_out"], 16 * r)
                            ins = dve.tensor_tensor(y[r % 2][:, :, :], misc[:, 0:SEQ].rearrange("p (t c) -> p t c", t=QT),
                                                    base[:, bass.ds(it * (GROUP * QT) + r * QT, QT), :], ALU.add)
                            if "bo" in w:
                                chain(ins)
                                for t in range(QT):
                                    ins = dve.tensor_tensor(y[r % 2][:, t, :], y[r % 2][:, t, :], rows["bo"][:, :], ALU.add)
                            ins.then_inc(S["y_ready"], 1)
            ph.barrier()


def top_k(dve, chain, values, k, tri, greater, equal, rank, chosen):
    _, T, E = values.shape
    a = values.unsqueeze(3).broadcast_to([P, T, E, E])
    b = values.unsqueeze(2).broadcast_to([P, T, E, E])
    dve.tensor_tensor(greater, a, b, ALU.is_gt)
    chain(dve.tensor_tensor(equal, a, b, ALU.is_equal))
    chain(dve.tensor_tensor(equal, equal, tri.unsqueeze(1).broadcast_to([P, T, E, E]), ALU.mult))
    chain(dve.tensor_tensor(greater, greater, equal, ALU.add))
    chain(dve.tensor_reduce(rank, greater.rearrange("p t a b -> p t b a"), AX.X, ALU.add))
    chain(dve.tensor_scalar(chosen, rank, float(k), None, ALU.is_lt))


def experts_phase(nc, tag, kind, x_in, x_out, w, consts, extra=None):
    E, TT, D = 8, 4, DIM
    TOK = TT * P
    FT = 3 if kind == "silu" else 4
    FP = 114 if kind == "silu" else P
    STEPS = E * FT
    CHUNKS = LOOPS * SEQ // TOK
    TA = CHUNKS * TT
    two = kind != "relu"
    EARLY = {"relu": 6, "silu": 3, "clip": 5}[kind]

    with ExitStack() as ctx:
        ph = Phase(nc, ctx, tag)
        sb, ps, sem = ph.sb, ph.ps, ph.sem
        ident = sb("ident", [P, P])
        tri = sb("tri", [P, E, E])
        onehot = sb("onehot", [E, E, P])
        W1 = sb("W1", [P, E, FT * FP])
        Wg = sb("Wg", [P, E, FT * FP]) if two else None
        W2 = sb("W2", [FP, E, FT, D])
        b1 = sb("b1", [FP, STEPS])
        bg = sb("bg", [FP, STEPS]) if two else None
        b2 = sb("b2", [E, D]) if kind != "clip" else None
        bo = sb("bo", [P, E]) if kind == "clip" else None
        eg = sb("eg", [P, E]) if kind == "clip" else None
        eb = sb("eb", [P, E]) if kind == "clip" else None
        gw = sb("gw", [P, E])
        gb = sb("gb", [P, E]) if kind == "relu" else None
        lng = sb("lng", [P, D]) if kind == "clip" else (sb("lng", [P, 1]) if kind == "relu" else None)
        lnb = sb("lnb", [P, D]) if kind == "clip" else (sb("lnb", [P, 1]) if kind == "relu" else None)
        ones = sb("ones", [P, P]) if kind == "silu" else None
        csq = sb("csq", [P, E]) if kind == "silu" else None
        x_sb = sb("x_sb", [P, TA, D])
        r_sb = sb("r_sb", [P, TA, D]) if kind == "relu" else None
        stats = sb("stats", [P, TA, 6])
        mv = sb("mv", [P, TA, 2])
        rstd = sb("rstd", [P, TA, 1])
        var = sb("var", [P, TA, 1])
        root = sb("root", [P, TA, 1])
        xn = sb("xn", [P, TA, D])
        xm = sb("xm", [P, TA, D]) if kind == "clip" else None
        xT = sb("xT", [P, TA * P])
        cT = sb("cT", [P, TA * P]) if kind == "clip" else None
        eT = [sb(f"eT{i}", [P, TOK]) for i in range(2)] if kind == "clip" else None
        sq = sb("sq", [P, TA, D]) if kind == "silu" else None
        nrm = sb("nrm", [P, TA, 1])
        L = sb("L", [P, TA, E])
        d2 = sb("d2", [P, TA, E])
        t8 = sb("t8", [P, TA, E])
        greater = sb("greater", [P, TT, E, E])
        equal = sb("equal", [P, TT, E, E])
        rank = sb("rank", [P, TA, E])
        chosen = sb("chosen", [P, TA, E])
        top = sb("top", [P, TA, 1])
        total = sb("total", [P, TA, 1])
        gates = sb("gates", [P, TA, E])
        gT = sb("gT", [E, TA * P])
        gB = [sb(f"gB{i}", [P, TOK]) for i in range(2)]
        A = [sb(f"A{i}", [FP, TOK]) for i in range(3)]
        C = [sb(f"C{i}", [FP, TOK]) for i in range(3)] if kind == "clip" else None
        T = [sb(f"T{i}", [FP, TOK]) for i in range(3)] if two else None
        Hg = [sb(f"Hg{i}", [FP, TOK]) for i in range(3)]
        yo = sb("yo", [P, TOK]) if kind == "clip" else None
        yg = sb("yg", [P, TOK]) if kind == "clip" else None
        yT = sb("yT", [P, TOK])
        out = sb("out", [P, TT, D])
        up1 = [ps(f"up1_{i}", [P, TOK]) for i in range(2)]
        upg = [ps(f"upg_{i}", [P, TOK]) for i in range(2)]
        Y = [ps(f"Y{i}", [P, TOK]) for i in range(2)]
        GB = ps("GB", [P, TOK])
        misc = ps("misc", [P, TOK])
        first = [misc, GB] + Y
        second = up1 + upg

        names = ("setup consts_in chain_v xn_ready xm_ready xT_done cT_done xT_ready logits_done shifted gate_exp gates_ready gT_done "
                 "gb_done gb_ready e_ready upg_done up_done pre_done clipped act_done prod_done gated down_done y_taken acc_step yT_ready "
                 "out_done out_ready out_sent").split()
        S = {n: sem(n) for n in names}
        x_in_sem = [sem(f"x_in{c}") for c in range(CHUNKS)]

        rows = x_in.rearrange("b s c -> (b s) c")[0:TA * P].rearrange("(t p) c -> p t c", p=P)
        with nc.Block() as block:
            @block.sync
            def _(sp):
                if kind == "relu":
                    more = extra.rearrange("b s c -> (b s) c")[0:TA * P].rearrange("(t p) c -> p t c", p=P)
                for c in range(CHUNKS):
                    tiles = slice(c * TT, (c + 1) * TT)
                    if kind == "relu":
                        sp.dma_start(r_sb[:, tiles, :], more[:, tiles, :]).then_inc(x_in_sem[c], 16)
                    else:
                        sp.dma_start(x_sb[:, tiles, :], rows[:, tiles, :]).then_inc(x_in_sem[c], 16)
                early = [(ident[:, :], consts["ident"]), (tri[:, :, :], consts["tri8"]), (gw[:, :], w["gw"])]
                loads = [(onehot[:, :, :], consts["onehot"]),
                         (W1[:, :, :], w["W1"]), (W2[:, :, :, :], w["W2"]), (b1[:, :], w["b1"])]
                if two:
                    loads += [(Wg[:, :, :], w["Wg"]), (bg[:, :], w["bg"])]
                if kind == "clip":
                    loads += [(bo[:, :], w["bo"]), (eg[:, :], w["eg"]), (eb[:, :], w["eb"])]
                    early += [(t[:, :], w[n].rearrange("(o n) -> o n", o=1).broadcast_to([P, D])) for t, n in ((lng, "lng"), (lnb, "lnb"))]
                else:
                    loads += [(b2[:, :], w["b2"])]
                if kind == "relu":
                    early += [(t[:, :], w[n].rearrange("(p o) -> p o", o=1)) for t, n in ((lng, "lng"), (lnb, "lnb"))]
                    early += [(gb[:, :], w["gb"].rearrange("(o n) -> o n", o=1).broadcast_to([P, E]))]
                for dst, src in early:
                    sp.dma_start(dst, src).then_inc(S["consts_in"], 16)
                if kind == "relu":
                    loads += [(x_sb[:, :, :], rows)]
                for dst, src in loads:
                    sp.dma_start(dst, src).then_inc(S["setup"], 16)
                sp.wait_ge(S["setup"], 16 * len(loads))

            @block.scalar
            def _(act):
                act.wait_ge(S["shifted"], 1)
                act.activation(t8[:, :, :], L[:, :, :], ACT.Exp).then_inc(S["gate_exp"], 1)

            @block.tensor
            def _(pe):
                pe.wait_ge(S["consts_in"], 16 * EARLY)
                for c in range(CHUNKS):
                    pe.wait_ge(S["xn_ready"], c + 1)
                    for t in range(TT):
                        ins = pe.transpose(first[c][:, t * P:(t + 1) * P], xn[:, c * TT + t, :], ident[:, :])
                    ins.then_inc(S["xT_done"], 1)
                    if kind == "clip":
                        pe.wait_ge(S["xm_ready"], c + 1)
                        for t in range(TT):
                            ins = pe.transpose(second[c][:, t * P:(t + 1) * P], xm[:, c * TT + t, :], ident[:, :])
                        ins.then_inc(S["cT_done"], 1)
                pe.wait_ge(S["xT_ready"], CHUNKS)
                for t in range(TA):
                    o = misc[:, t * E:(t + 1) * E]
                    if kind == "silu":
                        pe.matmul(o, ones[:, :], csq[:, :], start=(t == 0), stop=False, skip_group_check=True)
                    ins = pe.matmul(o, xT[:, t * P:(t + 1) * P], gw[:, :], start=(t == 0 and kind != "silu"), stop=True, skip_group_check=True)
                ins.then_inc(S["logits_done"], 1)
                pe.wait_ge(S["gates_ready"], 1)
                for t in range(TA):
                    ins = pe.transpose(first[t // TT][0:E, t % TT * P:(t % TT + 1) * P], gates[:, t, :], ident[:, :])
                ins.then_inc(S["gT_done"], 1)

            @block.vector
            def _(dve):
                chain = Chain(dve, S["chain_v"])

                if kind == "silu":
                    dve.memset(ones[:, :], 1.0)
                    dve.wait_ge(S["consts_in"], 16 * EARLY)
                    chain(dve.tensor_tensor(csq[:, :], gw[:, :], gw[:, :], ALU.mult))
                    chain(dve.tensor_scalar(gw[:, :], gw[:, :], -2.0, None, ALU.mult))
                if kind == "clip":
                    dve.wait_ge(S["consts_in"], 16 * EARLY)
                scratch = (stats, mv, rstd, var, root)
                if kind == "clip":
                    normalise(dve, chain, x_sb, xn, *scratch, arrived=x_in_sem)
                    normalise(dve, chain, xn, xm, *scratch)
                    chain(dve.tensor_tensor(xn[:, :, :], xm[:, :, :], lng[:, :].unsqueeze(1).broadcast_to([P, TA, D]), ALU.mult))
                    ins = dve.tensor_tensor(xn[:, :, :], xn[:, :, :], lnb[:, :].unsqueeze(1).broadcast_to([P, TA, D]), ALU.add)
                    chain(ins)
                    dve.sem_inc(S["xn_ready"], CHUNKS)
                    normalise(dve, chain, xn, xm, *scratch, done=S["xm_ready"])
                else:
                    normalise(dve, chain, r_sb if kind == "relu" else x_sb, xn, *scratch, arrived=x_in_sem, done=S["xn_ready"])
                if kind == "relu":
                    dve.wait_ge(S["consts_in"], 16 * EARLY)
                for c in range(CHUNKS):
                    cols = slice(c * TOK, (c + 1) * TOK)
                    dve.wait_ge(S["xT_done"], c + 1)
                    if kind == "relu":
                        dve.tensor_scalar(xT[:, cols], first[c][:, :], lng[:, :], lnb[:, :], ALU.mult, ALU.add).then_inc(S["xT_ready"], 1)
                    else:
                        dve.tensor_copy(xT[:, cols], first[c][:, :]).then_inc(S["xT_ready"], 1)
                    if kind == "clip":
                        dve.wait_ge(S["cT_done"], c + 1)
                        dve.tensor_copy(cT[:, cols], second[c][:, :])
                if kind == "silu":
                    chain(dve.tensor_tensor(sq[:, :, :], xn[:, :, :], xn[:, :, :], ALU.mult))
                    chain(dve.tensor_reduce(nrm[:, :, :], sq[:, :, :], AX.X, ALU.add))
                dve.wait_ge(S["logits_done"], 1)
                raw = misc[:, 0:TA * E].rearrange("p (t e) -> p t e", e=E)
                if kind == "relu":
                    chain(dve.tensor_tensor(L[:, :, :], raw, gb[:, :].unsqueeze(1).broadcast_to([P, TA, E]), ALU.add))
                elif kind == "clip":
                    chain(dve.tensor_copy(L[:, :, :], raw))
                else:
                    chain(dve.tensor_tensor(d2[:, :, :], raw, nrm[:, :, :].broadcast_to([P, TA, E]), ALU.add))
                    chain(dve.tensor_scalar(d2[:, :, :], d2[:, :, :], 1e-12, None, ALU.max))
                    inverse_root(dve, chain, L[:, :, :], d2[:, :, :], rank, t8, eps=0.0)
                    chain(dve.tensor_tensor(L[:, :, :], L[:, :, :], d2[:, :, :], ALU.mult))
                for c in range(CHUNKS):
                    whole = slice(c * TT, (c + 1) * TT)
                    top_k(dve, chain, L[:, whole, :], 2, tri[:, :, :], greater[:, :, :, :], equal[:, :, :, :], rank[:, whole, :], chosen[:, whole, :])
                chain(dve.tensor_reduce(top[:, :, :], L[:, :, :], AX.X, ALU.max))
                dve.tensor_tensor(L[:, :, :], L[:, :, :], top[:, :, :].broadcast_to([P, TA, E]), ALU.subtract).then_inc(S["shifted"], 1)
                dve.wait_ge(S["gate_exp"], 1)
                chain(dve.tensor_tensor(t8[:, :, :], t8[:, :, :], chosen[:, :, :], ALU.mult))
                chain(dve.tensor_reduce(total[:, :, :], t8[:, :, :], AX.X, ALU.add))
                chain(dve.reciprocal(total[:, :, :], total[:, :, :]))
                dve.tensor_tensor(gates[:, :, :], t8[:, :, :], total[:, :, :].broadcast_to([P, TA, E]), ALU.mult).then_inc(S["gates_ready"], 1)
                dve.wait_ge(S["gT_done"], 1)
                for c in range(CHUNKS):
                    dve.tensor_copy(gT[:, c * TOK:(c + 1) * TOK], first[c][0:E, :])
        ph.barrier()

        with nc.Fori(0, CHUNKS) as i:
            rows_out = x_out.rearrange("b s c -> (b s) c").rearrange("(n t p) c -> n p t c", t=TT, p=P)
            now = bass.ds(i * TOK, TOK)
            with nc.Block() as block:
                @block.sync
                def _(sp):
                    sp.wait_ge(S["out_ready"], 1)
                    sp.dma_start(rows_out[i], out[:, :, :]).then_inc(S["out_sent"], 16)
                    sp.wait_ge(S["out_sent"], 16)

                @block.gpsimd
                def _(pool):
                    if kind == "silu":
                        for s in range(STEPS):
                            pool.wait_ge(S["prod_done"], s + 1)
                            if s >= 3:
                                pool.wait_ge(S["down_done"], s - 2)
                            if s % FT == 0:
                                pool.wait_ge(S["gb_ready"], s // FT + 1)
                            pool.tensor_tensor(Hg[s % 3][:, :], T[s % 3][:, :], gB[s // FT % 2][0:FP, :], ALU.mult).then_inc(S["gated"], 1)

                @block.scalar
                def _(act):
                    def pre(s):
                        act.wait_ge(S["upg_done"], s + 1)
                        if s >= 3:
                            act.wait_ge(S["act_done"], s - 2)
                        act.activation(C[s % 3][:, :], upg[s % 2][:, :], ACT.Identity, bias=bg[:, s:s + 1]).then_inc(S["pre_done"], 1)

                    if kind == "clip":
                        pre(0)
                    for s in range(STEPS):
                        if kind == "clip":
                            if s + 1 < STEPS:
                                pre(s + 1)
                            act.wait_ge(S["clipped"], s + 1)
                            src, bias = C[s % 3][:, :], 0.0
                        else:
                            act.wait_ge(S["upg_done" if two else "up_done"], s + 1)
                            src = (upg if two else up1)[s % 2][0:FP, :]
                            bias = (bg if two else b1)[:, s:s + 1]
                        if s >= 3:
                            act.wait_ge(S["prod_done" if two else "gated"], s - 2)
                        act.activation(A[s % 3][:, :], src, ACT.Silu if two else ACT.Relu, bias=bias).then_inc(S["act_done"], 1)

                @block.tensor
                def _(pe):
                    def spread(e):
                        if e:
                            pe.wait_ge(S["gb_ready"], e)
                        pe.matmul(GB[:, :], onehot[:, e, :], gT[:, now], start=True, stop=True).then_inc(S["gb_done"], 1)

                    def up(s):
                        e, f = divmod(s, FT)
                        if kind == "clip" and f == 0:
                            pe.wait_ge(S["e_ready"], e + 1)
                        if s >= 2:
                            if two:
                                pe.wait_ge(S["pre_done" if kind == "clip" else "act_done"], s - 1)
                            else:
                                pe.wait_ge(S["act_done"], s - 1)
                        x = eT[e % 2][:, :] if kind == "clip" else xT[:, now]
                        if two:
                            pe.matmul(upg[s % 2][0:FP, :], Wg[:, e, f * FP:(f + 1) * FP], x, start=True, stop=True).then_inc(S["upg_done"], 1)
                            if s >= 2:
                                pe.wait_ge(S["prod_done"], s - 1)
                        pe.matmul(up1[s % 2][0:FP, :], W1[:, e, f * FP:(f + 1) * FP], x, start=True, stop=True).then_inc(S["up_done"], 1)

                    def down(s):
                        e, f = divmod(s, FT)
                        pe.wait_ge(S["gated"], s + 1)
                        if kind == "clip":
                            if f == 0 and e >= 2:
                                pe.wait_ge(S["y_taken"], e - 1)
                            pe.matmul(Y[e % 2][:, :], W2[:, e, f, :], Hg[s % 3][:, :], start=(f == 0), stop=(f == FT - 1)).then_inc(S["down_done"], 1)
                        else:
                            pe.matmul(Y[0][:, :], W2[:, e, f, :], Hg[s % 3][:, :], start=False, stop=(s == STEPS - 1)).then_inc(S["down_done"], 1)

                    spread(0)
                    up(0)
                    up(1)
                    if kind != "clip":
                        pe.matmul(Y[0][:, :], b2[:, :], gT[:, now], start=True, stop=False)
                    for s in range(STEPS):
                        if s % FT == FT - 2 and s // FT + 1 < E:
                            spread(s // FT + 1)
                        if s + 2 < STEPS:
                            up(s + 2)
                        down(s)
                    pe.wait_ge(S["yT_ready"], 1)
                    for t in range(TT):
                        ins = pe.transpose(misc[:, t * P:(t + 1) * P], yT[:, t * P:(t + 1) * P], ident[:, :])
                    ins.then_inc(S["out_done"], 1)

                @block.vector
                def _(dve):
                    chain = Chain(dve, S["chain_v"])

                    def take_gate(e):
                        dve.wait_ge(S["gb_done"], e + 1)
                        if kind == "silu" and e >= 2:
                            dve.wait_ge(S["gated"], (e - 1) * FT)
                        dve.tensor_copy(gB[e % 2][:, :], GB[:, :]).then_inc(S["gb_ready"], 1)

                    def expert_input(e):
                        if e >= 2:
                            dve.wait_ge(S["up_done"], (e - 1) * FT)
                        dve.tensor_scalar(eT[e % 2][:, :], cT[:, now], eg[:, e:e + 1], eb[:, e:e + 1], ALU.mult, ALU.add).then_inc(S["e_ready"], 1)

                    def clip_gate(s):
                        dve.wait_ge(S["pre_done"], s + 1)
                        dve.tensor_scalar(C[s % 3][:, :], C[s % 3][:, :], 20.0, -20.0, ALU.min, ALU.max).then_inc(S["clipped"], 1)

                    if kind == "clip":
                        expert_input(0)
                        dve.memset(yT[:, :], 0.0).then_inc(S["acc_step"], 1)
                        clip_gate(0)
                    for s in range(STEPS):
                        e, f = divmod(s, FT)
                        if f == 0:
                            take_gate(e)
                            if kind == "clip" and e + 1 < E:
                                expert_input(e + 1)
                        if kind == "relu":
                            if f == 0:
                                dve.wait_ge(S["gb_ready"], e + 1)
                            dve.wait_ge(S["act_done"], s + 1)
                            if s >= 3:
                                dve.wait_ge(S["down_done"], s - 2)
                            dve.tensor_tensor(Hg[s % 3][:, :], A[s % 3][:, :], gB[e % 2][:, :], ALU.mult).then_inc(S["gated"], 1)
                            continue
                        if kind == "clip" and s + 1 < STEPS:
                            clip_gate(s + 1)
                        dve.wait_ge(S["act_done"], s + 1)
                        dve.wait_ge(S["up_done"], s + 1)
                        if s >= 3:
                            dve.wait_ge(S["gated"], s - 2)
                        dve.scalar_tensor_tensor(T[s % 3][:, :], up1[s % 2][0:FP, :], b1[:, s:s + 1], A[s % 3][:, :], ALU.add, ALU.mult
                                                 ).then_inc(S["prod_done"], 1)
                        if kind == "silu":
                            continue
                        dve.wait_ge(S["prod_done"], s + 1)
                        if s >= 3:
                            dve.wait_ge(S["down_done"], s - 2)
                        dve.tensor_scalar(Hg[s % 3][:, :], T[s % 3][:, :], 1e4, -1e4, ALU.min, ALU.max).then_inc(S["gated"], 1)
                        if f == 2 and e or s == STEPS - 1:
                            for k in ([e - 1] if s < STEPS - 1 else [e]):
                                dve.wait_ge(S["down_done"], (k + 1) * FT)
                                dve.tensor_scalar(yo[:, :], Y[k % 2][:, :], bo[:, k:k + 1], 1e4, ALU.add, ALU.min).then_inc(S["y_taken"], 1)
                                dve.wait_ge(S["y_taken"], k + 1)
                                dve.wait_ge(S["gb_ready"], k + 1)
                                chain(dve.scalar_tensor_tensor(yg[:, :], yo[:, :], -1e4, gB[k % 2][:, :], ALU.max, ALU.mult))
                                ins = dve.tensor_tensor(yT[:, :], yT[:, :], yg[:, :], ALU.add)
                                if k == E - 1:
                                    ins.then_inc(S["yT_ready"], 1)
                                else:
                                    chain(ins)
                    if kind != "clip":
                        dve.wait_ge(S["down_done"], STEPS)
                        dve.tensor_copy(yT[:, :], Y[0][:, :]).then_inc(S["yT_ready"], 1)
                    dve.wait_ge(S["out_done"], 1)
                    these = bass.ds(i * TT, TT)
                    ins = dve.tensor_tensor(out[:, :, :], misc[:, :].rearrange("p (t c) -> p t c", t=TT), x_sb[:, these, :], ALU.add)
                    if kind == "relu":
                        chain(ins)
                        ins = dve.tensor_tensor(out[:, :, :], out[:, :, :], r_sb[:, these, :], ALU.add)
                    ins.then_inc(S["out_ready"], 1)
            ph.barrier()


def switch_phase(nc, tag, x_in, x_out, w, consts):
    H, E, K, DH = 8, 5, 3, 64
    HD_ALL = H * DH
    ZT_TILES = ceil(E * DH, P)
    TA = LOOPS * QT
    CT = 4
    CHUNKS = TA // CT
    GROUP = 4 if LOOPS % 4 == 0 else 2
    GT = 2 * H
    USES = [(j, e, t) for j in range(3) for e in range(E) for t in range(QT)]

    with ExitStack() as ctx:
        ph = Phase(nc, ctx, tag)
        sb, ps, sem = ph.sb, ph.ps, ph.sem
        ident = sb("ident", [P, P])
        tri = sb("tri", [P, E, E])
        W = sb("W", [P, 3, E, HD_ALL])
        Wr = sb("Wr", [P, 2, H * E])
        Wo = sb("Wo", [P, ZT_TILES, DIM])
        x_sb = sb("x_sb", [P, TA, DIM])
        stats = sb("stats", [P, TA, 6])
        mv = sb("mv", [P, TA, 2])
        rstd = sb("rstd", [P, TA, 1])
        var = sb("var", [P, TA, 1])
        root = sb("root", [P, TA, 1])
        xn = sb("xn", [P, TA, DIM])
        xT = sb("xT", [P, TA * P])
        xb = [sb(f"xb{i}", [P, SEQ]) for i in range(2)]
        sig = sb("sig", [P, TA * GT, E])
        greater = sb("greater", [P, CT * GT, E, E])
        equal = sb("equal", [P, CT * GT, E, E])
        rank = sb("rank", [P, CT * GT, E])
        chosen = sb("chosen", [P, TA * GT, E])
        gate = sb("gate", [P, TA * GT, E])
        prod = [sb(f"prod{i}", [P, HD_ALL]) for i in range(3)]
        acc = sb("acc", [P, 3, QT, HD_ALL])
        qT = sb("qT", [P, H // 2, SEQ])
        kT = sb("kT", [P, H // 2, SEQ])
        mx = sb("mx", [P, H, QT])
        sums = sb("sums", [P, QT, H])
        rec = sb("rec", [P, QT, H])
        pr = [sb(f"pr{i}", [P, QT, SEQ]) for i in range(3)]
        pT = [sb(f"pT{i}", [P, QT, SEQ]) for i in range(3)]
        pick = sb("pick", [P, QT, H, E])
        zp = [sb(f"zp{i}", [P, QT, E, DH]) for i in range(2)]
        Z = sb("Z", [P, QT, E, DH])
        ZT = sb("ZT", [P, QT, ZT_TILES, P])
        out = [sb(f"out{i}", [P, QT, DIM]) for i in range(2)]
        bank = [ps(f"bank{i}", [P, 512]) for i in range(8)]

        names = ("setup consts_in chain_v xn_ready xT_done xT_ready logits_done sig_exp proj_done prod_done acc_done "
                 "qk_done qk_ready s_done max_ready exp_done pt_done pt_ready pv_done zp_done z_added z_ready xb_ready zt_done zt_ready out_done "
                 "out_ready out_sent").split()
        S = {n: sem(n) for n in names}
        chunk_in = [sem(f"chunk_in{c}") for c in range(CHUNKS)]

        with nc.Block() as block:
            @block.sync
            def _(sp):
                flat = x_in.rearrange("b s c -> (b s) c")[0:TA * P].rearrange("(t p) c -> p t c", p=P)
                for c in range(CHUNKS):
                    sp.dma_start(x_sb[:, c * CT:(c + 1) * CT, :], flat[:, c * CT:(c + 1) * CT, :]).then_inc(chunk_in[c], 16)
                for dst, src in ((ident[:, :], consts["ident"]), (tri[:, :, :], consts["tri5"]), (Wr[:, :, :], w["Wr"])):
                    sp.dma_start(dst, src).then_inc(S["consts_in"], 16)
                loads = [(W[:, j, :, :], w["W"][:, j]) for j in range(3)]
                loads += [(Wo[:, 0:2, :], w["Wo"][0:2 * P].rearrange("(t p) n -> p t n", p=P)), (Wo[0:DH, 2, :], w["Wo"][2 * P:])]
                for dst, src in loads:
                    sp.dma_start(dst, src).then_inc(S["setup"], 16)
                sp.wait_ge(S["setup"], 16 * len(loads))

            @block.scalar
            def _(act):
                for c in range(CHUNKS):
                    act.wait_ge(S["logits_done"], c + 1)
                    for half in range(2):
                        at = (2 * c + half) * 2 * GT
                        ins = act.activation(sig[:, at:at + 2 * GT, :], bank[4 + (2 * c + half) % 4][:, 0:2 * GT * E].rearrange("p (g e) -> p g e", e=E),
                                             ACT.Exp, scale=-1.0)
                    ins.then_inc(S["sig_exp"], 1)

            @block.tensor
            def _(pe):
                pe.wait_ge(S["consts_in"], 48)
                for c in range(CHUNKS):
                    pe.wait_ge(S["xn_ready"], c + 1)
                    for t in range(CT):
                        ins = pe.transpose(bank[c % 4][:, t * P:(t + 1) * P], xn[:, c * CT + t, :], ident[:, :])
                    ins.then_inc(S["xT_done"], 1)
                for c in range(CHUNKS):
                    pe.wait_ge(S["xT_ready"], c + 1)
                    if c >= 2:
                        pe.wait_ge(S["sig_exp"], c - 1)
                    for t in range(CT):
                        at = t % 2 * GT * E
                        ins = pe.matmul(bank[4 + (2 * c + t // 2) % 4][:, at:at + GT * E], xT[:, (c * CT + t) * P:(c * CT + t + 1) * P],
                                        Wr[:, :, :].rearrange("p r n -> p (r n)"), start=(t % 2 == 0), stop=True, skip_group_check=True)
                    ins.then_inc(S["logits_done"], 1)

            @block.vector
            def _(dve):
                chain = Chain(dve, S["chain_v"])
                normalise(dve, chain, x_sb, xn, stats, mv, rstd, var, root, arrived=chunk_in, done=S["xn_ready"])
                for c in range(CHUNKS):
                    dve.wait_ge(S["xT_done"], c + 1)
                    dve.tensor_copy(xT[:, c * 512:(c + 1) * 512], bank[c % 4][:, :]).then_inc(S["xT_ready"], 1)
                dve.wait_ge(S["consts_in"], 48)
                for c in range(CHUNKS):
                    g = slice(c * CT * GT, (c + 1) * CT * GT)
                    dve.wait_ge(S["sig_exp"], c + 1)
                    chain(dve.tensor_scalar(sig[:, g, :], sig[:, g, :], 1.0, None, ALU.add))
                    chain(dve.reciprocal(sig[:, g, :], sig[:, g, :]))
                    top_k(dve, chain, sig[:, g, :], K, tri[:, :, :], greater[:, :, :, :], equal[:, :, :, :], rank[:, :, :], chosen[:, g, :])
                    ins = dve.tensor_tensor(gate[:, g, :], sig[:, g, :], chosen[:, g, :], ALU.mult)
                    chain(ins)
        ph.barrier()

        U, ADDS = len(USES), 3 * QT * (E - 1)

        def added(k):
            return k // U * ADDS + sum(v[1] > 0 for v in USES[:k % U])

        with nc.Fori(0, LOOPS // GROUP) as b:
            with nc.Block() as block:
                @block.sync
                def _(sp):
                    for r in range(GROUP):
                        sp.wait_ge(S["out_ready"], r + 1)
                        sp.dma_start(x_out[b * GROUP + r].rearrange("(t p) c -> p t c", p=P), out[r % 2][:, :, :]).then_inc(S["out_sent"], 16)
                    sp.wait_ge(S["out_sent"], 16 * GROUP)

                @block.gpsimd
                def _(pool):
                    for r in range(GROUP):
                        for u, (j, e, t) in enumerate(USES):
                            if e == 0:
                                continue
                            k = r * U + u
                            pool.wait_ge(S["prod_done"], k + 1)
                            if e > 1:
                                pool.wait_ge(S["acc_done"], added(k) - QT + 1)
                            pool.tensor_tensor(acc[:, j, t, :], acc[:, j, t, :], prod[k % 3][:, :], ALU.add).then_inc(S["acc_done"], 1)
                        for h in range(1, H - 1):
                            pool.wait_ge(S["zp_done"], H * r + h + 1)
                            if h > 1:
                                pool.wait_ge(S["z_added"], (H - 2) * r + h - 1)
                            pool.tensor_tensor(Z[:, :, :, :], Z[:, :, :, :], zp[h % 2][:, :, :, :], ALU.add).then_inc(S["z_added"], 1)

                @block.scalar
                def _(act):
                    def turn_out(i):
                        act.wait_ge(S["pt_done"], i + 1)
                        if i >= 3:
                            act.wait_ge(S["pv_done"], i - 2)
                        act.copy(pT[i % 3][:, :, :], bank[3 + i % 2][:, :].rearrange("p (t q) -> p t q", t=QT)).then_inc(S["pt_ready"], 1)

                    for r in range(GROUP):
                        if r >= 2:
                            act.wait_ge(S["proj_done"], U * (r - 1))
                        act.copy(xb[r % 2][:, :], xT[:, bass.ds(b * (GROUP * SEQ) + r * SEQ, SEQ)]).then_inc(S["xb_ready"], 1)
                        for h in range(H):
                            i = H * r + h
                            act.wait_ge(S["max_ready"], i + 1)
                            if i >= 3:
                                act.wait_ge(S["pt_done"], i - 2)
                            for qt in range(QT):
                                ins = act.activation(pr[i % 3][:, qt, :], bank[h % 3][:, qt * SEQ:(qt + 1) * SEQ], ACT.Exp,
                                                     bias=mx[:, h, qt:qt + 1], accum_out=sums[:, qt, h:h + 1])
                            ins.then_inc(S["exp_done"], 1)
                            if h:
                                turn_out(i - 1)
                        turn_out(H * r + H - 1)

                @block.tensor
                def _(pe):
                    def project(r, uses):
                        for u in uses:
                            j, e, t = USES[u]
                            k = r * U + u
                            if u == 0:
                                pe.wait_ge(S["xb_ready"], r + 1)
                            if u >= 4:
                                pe.wait_ge(S["prod_done"], k - 3)
                            pe.matmul(bank[u % 4][:, :], xb[r % 2][:, t * P:(t + 1) * P], W[:, j, e, :], start=True, stop=True
                                      ).then_inc(S["proj_done"], 1)
                            if j == 2 and e == 2 and t == 0:
                                pe.wait_ge(S["acc_done"], ADDS * r + 2 * QT * (E - 1))
                                for jj in range(2):
                                    for c in range(H // 2):
                                        for tt in range(QT):
                                            ins = pe.transpose(bank[4 + 2 * jj + c // 2][:, c % 2 * SEQ + tt * P:c % 2 * SEQ + (tt + 1) * P],
                                                               acc[:, jj, tt, c * P:(c + 1) * P], ident[:, :])
                                    ins.then_inc(S["qk_done"], 1)

                    def scores(r, h):
                        i = H * r + h
                        if h >= 3:
                            pe.wait_ge(S["exp_done"], i - 2)
                        at = DH * (h % 2)
                        for qt in range(QT):
                            ins = pe.matmul(bank[h % 3][:, qt * SEQ:(qt + 1) * SEQ], qT[at:at + DH, h // 2, qt * P:(qt + 1) * P],
                                            kT[at:at + DH, h // 2, :], start=(qt == 0), stop=True, skip_group_check=True)
                        ins.then_inc(S["s_done"], 1)

                    def turn(r, h):
                        i = H * r + h
                        pe.wait_ge(S["exp_done"], i + 1)
                        if h >= 2:
                            pe.wait_ge(S["pt_ready"], i - 1)
                        for kt in range(QT):
                            for qt in range(QT):
                                ins = pe.transpose(bank[3 + i % 2][:, kt * SEQ + qt * P:kt * SEQ + (qt + 1) * P],
                                                   pr[i % 3][:, qt, kt * P:(kt + 1) * P], ident[:, :])
                        ins.then_inc(S["pt_done"], 1)

                    def weigh(r, h):
                        i = H * r + h
                        pe.wait_ge(S["pt_ready"], i + 1)
                        if h == 0:
                            pe.wait_ge(S["acc_done"], ADDS * (r + 1))
                        if h >= 2:
                            pe.wait_ge(S["zp_done"], i - 1)
                        for qt in range(QT):
                            for kt in range(QT):
                                ins = pe.matmul(bank[5 + h % 2][:, qt * DH:(qt + 1) * DH], pT[i % 3][:, kt, qt * P:(qt + 1) * P],
                                                acc[:, 2, kt, h * DH:(h + 1) * DH], start=(qt == 0 and kt == 0), stop=(kt == QT - 1),
                                                skip_group_check=True)
                        ins.then_inc(S["pv_done"], 1)

                    def turn_z(r):
                        pe.wait_ge(S["z_ready"], r + 1)
                        for qt in range(QT):
                            for c in range(ZT_TILES):
                                n = min(P, E * DH - c * P)
                                ins = pe.transpose(bank[5 + qt][0:n, c * P:(c + 1) * P],
                                                   Z[:, qt, :, :].rearrange("p e d -> p (e d)")[:, c * P:c * P + n], ident[:, :])
                            ins.then_inc(S["zt_done"], 1)

                    def project_out(r):
                        for qt in range(QT):
                            pe.wait_ge(S["zt_ready"], 2 * QT * r + 2 * (qt + 1))
                            for c in range(ZT_TILES):
                                n = min(P, E * DH - c * P)
                                ins = pe.matmul(bank[7][:, qt * P:(qt + 1) * P], ZT[0:n, qt, c, :], Wo[0:n, c, :],
                                                start=(qt == 0 and c == 0), stop=(c == ZT_TILES - 1), skip_group_check=True)
                        ins.then_inc(S["out_done"], 1)

                    for r in range(GROUP):
                        if r == 0:
                            project(r, range(U))
                        else:
                            project(r, range(0, 4))
                            turn_z(r - 1)
                            project(r, range(4, 8))
                            project_out(r - 1)
                            project(r, range(8, 16))
                            pe.wait_ge(S["out_ready"], r)
                            project(r, range(16, U))
                        pe.wait_ge(S["qk_ready"], 4 * (r + 1))
                        pe.wait_ge(S["prod_done"], U * (r + 1))
                        scores(r, 0)
                        scores(r, 1)
                        for h in range(H):
                            turn(r, h)
                            if h + 2 < H:
                                scores(r, h + 2)
                            if h:
                                weigh(r, h - 1)
                        weigh(r, H - 1)
                    turn_z(GROUP - 1)
                    project_out(GROUP - 1)

                @block.vector
                def _(dve):
                    chain = Chain(dve, S["chain_v"])

                    def gated(r, uses):
                        now = bass.ds(b * (GROUP * QT * GT) + r * (QT * GT), QT * GT)
                        gv = gate[:, now, :].rearrange("p (t r h) e -> p t r h e", t=QT, r=2)
                        for u in uses:
                            j, e, t = USES[u]
                            k = r * U + u
                            dve.wait_ge(S["proj_done"], k + 1)
                            g = gv[:, t, 1 if j == 0 else 0, :, e:e + 1].broadcast_to([P, H, DH])
                            src = bank[u % 4][:, :].rearrange("p (h d) -> p h d", d=DH)
                            if e == 0:
                                dst = acc[:, j, t, :]
                            else:
                                dst = prod[k % 3][:, :]
                                before = [i for i in range(k) if i % 3 == k % 3 and USES[i % U][1]]
                                if before:
                                    dve.wait_ge(S["acc_done"], added(before[-1]) + 1)
                            dve.tensor_tensor(dst.rearrange("p (h d) -> p h d", d=DH), src, g, ALU.mult).then_inc(S["prod_done"], 1)
                            if j == 2 and e == 3 and t == 0:
                                for jj in range(2):
                                    dve.wait_ge(S["qk_done"], 2 * r + jj + 1)
                                    for c in range(2):
                                        dst, src = (qT, kT)[jj][:, 2 * c:2 * c + 2, :], bank[4 + 2 * jj + c][:, :].rearrange("p (c t) -> p c t", c=2)
                                        dve.tensor_scalar(dst, src, DH ** -0.5 if jj == 0 else 1.0, None, ALU.mult).then_inc(S["qk_ready"], 1)

                    def share(r, h):
                        i = H * r + h
                        now = bass.ds(b * (GROUP * QT * GT) + r * (QT * GT), QT * GT)
                        cv = chosen[:, now, :].rearrange("p (t r h) e -> p t r h e", t=QT, r=2)
                        dve.wait_ge(S["exp_done"], i + 1)
                        chain(dve.reciprocal(rec[:, :, h:h + 1], sums[:, :, h:h + 1]))
                        chain(dve.tensor_tensor(pick[:, :, h, :], cv[:, :, 1, h, :], rec[:, :, h:h + 1].broadcast_to([P, QT, E]), ALU.mult))
                        dve.wait_ge(S["pv_done"], i + 1)
                        if h >= 3:
                            dve.wait_ge(S["z_added"], (H - 2) * r + h - 2)
                        dst = zp[h % 2] if h else Z
                        src = bank[5 + h % 2][:, 0:QT * DH].rearrange("p (t o d) -> p t o d", t=QT, o=1)
                        dve.tensor_tensor(dst[:, :, :, :], src.broadcast_to([P, QT, E, DH]), pick[:, :, h, :].unsqueeze(3).broadcast_to([P, QT, E, DH]),
                                          ALU.mult).then_inc(S["zp_done"], 1)

                    def copy_z(r):
                        for qt in range(QT):
                            dve.wait_ge(S["zt_done"], QT * r + qt + 1)
                            dve.tensor_copy(ZT[:, qt, 0:2, :], bank[5 + qt][:, 0:2 * P].rearrange("p (c q) -> p c q", c=2)).then_inc(S["zt_ready"], 1)
                            dve.tensor_copy(ZT[0:DH, qt, 2, :], bank[5 + qt][0:DH, 2 * P:3 * P]).then_inc(S["zt_ready"], 1)

                    def add_rows(r):
                        dve.wait_ge(S["out_done"], r + 1)
                        if r >= 2:
                            dve.wait_ge(S["out_sent"], 16 * r)
                        dve.tensor_tensor(out[r % 2][:, :, :], bank[7][:, 0:SEQ].rearrange("p (t c) -> p t c", t=QT),
                                          x_sb[:, bass.ds(b * (GROUP * QT) + r * QT, QT), :], ALU.add).then_inc(S["out_ready"], 1)

                    for r in range(GROUP):
                        if r == 0:
                            gated(r, range(U))
                        else:
                            gated(r, range(0, 4))
                            copy_z(r - 1)
                            gated(r, range(4, 8))
                            add_rows(r - 1)
                            gated(r, range(8, U))
                        for h in range(H):
                            dve.wait_ge(S["s_done"], H * r + h + 1)
                            chain(dve.tensor_reduce(mx[:, h, :], bank[h % 3][:, :].rearrange("p (t k) -> p t k", t=QT), AX.X, ALU.max))
                            dve.tensor_scalar(mx[:, h, :], mx[:, h, :], -1.0, None, ALU.mult).then_inc(S["max_ready"], 1)
                            if h >= 2:
                                share(r, h - 2)
                        share(r, H - 2)
                        share(r, H - 1)
                        dve.wait_ge(S["zp_done"], H * (r + 1))
                        dve.wait_ge(S["z_added"], (H - 2) * (r + 1))
                        dve.tensor_tensor(Z[:, :, :, :], Z[:, :, :, :], zp[(H - 1) % 2][:, :, :, :], ALU.add).then_inc(S["z_ready"], 1)
                    copy_z(GROUP - 1)
                    add_rows(GROUP - 1)
            ph.barrier()


def lay_out(inputs):
    import numpy as np

    a = {k: np.asarray(v) for k, v in inputs.items()}
    head = np.array([[[2 * s + par for s in range(PAIRS)] for _ in range(HD)] for par in range(2)]).reshape(-1)
    d = np.array([[[k] * PAIRS for k in range(HD)] for _ in range(2)]).reshape(-1)
    packed = head * HD + d
    o = {"x": a["x"]}
    o["ctxT"] = np.ascontiguousarray(a["ctx_1024"].transpose(0, 2, 1))
    o["ctx_rows"] = a["ctx_1024"].reshape(BATCH * CTX, DIM)
    for n, m in (("mask8", a["mask_Bx1xSxS2_ik1"]), ("mask1", a["mask_1x1xSxS2_ik1"])):
        o[n] = m
        o[n + "T"] = np.ascontiguousarray(m[:, 0].transpose(0, 2, 1))
    o["a0_wq"], o["a0_wk"] = a["L0_xattn_wq"].T[:, packed], a["L0_xattn_wk"].T[:, packed]
    o["a0_wv"], o["a0_wo"] = a["L0_xattn_wv"].T, a["L0_xattn_wo"].T
    o["a0_bq"], o["a0_bk"] = a["L0_xattn_bq"][packed], a["L0_xattn_bk"][packed]
    o["a0_bv"], o["a0_bo"] = a["L0_xattn_bv"], a["L0_xattn_bo"]
    wqkv, bqkv = a["L0_ffn_w_qkv"], a["L0_ffn_b_qkv"]
    o["s0_wq"], o["s0_wk"], o["s0_wv"] = wqkv[:, 0:128][:, packed], wqkv[:, 128:256][:, packed], wqkv[:, 256:384]
    o["s0_bq"], o["s0_bk"], o["s0_bv"] = bqkv[0:128][packed], bqkv[128:256][packed], bqkv[256:384]
    o["s0_wo"], o["s0_bo"] = a["L0_ffn_w_o"], a["L0_ffn_b_o"]
    o["s0_lng"], o["s0_lnb"] = a["L0_ffn_ln1_g"], a["L0_ffn_ln1_b"]

    def diagonal(m):
        out = np.zeros((DIM, DIM), m.dtype)
        for h in range(HEADS):
            out[h * HD:(h + 1) * HD, h * HD:(h + 1) * HD] = m.T
        return out
    o["a1_wq"], o["a1_wk"] = diagonal(a["L1_xattn_Wq"])[:, packed], diagonal(a["L1_xattn_Wk"])[:, packed]
    o["a1_wv"], o["a1_wo"], o["a1_bo"] = diagonal(a["L1_xattn_Wv"]), a["L1_xattn_Wo"].T, a["L1_xattn_bo"]
    o["a2_wq"], o["a2_wqn"] = a["L2_xattn_Wq"].T[:, packed], a["L2_xattn_Wq"].T
    o["a2_wk"] = a["L2_xattn_Wkv"].T[:, d]
    o["a2_wv"] = a["L2_xattn_Wkv"].T[:, np.tile(np.arange(HD), HEADS) + HD]
    o["a2_wo"] = a["L2_xattn_Wc"].T
    for k in "qk":
        o["a3_w" + k], o["a3_b" + k] = a["L3_xattn_W" + k][:, packed], a["L3_xattn_b" + k][packed]
    o["a3_wv"], o["a3_bv"], o["a3_wo"], o["a3_bo"] = (a["L3_xattn_" + k] for k in ("Wv", "bv", "Wo", "bo"))

    def experts(tag, up, down, biases, tiles):
        for n, m in up.items():
            o[f"{tag}_{n}"] = m.transpose(1, 0, 2)
        E, F, D = down.shape
        o[f"{tag}_W2"] = down.reshape(E, tiles, F // tiles, D).transpose(2, 0, 1, 3)
        for n, m in biases.items():
            o[f"{tag}_{n}"] = m.reshape(E * tiles, F // tiles).T
    experts("m0", {"W1": a["L0_ffn_W1"]}, a["L0_ffn_W2"], {"b1": a["L0_ffn_b1"]}, 4)
    o["m0_b2"], o["m0_gw"], o["m0_gb"] = a["L0_ffn_b2"], a["L0_ffn_gate_w"], a["L0_ffn_gate_b"]
    o["m0_lng"], o["m0_lnb"] = a["L0_ffn_ln2_g"], a["L0_ffn_ln2_b"]
    experts("m1", {"W1": a["L1_ffn_W1"], "Wg": a["L1_ffn_Wg"]}, a["L1_ffn_W2"], {"b1": a["L1_ffn_b1"], "bg": a["L1_ffn_bg"]}, 3)
    o["m1_b2"], o["m1_gw"] = a["L1_ffn_b2"], a["L1_ffn_centroid"].T
    experts("m2", {"W1": a["L2_ffn_W1"], "Wg": a["L2_ffn_W2"]}, a["L2_ffn_Wo"], {"b1": a["L2_ffn_b1"], "bg": a["L2_ffn_b2"]}, 4)
    o["m2_gw"], o["m2_lng"], o["m2_lnb"] = a["L2_ffn_router_w"], a["L2_ffn_ln_g"], a["L2_ffn_ln_b"]
    o["m2_bo"], o["m2_eg"], o["m2_eb"] = a["L2_ffn_bo"].T, a["L2_ffn_eg"].T, a["L2_ffn_eb"].T
    wq = a["L3_ffn_Wq"].reshape(DIM, 1, 8, 5, 64)
    wkv = a["L3_ffn_Wkv"].reshape(DIM, 2, 8, 5, 64)
    o["m3_W"] = np.concatenate([wq, wkv], axis=1).transpose(0, 1, 3, 2, 4).reshape(DIM, 3, 5, 512)
    o["m3_Wr"] = np.stack([a["L3_ffn_Ws"], a["L3_ffn_Wd"]], axis=1)
    o["m3_Wo"] = a["L3_ffn_Wo"].reshape(64, 5, DIM).transpose(1, 0, 2).reshape(320, DIM)
    for e in (5, 8):
        o[f"tri{e}"] = np.broadcast_to(np.triu(np.ones((e, e), np.float32), 1), (P, e, e))
    o["onehot"] = np.broadcast_to(np.eye(8, dtype=np.float32)[:, :, None], (8, 8, P))
    o["ident"] = np.eye(P, dtype=np.float32)
    pick = np.zeros((P, 2, HD + 1), np.float32)
    for tile in range(2):
        for par in range(2):
            for k in range(HD + 1):
                pick[32 * (2 * tile + par) + k, par, k] = 1.0
    o["pick"] = pick.reshape(P, -1)
    sel = np.zeros((P, P), np.float32)
    for par in range(2):
        sel[SHIFT + 2 * par:SHIFT + 2 * par + 2] = 1.0
    o["shiftsel"] = sel
    o["rowbase"] = np.repeat(np.arange(BATCH, dtype=np.float32)[None, :] * CTX, P, axis=0)
    return {k: np.ascontiguousarray(v) for k, v in o.items()}


def build(nc, t, phases=("a0", "s0", "m0", "a1", "m1", "a2", "m2", "a3", "m3")):
    def weights(tag, *names):
        return {n: t[f"{tag}_{n}"] for n in names}

    consts = {k: t[k] for k in ("ident", "pick", "shiftsel", "rowbase", "tri5", "tri8", "onehot")}
    ROOT8 = float(HD) ** -0.5
    cur = before = t["x"]
    if phases[0] == "m0":
        cur = t["y0"]

    def nxt(tag):
        if tag == phases[-1]:
            return t["out"]
        return nc.dram_tensor(f"x_after_{tag}", [BATCH, SEQ, DIM], F32).ap()
    for tag in phases:
        dst = nxt(tag)
        if tag == "a0":
            attention_phase(nc, tag, cur, dst, weights(tag, "wq", "wk", "wv", "wo", "bq", "bk", "bv", "bo"), consts, ctxT=t["ctxT"],
                            mask=t["mask8"], maskT=t["mask8T"], scale=ROOT8, clip=100.0)
        elif tag == "s0":
            short_attention_phase(nc, tag, cur, dst, weights(tag, "wq", "wk", "wv", "wo", "bq", "bk", "bv", "bo", "lng", "lnb"), consts,
                            scale=ROOT8, self_ln=True)
        elif tag == "a1":
            attention_phase(nc, tag, cur, dst, weights(tag, "wq", "wk", "wv", "wo", "bo"), consts, ctxT=t["ctxT"],
                            mask=t["mask1"], maskT=t["mask1T"], scale=float(DIM) ** -0.5)
        elif tag == "a2":
            short_attention_phase(nc, tag, cur, dst, weights(tag, "wq", "wqn", "wk", "wv", "wo"), consts, ctxT=t["ctxT"],
                            ctx_rows=t["ctx_rows"], scale=ROOT8)
        elif tag == "a3":
            attention_phase(nc, tag, cur, dst, weights(tag, "wq", "wk", "wv", "wo", "bq", "bk", "bv", "bo"), consts, ctxT=t["ctxT"],
                            scale=ROOT8)
        elif tag == "m0":
            experts_phase(nc, tag, "relu", before, dst, weights(tag, "W1", "W2", "b1", "b2", "gw", "gb", "lng", "lnb"), consts, extra=cur)
        elif tag == "m1":
            experts_phase(nc, tag, "silu", cur, dst, weights(tag, "W1", "Wg", "W2", "b1", "bg", "b2", "gw"), consts)
        elif tag == "m2":
            experts_phase(nc, tag, "clip", cur, dst, weights(tag, "W1", "Wg", "W2", "b1", "bg", "bo", "eg", "eb", "gw", "lng", "lnb"), consts)
        elif tag == "m3":
            switch_phase(nc, tag, cur, dst, weights(tag, "W", "Wr", "Wo"), consts)
        before, cur = cur, dst


def kernel(**inputs):
    import numpy as _np
    import concourse.bacc as _bacc
    from concourse.bass_utils import run_bass_kernel_spmd as _run

    nc = _bacc.Bacc("TRN2", target_bir_lowering=False, num_devices=1)
    arrays, t = {}, {}
    for name, a in lay_out(inputs).items():
        arrays[f"in_{name}"] = a
        t[name] = nc.dram_tensor(f"in_{name}", a.shape, mybir.dt.from_np(a.dtype), kind="ExternalInput").ap()
    t["out"] = nc.dram_tensor("out_x", [BATCH, SEQ, DIM], F32, kind="ExternalOutput").ap()
    build(nc, t)
    return _run(nc, [arrays], core_ids=[0]).results[0]["out_x"]
```
